# Optimizing a Trainium2 kernel written in Bass

```python
import numpy as np
import jax
import jax.numpy as jnp

def _softmax(x, axis=-1):
    return jax.nn.softmax(x, axis=axis)

def _gelu(x):
    return jax.nn.gelu(x, approximate=True)

def _silu(x):
    return jax.nn.silu(x)

def _sigmoid(x):
    return jax.nn.sigmoid(x)

def _layernorm(x, axis=-1, eps=1e-05):
    m = jnp.mean(x, axis=axis, keepdims=True)
    v = jnp.var(x, axis=axis, keepdims=True)
    return (x - m) / jnp.sqrt(v + eps)

def _scatter_add(tgt, idx, src, axis=0):
    return tgt.at[idx].add(src)

def _segment_sum(src, seg, n):
    return jax.ops.segment_sum(src, seg, n)
kernel_name = 'mk_seq_preln_d2_jaxref_r8_c53f82'

def setup_inputs(seed: int=0):
    np.random.seed(seed)
    _w = jnp.asarray

    def _L0_attn_setup():
        import math
        import jax, jax.numpy as jnp
        import numpy as np
        D_MODEL = 256
        NUM_HEADS = 16
        D_HEAD = D_MODEL // NUM_HEADS
        THETA = 10000.0

        def _rope_tables(seq_len, d_head):
            idx = jnp.arange(0, d_head, 2, dtype=jnp.float32)
            inv_freq = THETA ** (-idx / d_head)
            angles = jnp.arange(seq_len, dtype=jnp.float32)[:, None] * inv_freq[None, :]
            return (jnp.cos(angles), jnp.sin(angles))

        def _apply_rope(x, cos, sin):
            B, H, S, d = x.shape
            xp = x.reshape(B, H, S, d // 2, 2)
            xe, xo = (xp[..., 0], xp[..., 1])
            rot = jnp.stack([xe * cos - xo * sin, xe * sin + xo * cos], axis=-1)
            return rot.reshape(B, H, S, d)
        key = jax.random.key(seed)
        k_x, k_q, k_k, k_v, k_o = jax.random.split(key, 5)
        std = math.sqrt(2.0 / (D_MODEL + D_MODEL))
        x = jax.random.normal(k_x, (4, 256, D_MODEL), dtype=jnp.float32)
        Wq = jax.random.normal(k_q, (D_MODEL, D_MODEL), dtype=jnp.float32) * std
        Wk = jax.random.normal(k_k, (D_MODEL, D_MODEL), dtype=jnp.float32) * std
        Wv = jax.random.normal(k_v, (D_MODEL, D_MODEL), dtype=jnp.float32) * std
        Wo = jax.random.normal(k_o, (D_MODEL, D_MODEL), dtype=jnp.float32) * std
        return {'x': x, 'Wq': Wq, 'Wk': Wk, 'Wv': Wv, 'Wo': Wo}
    _L0_attn_in = _L0_attn_setup()

    def _L0_ffn_setup():
        import jax, jax.numpy as jnp
        import numpy as np
        D_IN = 256
        D_OUT = 256
        EPS = 1e-05
        key = jax.random.key(seed)
        k_x, k_w = jax.random.split(key)
        x = jax.random.normal(k_x, (8, 256, D_IN), dtype=jnp.float32)
        weight = jax.random.normal(k_w, (D_OUT, D_IN), dtype=jnp.float32)
        gamma = jnp.ones((D_OUT,), dtype=jnp.float32)
        beta = jnp.zeros((D_OUT,), dtype=jnp.float32)
        ln_weight = jnp.ones((D_IN,), dtype=jnp.float32)
        ln_bias = jnp.zeros((D_IN,), dtype=jnp.float32)
        return {'x': x, 'weight': weight, 'gamma': gamma, 'beta': beta, 'ln_weight': ln_weight, 'ln_bias': ln_bias}
    _L0_ffn_in = _L0_ffn_setup()

    def _L1_attn_setup():
        import jax, jax.numpy as jnp
        import numpy as np
        BATCH, SEQ, D_MODEL, N_HEADS, D_HEAD = (2, 256, 256, 16, 128)
        ATTN_SCALE = np.sqrt(D_HEAD).astype(np.float32)
        IGNORE = jnp.float32(-100000.0)
        key = jax.random.key(seed)
        ks = jax.random.split(key, 5)
        init = 1.0 / np.sqrt(D_MODEL)
        return {'x': jax.random.normal(ks[0], (BATCH, SEQ, D_MODEL), jnp.float32), 'W_Q': jax.random.normal(ks[1], (N_HEADS, D_MODEL, D_HEAD), jnp.float32) * init, 'W_K': jax.random.normal(ks[2], (N_HEADS, D_MODEL, D_HEAD), jnp.float32) * init, 'W_V': jax.random.normal(ks[3], (N_HEADS, D_MODEL, D_HEAD), jnp.float32) * init, 'W_O': jax.random.normal(ks[4], (N_HEADS, D_HEAD, D_MODEL), jnp.float32) * init, 'b_Q': jnp.zeros((N_HEADS, D_HEAD), jnp.float32), 'b_K': jnp.zeros((N_HEADS, D_HEAD), jnp.float32), 'b_V': jnp.zeros((N_HEADS, D_HEAD), jnp.float32), 'b_O': jnp.zeros((D_MODEL,), jnp.float32)}
    _L1_attn_in = _L1_attn_setup()

    def _L1_ffn_setup():
        import jax, jax.numpy as jnp
        import numpy as np
        TOP_K = 6
        N_GROUP = 8
        TOPK_GROUP = 3
        CAPACITY = 96
        RSF = 1.0
        key = jax.random.key(seed)
        ks = jax.random.split(key, 8)
        B, S, H = (1, 512, 256)
        E, M = (64, 176)
        MS = 352
        sc = 0.02
        return {'hidden_states': jax.random.normal(ks[0], (B, S, H), jnp.float32), 'gate_weight': jax.random.normal(ks[1], (E, H), jnp.float32) * sc, 'Wg': jax.random.normal(ks[2], (E, M, H), jnp.float32) * sc, 'Wu': jax.random.normal(ks[3], (E, M, H), jnp.float32) * sc, 'Wd': jax.random.normal(ks[4], (E, H, M), jnp.float32) * sc, 'Sg': jax.random.normal(ks[5], (MS, H), jnp.float32) * sc, 'Su': jax.random.normal(ks[6], (MS, H), jnp.float32) * sc, 'Sd': jax.random.normal(ks[7], (H, MS), jnp.float32) * sc}
    _L1_ffn_in = _L1_ffn_setup()
    _d = {'L0_attn_x': _L0_attn_in['x'], 'L0_attn_Wq': _L0_attn_in['Wq'], 'L0_attn_Wk': _L0_attn_in['Wk'], 'L0_attn_Wv': _L0_attn_in['Wv'], 'L0_attn_Wo': _L0_attn_in['Wo'], 'L0_ffn_weight': _L0_ffn_in['weight'], 'L0_ffn_gamma': _L0_ffn_in['gamma'], 'L0_ffn_beta': _L0_ffn_in['beta'], 'L0_ffn_ln_weight': _L0_ffn_in['ln_weight'], 'L0_ffn_ln_bias': _L0_ffn_in['ln_bias'], 'L1_attn_W_Q': _L1_attn_in['W_Q'], 'L1_attn_W_K': _L1_attn_in['W_K'], 'L1_attn_W_V': _L1_attn_in['W_V'], 'L1_attn_W_O': _L1_attn_in['W_O'], 'L1_attn_b_Q': _L1_attn_in['b_Q'], 'L1_attn_b_K': _L1_attn_in['b_K'], 'L1_attn_b_V': _L1_attn_in['b_V'], 'L1_attn_b_O': _L1_attn_in['b_O'], 'L1_ffn_gate_weight': _L1_ffn_in['gate_weight'], 'L1_ffn_Wg': _L1_ffn_in['Wg'], 'L1_ffn_Wu': _L1_ffn_in['Wu'], 'L1_ffn_Wd': _L1_ffn_in['Wd'], 'L1_ffn_Sg': _L1_ffn_in['Sg'], 'L1_ffn_Su': _L1_ffn_in['Su'], 'L1_ffn_Sd': _L1_ffn_in['Sd']}
    _x0 = _d['L0_attn_x']
    _d['L0_attn_x'] = jax.random.normal(jax.random.fold_in(jax.random.key(seed), 1), (2, 1024, 256), dtype=_x0.dtype)
    del _x0
    return _d

def reference(L0_attn_x, L0_attn_Wq, L0_attn_Wk, L0_attn_Wv, L0_attn_Wo, L0_ffn_weight, L0_ffn_gamma, L0_ffn_beta, L0_ffn_ln_weight, L0_ffn_ln_bias, L1_attn_W_Q, L1_attn_W_K, L1_attn_W_V, L1_attn_W_O, L1_attn_b_Q, L1_attn_b_K, L1_attn_b_V, L1_attn_b_O, L1_ffn_gate_weight, L1_ffn_Wg, L1_ffn_Wu, L1_ffn_Wd, L1_ffn_Sg, L1_ffn_Su, L1_ffn_Sd):

    def _L0_attn_ref(x, Wq, Wk, Wv, Wo):
        import math
        import jax, jax.numpy as jnp
        import numpy as np
        D_MODEL = 256
        NUM_HEADS = 16
        D_HEAD = D_MODEL // NUM_HEADS
        THETA = 10000.0

        def _rope_tables(seq_len, d_head):
            idx = jnp.arange(0, d_head, 2, dtype=jnp.float32)
            inv_freq = THETA ** (-idx / d_head)
            angles = jnp.arange(seq_len, dtype=jnp.float32)[:, None] * inv_freq[None, :]
            return (jnp.cos(angles), jnp.sin(angles))

        def _apply_rope(x, cos, sin):
            B, H, S, d = x.shape
            xp = x.reshape(B, H, S, d // 2, 2)
            xe, xo = (xp[..., 0], xp[..., 1])
            rot = jnp.stack([xe * cos - xo * sin, xe * sin + xo * cos], axis=-1)
            return rot.reshape(B, H, S, d)
        B, S, D = x.shape
        H, dh = (NUM_HEADS, D_HEAD)

        def proj(W):
            y = jnp.einsum('bsi,oi->bso', x, W)
            return y.reshape(B, S, H, dh).transpose(0, 2, 1, 3)
        q, k, v = (proj(Wq), proj(Wk), proj(Wv))
        cos, sin = _rope_tables(S, dh)
        q = _apply_rope(q, cos, sin)
        k = _apply_rope(k, cos, sin)
        scores = jnp.einsum('bhqd,bhkd->bhqk', q.astype(jnp.float32), k.astype(jnp.float32)) / math.sqrt(dh)
        causal = jnp.tril(jnp.ones((S, S), dtype=bool))
        scores = jnp.where(causal, scores, jnp.finfo(jnp.float32).min)
        probs = jax.nn.softmax(scores, axis=-1).astype(v.dtype)
        attn = jnp.einsum('bhqk,bhkd->bhqd', probs, v)
        attn = attn.transpose(0, 2, 1, 3).reshape(B, S, D)
        return jnp.einsum('bsi,oi->bso', attn, Wo)

    def _L0_ffn_ref(x, weight, gamma, beta, ln_weight, ln_bias):
        import jax, jax.numpy as jnp
        import numpy as np
        D_IN = 256
        D_OUT = 256
        EPS = 1e-05
        mean = jnp.mean(x, axis=-1, keepdims=True)
        var = jnp.mean(jnp.square(x - mean), axis=-1, keepdims=True)
        xn = (x - mean) * jax.lax.rsqrt(var + EPS) * ln_weight + ln_bias
        quant_w = jnp.sign(weight)
        scale = jnp.max(jnp.abs(weight))
        out = jnp.einsum('bsk,ok->bso', xn, quant_w)
        return out * scale * gamma + beta

    def _L1_attn_ref(x, W_Q, W_K, W_V, W_O, b_Q, b_K, b_V, b_O):
        import jax, jax.numpy as jnp
        import numpy as np
        BATCH, SEQ, D_MODEL, N_HEADS, D_HEAD = (2, 256, 256, 16, 128)
        ATTN_SCALE = np.sqrt(D_HEAD).astype(np.float32)
        IGNORE = jnp.float32(-100000.0)
        q = jnp.einsum('bpd,hde->bphe', x, W_Q) + b_Q
        k = jnp.einsum('bpd,hde->bphe', x, W_K) + b_K
        v = jnp.einsum('bpd,hde->bphe', x, W_V) + b_V
        scores = jnp.einsum('bqhe,bkhe->bhqk', q, k) / ATTN_SCALE
        S = x.shape[1]
        causal = jnp.tril(jnp.ones((S, S), bool))
        scores = jnp.where(causal, scores, IGNORE)
        attn = jax.nn.softmax(scores, axis=-1)
        z = jnp.einsum('bkhe,bhqk->bqhe', v, attn)
        out = jnp.einsum('bqhe,hed->bqd', z, W_O) + b_O
        return out

    def _L1_ffn_ref(hidden_states, gate_weight, Wg, Wu, Wd, Sg, Su, Sd):
        import jax, jax.numpy as jnp
        import numpy as np
        TOP_K = 6
        N_GROUP = 8
        TOPK_GROUP = 3
        CAPACITY = 96
        RSF = 1.0
        B, S, H = hidden_states.shape
        E, M, _ = Wg.shape
        K, NG, TG, C = (TOP_K, N_GROUP, TOPK_GROUP, CAPACITY)
        x = hidden_states.reshape(-1, H)
        T = x.shape[0]
        logits = x.astype(jnp.float32) @ gate_weight.astype(jnp.float32).T
        scores = jax.nn.softmax(logits, axis=-1)
        group_scores = scores.reshape(T, NG, E // NG).max(axis=-1)
        _, gidx = jax.lax.top_k(group_scores, TG)
        gmask = jnp.zeros((T, NG), scores.dtype).at[jnp.arange(T)[:, None], gidx].set(1.0)
        smask = jnp.repeat(gmask, E // NG, axis=1)
        tmp_scores = jnp.where(smask > 0, scores, 0.0)
        topk_w, topk_i = jax.lax.top_k(tmp_scores, K)
        topk_w = topk_w * RSF
        flat = topk_i.reshape(-1)
        oh = jax.nn.one_hot(flat, E, dtype=jnp.int32)
        pos = jnp.sum(jnp.cumsum(oh, axis=0) * oh, axis=-1) - 1
        slot = flat * C + jnp.minimum(pos, C - 1)
        tok = jnp.arange(T * K) // K
        buf = jnp.zeros((E * C, H), x.dtype).at[slot].set(x[tok]).reshape(E, C, H)
        g = jnp.einsum('ech,emh->ecm', buf, Wg)
        u = jnp.einsum('ech,emh->ecm', buf, Wu)
        out = jnp.einsum('ecm,ehm->ech', jax.nn.silu(g) * u, Wd).reshape(E * C, H)
        yk = out[slot].reshape(T, K, H)
        y = jnp.sum(yk * topk_w[..., None].astype(yk.dtype), axis=1)
        shared = jax.nn.silu(x @ Sg.T) * (x @ Su.T) @ Sd.T
        return (y + shared).reshape(B, S, H)
    x = L0_attn_x
    x = x + _L0_attn_ref(_layernorm(x, axis=-1), L0_attn_Wq, L0_attn_Wk, L0_attn_Wv, L0_attn_Wo)
    x = x + _L0_ffn_ref(_layernorm(x, axis=-1), L0_ffn_weight, L0_ffn_gamma, L0_ffn_beta, L0_ffn_ln_weight, L0_ffn_ln_bias)
    x = x + _L1_attn_ref(_layernorm(x, axis=-1), L1_attn_W_Q, L1_attn_W_K, L1_attn_W_V, L1_attn_W_O, L1_attn_b_Q, L1_attn_b_K, L1_attn_b_V, L1_attn_b_O)
    x = x + _L1_ffn_ref(_layernorm(x, axis=-1), L1_ffn_gate_weight, L1_ffn_Wg, L1_ffn_Wu, L1_ffn_Wd, L1_ffn_Sg, L1_ffn_Su, L1_ffn_Sd)
    return x

_drawn_inputs = setup_inputs


def setup_inputs(seed=0):
    import zlib

    import numpy as np

    out = dict(_drawn_inputs(seed))
    spreads = {'L0_ffn_gamma': (1.0, 0.2),
     'L0_ffn_beta': (0.0, 0.8),
     'L0_ffn_ln_weight': (1.0, 0.2),
     'L0_ffn_ln_bias': (0.0, 0.1),
     'L1_attn_b_Q': (0.0, 0.8),
     'L1_attn_b_K': (0.0, 0.8),
     'L1_attn_b_V': (0.0, 0.8),
     'L1_attn_b_O': (0.0, 0.8)}
    factors = {'L1_attn_W_Q': 8.0,
     'L1_attn_W_K': 8.0,
     'L1_attn_W_V': 8.0,
     'L1_attn_W_O': 7.056,
     'L1_ffn_gate_weight': 8.0,
     'L1_ffn_Wg': 8.0,
     'L1_ffn_Wu': 8.0,
     'L1_ffn_Wd': 8.0,
     'L1_ffn_Sg': 8.0,
     'L1_ffn_Su': 8.0,
     'L1_ffn_Sd': 8.0}
    for name, (base, spread) in spreads.items():
        noise = np.random.default_rng([zlib.crc32(name.encode()), seed]).standard_normal(out[name].shape)
        drawn = base * np.exp(spread * noise) if base else spread * noise
        out[name] = jnp.asarray(drawn.astype(out[name].dtype))
    for name, factor in factors.items():
        out[name] = (out[name] * factor).astype(out[name].dtype)
    return out
```

```python
from contextlib import ExitStack

import numpy as np
import concourse.bass as bass
from concourse import mybir

F32 = mybir.dt.float32
F16 = mybir.dt.float16
BF16 = mybir.dt.bfloat16
U32 = mybir.dt.uint32
ALU = mybir.AluOpType
ACT = mybir.ActivationFunctionType
AX = mybir.AxisListType
ds = bass.ds

P = 128
B, S, D = 2, 1024, 256
T = B * S
NT = T // P
BT = S // P
DC = D // P
H = 16
DH0 = D // H
DH1 = 128
EPS = 1e-5
THETA = 10000.0
E, M, C = 64, 176, 96
MH = M // 2
K, NG, TG = 6, 8, 3
GS = E // NG
MS = 352
NMS = MS // MH
NEG = -1e30
ZD = 6
STOP = None


def constants():
    inv = THETA ** (-np.arange(0, DH0, 2, dtype=np.float32) / DH0)
    ang = np.arange(S, dtype=np.float32)[:, None] * inv[None, :].astype(np.float32)
    cos = np.repeat(np.cos(ang), 2, axis=1).astype(np.float32)
    sin = np.repeat(np.sin(ang), 2, axis=1).astype(np.float32)
    sin[:, 0::2] *= -1
    rope = np.stack([cos, sin], 1).reshape(BT, P, 2, DH0).transpose(1, 0, 2, 3)
    ident = np.eye(P, dtype=np.float32)
    mask = np.where(np.arange(P)[:, None] >= np.arange(P)[None, :], 0.0, NEG).astype(np.float32)
    before = (np.arange(P)[:, None] < np.arange(P)[None, :]).astype(np.float32)
    iota = np.broadcast_to(np.arange(E, dtype=np.float32), (P, E))
    return {"c_rope": np.ascontiguousarray(rope), "c_ident": ident, "c_mask": mask,
            "c_before": before, "c_iota": np.ascontiguousarray(iota)}


class Prog:
    pass


def build(nc, t_in, out):
    g = Prog()
    with ExitStack() as ctx:
        def sb(name, shape, dt=F32, c=ctx):
            return c.enter_context(nc.sbuf_tensor(name, shape, dt))

        made = {}

        def sem(name):
            if name not in made:
                made[name] = ctx.enter_context(nc.semaphore(name))
            return made[name]

        g.sb, g.sem, g.t = sb, sem, t_in
        g.bank = [ctx.enter_context(nc.psum_tensor(f"bank{i}", [P, 2, 512], F32)) for i in range(4)]
        g.x = sb("x", [P, NT, D])
        g.xT = sb("xT", [P, DC, T])
        g.identf = sb("identf", [P, P])
        g.identh = sb("identh", [P, P], F16)
        g.identb = sb("identb", [P, P], BF16)
        g.maskb = sb("maskb", [P, P], BF16)
        g.rstd = sb("rstd", [P, NT])
        g.zero = sb("zero", [P, E * C * D // P // ZD])
        g.xrows = nc.dram_tensor("slot_rows", (E * C, D), F32, kind="Internal").ap()
        g.orows = nc.dram_tensor("expert_rows", (E * C, D), F32, kind="Internal").ap()
        g.s_zero, g.s_memset = sem("zeros_landed"), sem("zeros_ready")
        g.mean = sb("mean", [P, NT])

        load(nc, g)
        norm(nc, g, "n0", None)
        with ExitStack() as c0:
            l0_qkv(nc, g, c0)
            for b in range(B):
                attention(nc, g, "a0", b, 0)
            proj_out(nc, g, "o0", 0)
        if STOP == "att0":
            return finish(nc, g, out)
        with ExitStack() as c1:
            ffn_weights(nc, g, c1)
            norm(nc, g, "n1", "ffn")
            l0_ffn(nc, g)
        if STOP == "ffn0":
            return finish(nc, g, out)
        norm(nc, g, "n2", None)
        with ExitStack() as c2:
            l1_buffers(nc, g, c2)
            for b in range(B):
                attention(nc, g, "a1", b, 1)
                proj_out(nc, g, "o1", 1, b)
        if STOP == "att1":
            return finish(nc, g, out)
        moe(nc, g, out)


def finish(nc, g, out):
    s_out = g.sem("dbg_out")
    with nc.Block() as block:
        @block.sync
        def _(sp):
            sp.dma_start(out.rearrange("b (n p) d -> p (b n) d", p=P), g.x[:, :, :]).then_inc(s_out, 16)
            sp.wait_ge(s_out, 16)


def load(nc, g):
    s_x, s_c, s_v = g.sem("ld_x"), g.sem("ld_const"), g.sem("ld_cast")
    with ExitStack() as c:
        maskf = g.sb("maskf", [P, P], F32, c)
        with nc.Block() as block:
            @block.sync
            def _(sp):
                sp.dma_start(g.identf[:, :], g.t["c_ident"]).then_inc(s_c, 16)
                sp.dma_start(maskf[:, :], g.t["c_mask"]).then_inc(s_c, 16)
                sp.dma_start(g.x[:, :, :], g.t["x"].rearrange("b (n p) d -> p (b n) d", p=P)).then_inc(s_x, 16)

                sp.wait_ge(g.s_memset, 1)
                zv = g.xrows.rearrange("(z p n) d -> z p (n d)", p=P, z=ZD)
                for z in range(ZD):
                    sp.dma_start(zv[z], g.zero[:, :]).then_inc(g.s_zero, 16)

            @block.gpsimd
            def _(pool):
                pool.memset(g.zero[:, :], 0.0).then_inc(g.s_memset, 1)

            @block.vector
            def _(dve):
                dve.wait_ge(s_c, 32)
                dve.tensor_copy(g.identh[:, :], g.identf[:, :]).then_inc(s_v, 1)
                dve.tensor_copy(g.identb[:, :], g.identf[:, :]).then_inc(s_v, 1)
                dve.tensor_copy(g.maskb[:, :], maskf[:, :]).then_inc(s_v, 1)
                dve.wait_ge(s_x, 16)
                dve.wait_ge(s_v, 3)


def norm(nc, g, tag, kind):
    s_st, s_ag, s_sq, s_ch = [g.sem(f"{tag}_{n}") for n in ("stats", "aggr", "sqrt", "chain")]
    s_xn, s_tr = g.sem(f"{tag}_xn"), g.sem(f"{tag}_tr")
    s_ev = [g.sem(f"{tag}_evac{i}") for i in range(2)]
    with ExitStack() as c:
        st = g.sb(f"{tag}_st", [P, NT, 6], F32, c)
        mv = g.sb(f"{tag}_mv", [P, NT, 2], F32, c)
        sq = g.sb(f"{tag}_sq", [P, NT], F32, c)
        tmp = g.sb(f"{tag}_tmp", [P, 2, NT], F32, c)
        xn = g.xn if kind == "keep" else g.sb(f"{tag}_xnb", [P, NT, D], F32, c)
        ve = tmp[:, 0, :]
        t1 = tmp[:, 1, :]
        levels = 2 if kind == "ffn" else 1
        with nc.Block() as block:
            def evac(eng, p):
                eng.wait_ge(s_tr, p + 1)
                for c_ in range(DC):
                    src = g.bank[p % 2][:, 0, c_ * 256:(c_ + 1) * 256]
                    dst = g.xT[:, c_, p * 256:(p + 1) * 256]
                    if p % 2:
                        if kind == "ffn":
                            ins = eng.tensor_scalar(dst, src, g.lnw[:, c_:c_ + 1], g.lnb[:, c_:c_ + 1],
                                                    ALU.mult, ALU.add)
                        else:
                            ins = eng.tensor_copy(dst, src)
                    elif kind == "ffn":
                        ins = eng.activation(dst, src, ACT.Identity, bias=g.lnb[:, c_:c_ + 1],
                                             scale=g.lnw[:, c_:c_ + 1])
                    else:
                        ins = eng.activation(dst, src, ACT.Copy)
                ins.then_inc(s_ev[p % 2], 1)

            @block.vector
            def _(dve):
                n = 0

                def chained(ins):
                    nonlocal n
                    n += 1
                    ins.then_inc(s_ch, 1)
                    dve.wait_ge(s_ch, n)

                for t in range(NT):
                    dve.bn_stats(st[:, t, :], g.x[:, t, :]).then_inc(s_st, 1)
                for t in range(NT):
                    dve.wait_ge(s_st, t + 1)
                    dve.bn_aggr(mv[:, t, :], st[:, t, :]).then_inc(s_ag, 1)
                dve.wait_ge(s_ag, NT)
                chained(dve.tensor_copy(g.mean[:, :], mv[:, :, 0]))
                chained(dve.tensor_copy(t1, mv[:, :, 1]))
                for lv in range(levels):
                    chained(dve.tensor_scalar(ve, t1, EPS, None, ALU.add))
                    dve.wait_ge(s_sq, lv + 1)
                    chained(dve.reciprocal(sq[:, :], sq[:, :]))
                    r = g.rstd[:, :]
                    one = sq[:, :]
                    chained(dve.tensor_tensor(t1, one, one, ALU.mult))
                    chained(dve.tensor_tensor(t1, t1, ve, ALU.mult))
                    chained(dve.tensor_scalar(t1, t1, -0.5, 1.5, ALU.mult, ALU.add))
                    if lv == 0:
                        chained(dve.tensor_tensor(r, one, t1, ALU.mult))
                    else:
                        chained(dve.tensor_tensor(one, one, t1, ALU.mult))
                        chained(dve.tensor_tensor(r, r, one, ALU.mult))
                    if lv + 1 < levels:
                        chained(dve.tensor_tensor(t1, r, r, ALU.mult))
                        chained(dve.tensor_tensor(t1, t1, mv[:, :, 1], ALU.mult))
                for t in range(NT):
                    dve.tensor_scalar(xn[:, t, :], g.x[:, t, :], g.mean[:, t:t + 1], g.rstd[:, t:t + 1],
                                      ALU.subtract, ALU.mult).then_inc(s_xn, 1)
                for p in range(1, NT // 2, 2):
                    evac(dve, p)

            @block.scalar
            def _(act):
                for lv in range(levels):
                    act.wait_ge(s_ch, 3 if lv == 0 else 11)
                    act.activation(sq[:, :], ve, ACT.Sqrt).then_inc(s_sq, 1)
                for p in range(0, NT // 2, 2):
                    evac(act, p)

            @block.tensor
            def _(pe):
                for p in range(NT // 2):
                    pe.wait_ge(s_xn, 2 * p + 2)
                    if p >= 2:
                        pe.wait_ge(s_ev[p % 2], p // 2)
                    for c_ in range(DC):
                        for j in range(2):
                            ins = pe.transpose(g.bank[p % 2][:, 0, (2 * c_ + j) * P:(2 * c_ + j + 1) * P],
                                               xn[:, 2 * p + j, c_ * P:(c_ + 1) * P], g.identf[:, :])
                    ins.then_inc(s_tr, 1)


def l0_qkv(nc, g, c0):
    g.qk = g.sb("qk_parts", [P, NT, 2, H, 2, DH0], F16, c0)
    g.v0 = g.sb("v0", [P, NT, D], F32, c0)
    g.z = g.sb("z0", [P, NT, D], F32, c0)
    g.wo0 = g.sb("wo0", [P, DC, D], F32, c0)
    g.qh = [g.sb(f"qh{i}", [P, BT, 2, 4 * DH0], F16, c0) for i in range(2)]
    s_w, s_mm = g.sem("q0_w"), g.sem("q0_mm")
    s_wo = g.sem("q0_wo")
    s_rot, s_v, s_add, s_hi, s_lo = [g.sem(f"q0_{n}") for n in ("rot", "v", "add", "hi", "lo")]
    with ExitStack() as c:
        w = g.sb("wqkv0", [P, DC, 3 * D], F32, c)
        rope = g.sb("rope", [P, BT, 2, DH0], F32, c)
        rot = [g.sb(f"rot{i}", [P, 2, 2 * D], F32, c) for i in range(2)]
        with nc.Block() as block:
            @block.sync
            def _(sp):
                sp.dma_start(w[:, :, :], g.t["wqkv0"].rearrange("(c p) n -> p c n", p=P)).then_inc(s_w, 16)
                sp.dma_start(rope[:, :, :, :], g.t["c_rope"]).then_inc(s_w, 16)
                sp.dma_start(g.wo0[:, :, :], g.t["wo0"].rearrange("(c p) n -> p c n", p=P)).then_inc(s_wo, 16)
                sp.wait_ge(s_wo, 16)

            @block.tensor
            def _(pe):
                pe.wait_ge(s_w, 32)
                for t in range(NT):
                    if t >= 2:
                        pe.wait_ge(s_rot, t - 1)
                        pe.wait_ge(s_v, t - 1)
                    for half in range(2):
                        cols = slice(0, 512) if half == 0 else slice(512, 768)
                        for c_ in range(DC):
                            ins = pe.matmul(g.bank[2 * half + t % 2][:, 0, 0:cols.stop - cols.start],
                                            g.xT[:, c_, t * P:(t + 1) * P], w[:, c_, cols],
                                            start=(c_ == 0), stop=(c_ == DC - 1))
                    ins.then_inc(s_mm, 1)

            @block.vector
            def _(dve):
                dve.wait_ge(s_w, 32)

                def low(t):
                    dve.wait_ge(s_add, t + 1)
                    dve.wait_ge(s_hi, t + 1)
                    r = rot[t % 2][:, 0, :].rearrange("p (q h d) -> p q h d", q=2, h=H)
                    for q in range(2):
                        ins = dve.tensor_tensor(g.qk[:, t, q, :, 1, :], r[:, q], g.qk[:, t, q, :, 0, :],
                                                ALU.subtract)
                    ins.then_inc(s_lo, 1)

                for t in range(NT):
                    dve.wait_ge(s_mm, t + 1)
                    ps = g.bank[t % 2][:, 0, :]
                    r = rot[t % 2]
                    if t >= 2:
                        dve.wait_ge(s_lo, t - 1)
                    cs = rope[:, t % BT, 0, :].unsqueeze(1).to_broadcast([P, 2 * H, DH0])
                    dve.tensor_tensor(r[:, 0, :].rearrange("p (h d) -> p h d", d=DH0),
                                      ps.rearrange("p (h d) -> p h d", d=DH0), cs, ALU.mult)
                    for e in range(2):
                        sn = rope[:, t % BT, 1, e::2].unsqueeze(1).to_broadcast([P, 2 * H, DH0 // 2])
                        ins = dve.tensor_tensor(
                            r[:, 1, :].rearrange("p (h i two) -> p h i two", i=DH0 // 2, two=2)[:, :, :, e],
                            ps.rearrange("p (h i two) -> p h i two", i=DH0 // 2, two=2)[:, :, :, 1 - e],
                            sn, ALU.mult)
                    ins.then_inc(s_rot, 1)
                    if t >= 1:
                        low(t - 1)
                low(NT - 1)

            @block.gpsimd
            def _(pool):
                for t in range(NT):
                    pool.wait_ge(s_rot, t + 1)
                    r = rot[t % 2]
                    pool.tensor_tensor(r[:, 0, :], r[:, 0, :], r[:, 1, :], ALU.add).then_inc(s_add, 1)

            @block.scalar
            def _(act):
                for t in range(NT):
                    act.wait_ge(s_mm, t + 1)
                    act.activation(g.v0[:, t, :], g.bank[2 + t % 2][:, 0, 0:D], ACT.Copy).then_inc(s_v, 1)
                    act.wait_ge(s_add, t + 1)
                    r = rot[t % 2][:, 0, :].rearrange("p (q h d) -> p q h d", q=2, h=H)
                    for q in range(2):
                        ins = act.activation(g.qk[:, t, q, :, 0, :], r[:, q], ACT.Copy)
                    ins.then_inc(s_hi, 1)


def head_steps(ahead):
    steps = []
    for j in range(BT + 2):
        if j < BT:
            steps.append(("scores", j))
        if j == BT:
            steps += [("ahead", k) for k in range(ahead)]
        if 1 <= j <= BT:
            steps.append(("turn", j - 1))
        if j >= 2:
            steps.append(("values", j - 2))
    return steps


def attention(nc, g, tag, b, layer):
    dh = DH1 if layer else DH0
    NCH = 6 if layer else 4
    GU = BT + NCH
    blocks = [BT - j for j in range(BT)]
    chunks = [-(-n // 4) for n in blocks]
    first = [sum(chunks[:j]) for j in range(BT + 1)]
    TC = first[BT]
    s_ready, m_ready, e_ready, r_ready, t_ready, g_ready = \
        [g.sem(f"{tag}_{n}") for n in ("s_ready", "m_ready", "e_ready", "r_ready", "t_ready", "g_ready")]
    g_act, g_dve = g.sem(f"{tag}_g_act"), g.sem(f"{tag}_g_dve")
    t_dve, t_act = g.sem(f"{tag}_t_dve"), g.sem(f"{tag}_t_act")
    w_in = [g.sem(f"{tag}_w{i}") for i in range(2)]
    N0 = b * H
    W1 = 16 if layer else 4
    steps = head_steps(NCH)
    takers = [st for st in steps if st[0] in ("values", "ahead")]
    g_use = {st: NCH + n for n, st in enumerate(takers)}

    def values_use(j, more):
        return g_use["values", j] - (0 if more or j < BT - 2 else NCH)

    with ExitStack() as c:
        probs = [g.sb(f"{tag}{b}_p{i}", [P, S], F32, c) for i in range(2)]
        turned = [g.sb(f"{tag}{b}_pt{i}", [P, S], F32, c) for i in range(2)]
        rows, qdt = (P, F32) if layer else (64, F16)
        qT = [g.sb(f"{tag}{b}_q{i}", [rows, S], qdt, c) for i in range(2)]
        kT = [g.sb(f"{tag}{b}_k{i}", [rows, S], qdt, c) for i in range(2)]
        negm = g.sb(f"{tag}{b}_negm", [P, 2, BT], F32, c)
        rsum = g.sb(f"{tag}{b}_rsum", [P, 2, BT], F32, c)
        rinv = g.sb(f"{tag}{b}_rinv", [P, 2, BT], F32, c)
        S_ps = [g.bank[0], g.bank[1]]
        T_ps = [g.bank[2][:, 0, :], g.bank[2][:, 1, :]]
        G_ps = [g.bank[3][:, 0, :], g.bank[3][:, 1, :]]

        def all_heads(eng, head):
            with eng.Fori(0, H // 2 - 1) as pair:
                head(eng, pair * 2, 0, True)
                head(eng, pair * 2 + 1, 1, True)
            head(eng, H - 2, 0, True)
            head(eng, H - 1, 1, False)

        def steps_of(more):
            return [st for st in steps if more or st[0] != "ahead"]

        def prep_pe(pe, k, par, ps):
            if layer:
                w = g.wh[par]
                if k < 4:
                    for c_ in range(DC):
                        ins = pe.matmul(ps, w[:, c_, (k // 2) * P:(k // 2 + 1) * P],
                                        g.xT[:, c_, b * S + (k % 2) * 512:b * S + (k % 2 + 1) * 512],
                                        start=(c_ == 0), stop=(c_ == DC - 1))
                else:
                    for j in range(4):
                        t = b * BT + (k - 4) * 4 + j
                        for c_ in range(DC):
                            ins = pe.matmul(ps[:, j * P:(j + 1) * P], g.xT[:, c_, t * P:(t + 1) * P],
                                            w[:, c_, 2 * P:3 * P], start=(c_ == 0), stop=(c_ == DC - 1))
            else:
                for j in range(4):
                    ins = pe.matmul(ps[0:64, j * P:(j + 1) * P], g.qh[par][:, (k % 2) * 4 + j, k // 2, :],
                                    g.identh[:, :], start=True, stop=True)
            return ins

        def prep_evac(eng, k, par, ps, h, is_act):
            cols = slice((k % 2) * 512, (k % 2 + 1) * 512)
            if layer and k >= 4:
                dst = g.vh[par][:, (k - 4) * 4:(k - 3) * 4, :].rearrange("p t d -> p (t d)")
                return eng.activation(dst, ps, ACT.Copy) if is_act else eng.tensor_copy(dst, ps)
            dst = (qT if k < 2 else kT)[par][:, cols]
            if not layer:
                scale = 1.0 if k < 2 else float(DH0) ** -0.5
                if is_act:
                    return eng.activation(dst, ps[0:64, :], ACT.Copy, scale=scale)
                return eng.tensor_scalar(dst, ps[0:64, :], scale, None, ALU.mult)
            bias = (g.bq if k < 2 else g.bk)[:, ds(h, 1)]
            scale = float(DH1) ** -0.5 if k < 2 else 1.0
            if is_act:
                return eng.activation(dst, ps, ACT.Identity, bias=bias, scale=scale)
            return eng.tensor_scalar(dst, ps, scale, bias, ALU.mult, ALU.add)

        with nc.Block() as block:
            if layer:
                @block.sync
                def _(sp):
                    def fetch(h, par, refill):
                        if refill:
                            sp.wait_ge(s_ready, (h + (N0 - 2)) * BT + 1)
                        sp.dma_start(g.wh[par][:, :, :], g.t["wqkv1"][ds(h, 1), :, :, :].rearrange(
                            "o p c n -> (o p) c n")).then_inc(w_in[par], 16)
                    fetch(0, 0, False)
                    fetch(1, 1, False)
                    with sp.Fori(1, H // 2) as pair:
                        fetch(pair * 2, 0, True)
                        fetch(pair * 2 + 1, 1, True)
            else:
                @block.gpsimd
                def _(pool):
                    def fetch(h, par, refill):
                        if refill:
                            pool.wait_ge(s_ready, (h + (N0 - 2)) * BT + 1)
                        src = g.qk[:, b * BT:(b + 1) * BT, :, :, :, :].rearrange("p t q h a d -> p t q (h a d)")
                        for a in range(2):
                            dst = g.qh[par][:, :, 0, a * 2 * DH0:(a + 1) * 2 * DH0]
                            pool.tensor_copy(dst, src[:, :, 0, ds(h * (2 * DH0), 2 * DH0)]).then_inc(w_in[par], 1)
                            dst = g.qh[par][:, :, 1, a * 2 * DH0:(a + 1) * 2 * DH0].rearrange(
                                "p t (r d) -> p t r d", r=2)
                            part = src[:, :, 1, ds(h * (2 * DH0) + a * DH0, DH0)]
                            pool.tensor_copy(dst, part.unsqueeze(2).to_broadcast([P, BT, 2, DH0])
                                             ).then_inc(w_in[par], 1)
                    fetch(0, 0, False)
                    fetch(1, 1, False)
                    with pool.Fori(1, H // 2) as pair:
                        fetch(pair * 2, 0, True)
                        fetch(pair * 2 + 1, 1, True)

            @block.tensor
            def _(pe):
                if b == 0:
                    pe.nop().then_inc(t_ready, TC)
                    pe.nop().then_inc(g_ready, GU)
                pe.wait_ge(w_in[0], N0 // 2 * W1 + W1)
                for k in range(NCH):
                    if k >= 2:
                        pe.wait_ge((g_act, g_dve)[k % 2], N0 * GU // 2 + k // 2)
                    prep_pe(pe, k, 0, G_ps[k % 2]).then_inc(g_ready, 1)
                pe.wait_ge(g_act, N0 * GU // 2 + NCH // 2)
                pe.wait_ge(g_dve, N0 * GU // 2 + NCH // 2)

                def head(eng, h, par, more):
                    for kind, j in steps_of(more):
                        if kind == "scores":
                            n, i = blocks[j], blocks[j] - 1
                            if j == 0:
                                eng.wait_ge(g_act, (h + N0) * (GU // 2) + (NCH // 2 - 1))
                                eng.wait_ge(g_dve, (h + N0) * (GU // 2) + (NCH // 2 - 1))
                            eng.wait_ge(e_ready, (h + N0) * BT + (BT + j - 1))
                            ps = S_ps[j % 2]
                            for c4 in range(-(-n // 4)):
                                w_ = min(4, n - 4 * c4) * P
                                diag = c4 == i // 4
                                eng.matmul(ps[:, c4, 0:w_], qT[par][:, i * P:(i + 1) * P],
                                           kT[par][:, c4 * 512:c4 * 512 + w_], start=True, stop=not diag)
                                if diag:
                                    o = (i % 4) * P
                                    ins = eng.matmul(ps[:, c4, o:o + P], g.identb[:, :], g.maskb[:, :],
                                                     start=False, stop=True)
                            ins.then_inc(s_ready, 1)
                        elif kind == "turn":
                            eng.wait_ge(e_ready, (h + N0) * BT + (BT + j + 1))
                            for k in range(chunks[j]):
                                ch = first[j] + k
                                eng.wait_ge((t_dve, t_act)[ch % 2], (h + N0) * (TC // 2) + (TC // 2 + ch // 2))
                                for q in range(4 * k, min(4 * k + 4, blocks[j])):
                                    ins = eng.transpose(T_ps[ch % 2][:, (q % 4) * P:(q % 4 + 1) * P],
                                                        probs[j % 2][:, q * P:(q + 1) * P], g.identf[:, :])
                                ins.then_inc(t_ready, 1)
                        elif kind == "values":
                            last = first[j + 1]
                            eng.wait_ge(t_dve, (h + N0) * (TC // 2) + (TC // 2 + (last + 1) // 2))
                            eng.wait_ge(t_act, (h + N0) * (TC // 2) + (TC // 2 + last // 2))
                            u = values_use(j, more)
                            eng.wait_ge((g_act, g_dve)[u % 2], (h + N0) * (GU // 2) + u // 2)
                            for q in range(blocks[j]):
                                v = g.vh[par][:, q, :] if layer else g.v0[:, b * BT + q, ds(h * DH0, DH0)]
                                ins = eng.matmul(G_ps[u % 2][:, 0:dh], turned[j % 2][:, q * P:(q + 1) * P], v,
                                                 start=(q == 0), stop=(q == blocks[j] - 1))
                            ins.then_inc(g_ready, 1)
                        else:
                            u = g_use[kind, j]
                            if j == 0:
                                eng.wait_ge(w_in[1 - par], (h + N0) * (W1 // 2) + (W1 + par * W1 // 2))
                            eng.wait_ge((g_act, g_dve)[u % 2], (h + N0) * (GU // 2) + u // 2)
                            prep_pe(eng, j, 1 - par, G_ps[u % 2]).then_inc(g_ready, 1)
                all_heads(pe, head)

            def turned_copy(eng, is_act, h, j):
                for k in range(chunks[j]):
                    ch = first[j] + k
                    if (ch % 2 == 1) != is_act:
                        continue
                    eng.wait_ge(t_ready, (h + N0) * TC + (TC + ch + 1))
                    if j >= 2:
                        eng.wait_ge(g_ready, (h + N0) * GU + (GU + g_use["values", j - 2] + 1))
                    else:
                        eng.wait_ge(g_ready, (h + N0) * GU + (g_use["values", BT - 2 + j] + 1))
                    w_ = min(4, blocks[j] - 4 * k) * P
                    dst = turned[j % 2][:, k * 512:k * 512 + w_]
                    src = T_ps[ch % 2][:, 0:w_]
                    ins = eng.activation(dst, src, ACT.Copy) if is_act else eng.tensor_copy(dst, src)
                    ins.then_inc(t_act if is_act else t_dve, 1)

            def chunk_out(eng, is_act, h, par, j):
                u = g_use["ahead", j]
                if (u % 2 == 0) == is_act:
                    eng.wait_ge(g_ready, (h + N0) * GU + (GU + u + 1))
                    prep_evac(eng, j, 1 - par, G_ps[u % 2], h + 1, is_act).then_inc(
                        g_act if is_act else g_dve, 1)

            def z_out(eng, is_act, h, par, j, more):
                u = values_use(j, more)
                if (u % 2 == 0) == is_act:
                    eng.wait_ge(g_ready, (h + N0) * GU + (GU + u + 1))
                    eng.wait_ge(r_ready, (h + N0) * BT + (j + 1))
                    t = blocks[j] - 1 + (0 if layer else b * BT)
                    dst = g.z[:, t, ds(h * dh, dh)]
                    src = G_ps[u % 2][:, 0:dh]
                    if is_act:
                        ins = eng.activation(dst, src, ACT.Copy, scale=rinv[:, par, j:j + 1])
                    else:
                        ins = eng.tensor_scalar(dst, src, rinv[:, par, j:j + 1], None, ALU.mult)
                    ins.then_inc(g_act if is_act else g_dve, 1)

            @block.scalar
            def _(act):
                if b == 0:
                    act.nop().then_inc(e_ready, BT)
                    act.nop().then_inc(t_act, TC // 2)
                for k in range(0, NCH, 2):
                    act.wait_ge(g_ready, (N0 + 1) * GU + k + 1)
                    prep_evac(act, k, 0, G_ps[0], 0, True).then_inc(g_act, 1)

                def head(eng, h, par, more):
                    for kind, j in steps_of(more):
                        if kind == "scores":
                            eng.wait_ge(m_ready, (h + N0) * BT + (j + 1))
                            if j >= 2:
                                eng.wait_ge(t_ready, (h + N0) * TC + (TC + first[j - 1]))
                            else:
                                eng.wait_ge(t_ready, (h + N0) * TC + first[BT - 1 + j])
                            n = blocks[j] * P
                            eng.activation(probs[j % 2][:, 0:n],
                                           S_ps[j % 2].rearrange("p a n -> p (a n)")[:, 0:n], ACT.Exp,
                                           bias=negm[:, par, j:j + 1],
                                           accum_out=rsum[:, par, j:j + 1]).then_inc(e_ready, 1)
                        elif kind == "turn":
                            turned_copy(eng, True, h, j)
                        elif kind == "values":
                            z_out(eng, True, h, par, j, more)
                        else:
                            chunk_out(eng, True, h, par, j)
                all_heads(act, head)

            @block.vector
            def _(dve):
                if b == 0:
                    dve.nop().then_inc(t_dve, TC // 2)
                for k in range(1, NCH, 2):
                    dve.wait_ge(g_ready, (N0 + 1) * GU + k + 1)
                    prep_evac(dve, k, 0, G_ps[1], 0, False).then_inc(g_dve, 1)

                def head(eng, h, par, more):
                    for kind, j in steps_of(more):
                        if kind == "scores":
                            eng.wait_ge(s_ready, (h + N0) * BT + (j + 1))
                            n = blocks[j] * P
                            eng.tensor_reduce(negm[:, par, j:j + 1],
                                              S_ps[j % 2].rearrange("p a n -> p (a n)")[:, 0:n],
                                              AX.X, ALU.max, negate=True).then_inc(m_ready, 1)
                        elif kind == "turn":
                            turned_copy(eng, False, h, j)
                        elif kind == "values":
                            eng.wait_ge(e_ready, (h + N0) * BT + (BT + j + 1))
                            eng.reciprocal(rinv[:, par, j:j + 1], rsum[:, par, j:j + 1]).then_inc(r_ready, 1)
                            z_out(eng, False, h, par, j, more)
                        else:
                            chunk_out(eng, False, h, par, j)
                all_heads(dve, head)


def proj_out(nc, g, tag, layer, b=0):
    NC = H if layer else DC
    GR = -(-NC // 4)
    tiles = list(range(BT)) if layer else list(range(NT))
    w = g.wo1 if layer else g.wo0
    s_t, s_c, s_mm, s_add, s_w = [g.sem(f"{tag}_{n}") for n in ("turn", "copy", "mm", "add", "w")]
    s_bo = g.sem(f"{tag}_bo")
    N0 = b * BT
    with ExitStack() as c:
        zT = [g.sb(f"{tag}{b}_zT{i}", [P, NC, P], F32, c) for i in range(2)]
        with nc.Block() as block:
            @block.tensor
            def _(pe):
                def out(n):
                    pe.wait_ge(s_c, (N0 + n + 1) * GR)
                    if n >= 2:
                        pe.wait_ge(s_add, N0 + n - 1)
                    for k in range(NC):
                        ins = pe.matmul(g.bank[2 + n % 2][:, 0, 0:D], zT[n % 2][:, k, :], w[:, k, :],
                                        start=(k == 0), stop=(k == NC - 1))
                    ins.then_inc(s_mm, 1)

                for n, t in enumerate(tiles):
                    for r in range(GR):
                        m = n * GR + r
                        if m >= 2:
                            pe.wait_ge(s_c, N0 * GR + m - 1)
                        nk = min(4, NC - 4 * r)
                        for k in range(nk):
                            ins = pe.transpose(g.bank[m % 2][:, 0, k * P:(k + 1) * P],
                                               g.z[:, t, (4 * r + k) * P:(4 * r + k + 1) * P], g.identf[:, :])
                        ins.then_inc(s_t, 1)
                    if n:
                        out(n - 1)
                out(len(tiles) - 1)

            @block.vector
            def _(dve):
                def add(n):
                    t = b * BT + tiles[n] if layer else tiles[n]
                    dve.wait_ge(s_mm, N0 + n + 1)
                    if layer:
                        dve.wait_ge(s_bo, N0 + n + 1)
                    dve.tensor_tensor(g.x[:, t, :], g.bank[2 + n % 2][:, 0, 0:D], g.x[:, t, :],
                                      ALU.add).then_inc(s_add, 1)

                for n, t in enumerate(tiles):
                    for r in range(GR):
                        m = n * GR + r
                        nk = min(4, NC - 4 * r)
                        dve.wait_ge(s_t, N0 * GR + m + 1)
                        if n >= 2:
                            dve.wait_ge(s_mm, N0 + n - 1)
                        dst = zT[n % 2][:, 4 * r:4 * r + nk, :]
                        src = g.bank[m % 2][:, 0, 0:nk * P].rearrange("p (k q) -> p k q", k=nk)
                        if layer:
                            bv = g.bv[:, 4 * r:4 * r + nk].unsqueeze(2).to_broadcast([P, nk, P])
                            dve.tensor_tensor(dst, src, bv, ALU.add).then_inc(s_c, 1)
                        else:
                            dve.tensor_copy(dst, src).then_inc(s_c, 1)
                    if n:
                        add(n - 1)
                add(len(tiles) - 1)

            if layer:
                @block.gpsimd
                def _(pool):
                    for n, t in enumerate(tiles):
                        pool.tensor_tensor(g.x[:, b * BT + t, :], g.x[:, b * BT + t, :], g.bo[:, :],
                                           ALU.add).then_inc(s_bo, 1)


def ffn_weights(nc, g, c1):
    g.wf = g.sb("wf", [P, DC, D], F32, c1)
    g.lnw = g.sb("lnw", [P, DC], F32, c1)
    g.lnb = g.sb("lnb", [P, DC], F32, c1)
    g.beta = g.sb("beta", [P, D], F32, c1)
    s_in, s_ch, s_ab, s_all = [g.sem(f"fw_{n}") for n in ("in", "chain", "absmax", "all")]
    s_sg = g.sem("fw_sign")
    with ExitStack() as c:
        w = g.sb("fw_w", [P, DC, D], F32, c)
        gam = g.sb("fw_gamma", [P, D], F32, c)
        am = g.sb("fw_am", [P, 2], F32, c)
        with nc.Block() as block:
            @block.sync
            def _(sp):
                sp.dma_start(w[:, :, :], g.t["ffn_w"].rearrange("(c p) n -> p c n", p=P)).then_inc(s_in, 16)
                sp.dma_start(gam[:, :], g.t["gamma"].partition_broadcast(P)).then_inc(s_in, 16)
                sp.dma_start(g.beta[:, :], g.t["beta"].partition_broadcast(P)).then_inc(s_in, 16)
                sp.dma_start(g.lnw[:, :], g.t["ln_w"]).then_inc(s_in, 16)
                sp.dma_start(g.lnb[:, :], g.t["ln_b"]).then_inc(s_in, 16)

            @block.vector
            def _(dve):
                dve.wait_ge(s_in, 80)
                dve.tensor_reduce(am[:, 0:1], w[:, :, :], AX.XY, ALU.max,
                                  apply_absolute_value=True).then_inc(s_ab, 1)
                dve.wait_ge(s_all, 1)
                dve.tensor_scalar(gam[:, :], gam[:, :], am[:, 1:2], None, ALU.mult).then_inc(s_ch, 1)
                dve.wait_ge(s_ch, 1)
                dve.wait_ge(s_sg, 1)
                dve.tensor_tensor(g.wf[:, :, :], g.wf[:, :, :],
                                  gam[:, :].unsqueeze(1).to_broadcast([P, DC, D]), ALU.mult).then_inc(s_ch, 1)
                dve.wait_ge(s_ch, 2)

            @block.gpsimd
            def _(pool):
                pool.wait_ge(s_ab, 1)
                pool.partition_all_reduce(am[:, 1:2], am[:, 0:1], P, bass.bass_isa.ReduceOp.max).then_inc(s_all, 1)

            @block.scalar
            def _(act):
                act.wait_ge(s_in, 80)
                act.activation(g.wf[:, :, :], w[:, :, :], ACT.Sign).then_inc(s_sg, 1)


def l0_ffn(nc, g):
    s_mm, s_bt, s_add = [g.sem(f"f0_{n}") for n in ("mm", "beta", "add")]
    with nc.Block() as block:
        @block.tensor
        def _(pe):
            for t in range(NT):
                if t >= 4:
                    pe.wait_ge(s_add, t - 3)
                for c_ in range(DC):
                    ins = pe.matmul(g.bank[t % 4][:, 0, 0:D], g.xT[:, c_, t * P:(t + 1) * P], g.wf[:, c_, :],
                                    start=(c_ == 0), stop=(c_ == DC - 1))
                ins.then_inc(s_mm, 1)

        @block.gpsimd
        def _(pool):
            for t in range(NT):
                pool.tensor_tensor(g.x[:, t, :], g.x[:, t, :], g.beta[:, :], ALU.add).then_inc(s_bt, 1)

        @block.vector
        def _(dve):
            for t in range(NT):
                dve.wait_ge(s_mm, t + 1)
                dve.wait_ge(s_bt, t + 1)
                dve.tensor_tensor(g.x[:, t, :], g.bank[t % 4][:, 0, 0:D], g.x[:, t, :], ALU.add).then_inc(s_add, 1)


def l1_buffers(nc, g, c2):
    g.wh = [g.sb(f"wh{i}", [P, DC, 3 * P], F32, c2) for i in range(2)]
    g.vh = [g.sb(f"vh{i}", [P, BT, P], F32, c2) for i in range(2)]
    g.z = g.sb("z1", [P, BT, H * DH1], F32, c2)
    g.wo1 = g.sb("wo1", [P, H, D], F32, c2)
    g.bq, g.bk, g.bv = [g.sb(f"b{n}1", [P, H], F32, c2) for n in "qkv"]
    g.bo = g.sb("bo1", [P, D], F32, c2)
    s_in, s_b = g.sem("l1_in"), g.sem("l1_bias")
    with nc.Block() as block:
        @block.sync
        def _(sp):
            for dst, name in ((g.bq, "b_Q"), (g.bk, "b_K"), (g.bv, "b_V")):
                sp.dma_start(dst[:, :], g.t[name]).then_inc(s_in, 16)
            sp.dma_start(g.bo[:, :], g.t["b_O"].partition_broadcast(P)).then_inc(s_in, 16)
            sp.dma_start(g.wo1[:, :, :], g.t["wo1"]).then_inc(s_in, 16)
            sp.wait_ge(s_in, 80)

        @block.vector
        def _(dve):
            dve.wait_ge(s_in, 80)
            dve.tensor_scalar(g.bq[:, :], g.bq[:, :], float(DH1) ** -0.5, None, ALU.mult).then_inc(s_b, 1)
            dve.wait_ge(s_b, 1)


OOB = 16384
XB = 8
XG = 4


def moe(nc, g, out):
    with ExitStack() as c:
        g.xn = g.sb("xn", [P, NT, D], F32, c)
        g.wk = g.sb("wk", [P, NT, 8], F32, c)
        g.widx = g.sb("widx", [P, K, NT], U32, c)
        g.ridx = g.sb("ridx", [P, K, NT], U32, c)
        g.wgu = [g.sb(f"wgu{i}", [P, DC, 2 * M], F32, c) for i in range(XB)]
        g.wd = [g.sb(f"wd{i}", [MH, 2, D], F32, c) for i in range(XB)]
        norm(nc, g, "n3", "keep")
        with ExitStack() as c2:
            router(nc, g, c2)
        with ExitStack() as c3:
            experts(nc, g, c3)
        with ExitStack() as c4:
            combine(nc, g, c4, out)


def router(nc, g, c):
    gate = g.sb("gate", [P, DC, E], F32, c)
    sgu = g.sb("sgu", [P, DC, 2 * MS], F32, c)
    sd = g.sb("sd", [MH, NMS, D], F32, c)
    before = g.sb("before", [P, P], F32, c)
    beforeb = g.sb("beforeb", [P, P], BF16, c)
    onesb = g.sb("onesb", [P, P], BF16, c)
    iota = g.sb("iota", [P, E], F32, c)
    base = g.sb("slot_base", [P, E], F32, c)
    sc = g.sb("scores", [P, NT, E], F32, c)
    msc = g.sb("masked_scores", [P, NT, E], F32, c)
    tmp = g.sb("r_tmp", [P, NT, E], F32, c)
    slot = g.sb("slot", [P, NT, E], F32, c)
    oh = g.sb("onehot", [P, K, NT, E], BF16, c)
    mask = g.sb("mask", [P, NT, E], BF16, c)
    cm = g.sb("cumulated", [P, NT + 1, E], BF16, c)
    small = g.sb("r_small", [P, 4, NT], F32, c)
    gmx = g.sb("gmx", [P, NT, NG], F32, c)
    g8 = g.sb("g8", [P, NT, 8], F32, c)
    gi = g.sb("gi", [P, NT, 8], U32, c)
    gif = g.sb("gif", [P, NT, 8], F32, c)
    gmask = g.sb("gmask", [P, 2, NT, NG], F32, c)
    cnt = g.sb("cnt", [P, E], F32, c)
    v = g.sb("v", [P, K, NT], F32, c)
    v2 = g.sb("v2", [P, K, NT], F32, c)
    hT = g.sb("shared_h", [MH, NMS, T], F32, c)
    sg = [g.sb(f"shared_g{i}", [MH, 512], F32, c) for i in range(2)]
    s_in, s_ch, s_lg, s_ex, s_m, s_pos, s_w = [g.sem(f"r_{n}") for n in
                                              ("in", "chain", "logits", "exp", "mask", "pos", "weights")]
    s_gu, s_sil, s_h, s_dn, s_add, s_idx, s_sc, s_cst = [g.sem(f"r_{n}") for n in
                                                       ("gu", "silu", "h", "down", "add", "idx", "scatter", "const")]
    g.s_wgu = [g.sem(f"x_wgu{i}") for i in range(XB)]
    logits = g.bank[0].rearrange("p a n -> p (a n)").rearrange("p (t e) -> p t e", e=E)
    pos = g.bank[1].rearrange("p a n -> p (a n)").rearrange("p (t e) -> p t e", e=E)
    count = g.bank[0][:, 0, 0:E]
    NQ = T // 512
    with nc.Block() as block:
        @block.sync
        def _(sp):
            for dst, name in ((gate, "gate"), ):
                sp.dma_start(dst[:, :, :], g.t[name].rearrange("(c p) n -> p c n", p=P)).then_inc(s_in, 16)
            sp.dma_start(before[:, :], g.t["c_before"]).then_inc(s_in, 16)
            sp.dma_start(iota[:, :], g.t["c_iota"]).then_inc(s_in, 16)
            sp.dma_start(sgu[:, :, :], g.t["sgu"]).then_inc(s_w, 16)
            sp.dma_start(sd[:, :, :], g.t["sd"]).then_inc(s_w, 16)
            for e in range(XB):
                sp.dma_start(g.wgu[e][:, :, :], g.t["wgu"][e]).then_inc(g.s_wgu[e], 16)
                sp.dma_start(g.wd[e][:, :, :], g.t["wd"][e]).then_inc(g.s_wgu[e], 16)

        gu_steps = [(q, m) for q in range(NQ) for m in range(NMS)]

        @block.tensor
        def _(pe):
            pe.wait_ge(s_in, 48)
            for t in range(NT):
                for c_ in range(DC):
                    ins = pe.matmul(logits[:, t, :], g.xT[:, c_, t * P:(t + 1) * P], gate[:, c_, :],
                                    start=(c_ == 0), stop=(c_ == DC - 1))
            ins.then_inc(s_lg, 1)
            pe.wait_ge(s_w, 32)

            def gate_up(n):
                q, m = gu_steps[n]
                if n >= 2:
                    pe.wait_ge(s_h, n - 1)
                for half in range(2):
                    for c_ in range(DC):
                        ins = pe.matmul(g.bank[2 + half][0:MH, n % 2, :],
                                        sgu[:, c_, half * MS + m * MH:half * MS + (m + 1) * MH],
                                        g.xT[:, c_, q * 512:(q + 1) * 512],
                                        start=(c_ == 0), stop=(c_ == DC - 1))
                ins.then_inc(s_gu, 1)

            for n in range(len(gu_steps)):
                gate_up(n)
            pe.wait_ge(s_m, 1)
            for half in range(2):
                pe.matmul(g.bank[1][:, half, :], beforeb[:, :],
                          mask[:, half * 8:half * 8 + 8, :].rearrange("p t e -> p (t e)"), start=True, stop=False)
                pe.matmul(g.bank[1][:, half, :], onesb[:, :],
                          cm[:, half * 8:half * 8 + 8, :].rearrange("p t e -> p (t e)"), start=False, stop=True)
            pe.matmul(count, onesb[:, :], cm[:, NT, :], start=True, stop=True).then_inc(s_pos, 1)
            for t in range(NT):
                if t == 0:
                    pe.wait_ge(s_h, len(gu_steps))
                if t >= 2:
                    pe.wait_ge(s_add, t - 1)
                for m in range(NMS):
                    ins = pe.matmul(g.bank[2 + t % 2][:, 0, 0:D], hT[:, m, t * P:(t + 1) * P], sd[:, m, :],
                                    start=(m == 0), stop=(m == NMS - 1))
                ins.then_inc(s_dn, 1)

        @block.scalar
        def _(act):
            act.wait_ge(s_ex, 1)
            act.activation(sc[:, :, :], tmp[:, :, :], ACT.Exp).then_inc(s_ex, 1)
            for n in range(len(gu_steps)):
                act.wait_ge(s_gu, n + 1)
                if n >= 2:
                    act.wait_ge(s_h, n - 1)
                act.activation(sg[n % 2][:, :], g.bank[2][0:MH, n % 2, :], ACT.Silu).then_inc(s_sil, 1)

        @block.vector
        def _(dve):
            n = 0

            def chained(ins):
                nonlocal n
                n += 1
                ins.then_inc(s_ch, 1)
                dve.wait_ge(s_ch, n)

            done = 0

            def shared(upto):
                nonlocal done
                while done < upto:
                    q, m = gu_steps[done]
                    dve.wait_ge(s_sil, done + 1)
                    dve.tensor_tensor(hT[:, m, q * 512:(q + 1) * 512], g.bank[3][0:MH, done % 2, :],
                                      sg[done % 2][:, :], ALU.mult).then_inc(s_h, 1)
                    done += 1

            dve.wait_ge(s_in, 48)
            chained(dve.tensor_copy(beforeb[:, :], before[:, :]))
            chained(dve.memset(onesb[:, :], 1.0))
            chained(dve.memset(cm[:, 0, :], 0.0))
            dve.tensor_scalar(base[:, :], iota[:, :], float(C), None, ALU.mult).then_inc(s_cst, 1)
            dve.wait_ge(s_cst, 1)
            dve.wait_ge(s_lg, 1)
            mx, rs = small[:, 0, :], small[:, 1, :]
            chained(dve.tensor_reduce(mx, logits, AX.X, ALU.max))
            dve.tensor_tensor(tmp[:, :, :], logits, mx.unsqueeze(2).to_broadcast([P, NT, E]),
                              ALU.subtract).then_inc(s_ex, 1)
            dve.wait_ge(s_ex, 2)
            chained(dve.tensor_reduce(rs, sc[:, :, :], AX.X, ALU.add))
            chained(dve.reciprocal(rs, rs))
            chained(dve.tensor_tensor(sc[:, :, :], sc[:, :, :], rs.unsqueeze(2).to_broadcast([P, NT, E]), ALU.mult))
            shared(2)
            chained(dve.tensor_reduce(gmx[:, :, :], sc.rearrange("p t (a b) -> p t a b", b=GS), AX.X, ALU.max))
            for t in range(NT):
                ins = dve.max(g8[:, t, :], gmx[:, t, :])
            chained(ins)
            for t in range(NT):
                ins = dve.max_index(gi[:, t, :], g8[:, t, :], gmx[:, t, :])
            chained(ins)
            chained(dve.tensor_copy(gif[:, :, :], gi[:, :, :]))
            gid = iota[:, 0:NG].unsqueeze(1).to_broadcast([P, NT, NG])
            for k in range(TG):
                chained(dve.tensor_tensor(gmask[:, min(k, 1)], gid, gif[:, :, k:k + 1].to_broadcast([P, NT, NG]),
                                          ALU.is_equal))
                if k:
                    chained(dve.tensor_tensor(gmask[:, 0], gmask[:, 0], gmask[:, 1], ALU.add))
            chained(dve.tensor_tensor(msc.rearrange("p t (a b) -> p (t a) b", b=GS),
                                      sc.rearrange("p t (a b) -> p (t a) b", b=GS),
                                      gmask[:, 0].rearrange("p t a -> p (t a)").unsqueeze(2).to_broadcast(
                                          [P, NT * NG, GS]), ALU.mult))
            shared(4)
            for t in range(NT):
                ins = dve.max(g.wk[:, t, :], msc[:, t, :])
            chained(ins)
            for t in range(NT):
                ins = dve.max_index(gi[:, t, :], g.wk[:, t, :], msc[:, t, :])
            chained(ins)
            chained(dve.tensor_copy(gif[:, :, :], gi[:, :, :]))
            shared(6)
            eid = iota[:, :].unsqueeze(1).to_broadcast([P, NT, E])
            for k in range(K):
                chained(dve.tensor_tensor(oh[:, k], eid, gif[:, :, k:k + 1].to_broadcast([P, NT, E]), ALU.is_equal))
                if k:
                    chained(dve.tensor_tensor(mask[:, :, :], oh[:, 0] if k == 1 else mask[:, :, :], oh[:, k], ALU.add))
                shared(7 + k)
            for t in range(NT):
                chained(dve.tensor_tensor(cm[:, t + 1, :], cm[:, t, :], mask[:, t, :], ALU.add))
            dve.nop().then_inc(s_m, 1)
            shared(len(gu_steps))
            dve.wait_ge(s_pos, 1)
            chained(dve.tensor_scalar(cnt[:, :], count, -1.0, None, ALU.add))
            chained(dve.tensor_tensor(tmp[:, :, :], pos, cnt[:, :].unsqueeze(1).to_broadcast([P, NT, E]),
                                      ALU.not_equal))
            chained(dve.tensor_scalar(slot[:, :, :], pos, C - 1.5, float(OOB), ALU.is_gt, ALU.mult))
            chained(dve.tensor_tensor(tmp[:, :, :], tmp[:, :, :], slot[:, :, :], ALU.mult))
            chained(dve.tensor_scalar(slot[:, :, :], pos, float(C - 1), None, ALU.min))
            chained(dve.tensor_tensor(slot[:, :, :], slot[:, :, :], tmp[:, :, :], ALU.add))
            chained(dve.tensor_tensor(slot[:, :, :], slot[:, :, :], base[:, :].unsqueeze(1).to_broadcast([P, NT, E]),
                                      ALU.add))
            for k in range(K):
                chained(dve.tensor_tensor(tmp[:, :, :], slot[:, :, :], oh[:, k], ALU.mult))
                chained(dve.tensor_reduce(v[:, k, :], tmp[:, :, :], AX.X, ALU.add))
            chained(dve.tensor_copy(g.widx[:, :, :], v[:, :, :]))
            dve.nop().then_inc(s_idx, 1)
            chained(dve.tensor_scalar(v2[:, :, :], v[:, :, :], float(OOB) - 0.5, -float(OOB), ALU.is_gt, ALU.mult))
            chained(dve.tensor_tensor(v[:, :, :], v[:, :, :], v2[:, :, :], ALU.add))
            chained(dve.tensor_copy(g.ridx[:, :, :], v[:, :, :]))
            for t in range(NT):
                dve.wait_ge(s_dn, t + 1)
                dve.tensor_tensor(g.x[:, t, :], g.bank[2 + t % 2][:, 0, 0:D], g.x[:, t, :], ALU.add).then_inc(s_add, 1)

        @block.gpsimd
        def _(pool):
            pool.wait_ge(g.s_zero, 16 * ZD)
            pool.wait_ge(s_idx, 1)
            for t in range(NT):
                for k in range(K):
                    pool.indirect_dma_start(out=g.xrows, out_offset=bass.IndirectOffsetOnAxis(
                        ap=g.widx[:, k, t:t + 1], axis=0), in_=g.xn[:, t, :], in_offset=None,
                        bounds_check=E * C - 1, oob_is_err=False).then_inc(s_sc, 16)
            pool.wait_ge(s_sc, 16 * NT * K)


def experts(nc, g, c):
    rows = [g.sb(f"x_rows{i}", [C, XG, D], F32, c) for i in range(XB // XG)]
    xeT = [g.sb(f"x_T{i}", [P, 2, DC, C], F32, c) for i in range(2)]
    sg = [g.sb(f"x_sg{i}", [MH, 2, C], F32, c) for i in range(2)]
    h = [g.sb(f"x_h{i}", [MH, 2, C], F32, c) for i in range(2)]
    orow = [g.sb(f"x_o{i}", [C, XG, D], F32, c) for i in range(XB // XG)]
    NR = XB // XG
    s_row = [g.sem(f"x_row{i}") for i in range(NR)]
    s_out = [g.sem(f"x_out{i}") for i in range(NR)]
    s_t, s_tc, s_gu, s_sil, s_h, s_dn, s_o = [g.sem(f"x_{n}") for n in ("t", "tc", "gu", "silu", "h", "down", "o")]
    xv = g.xrows.rearrange("(e c) d -> c e d", c=C)
    ov = g.orows.rearrange("(e c) d -> c e d", c=C)

    with nc.Block() as block:
        @block.sync
        def _(sp):
            for i in range(NR):
                sp.dma_start(rows[i][:, :, :], xv[:, i * XG:(i + 1) * XG, :]).then_inc(s_row[i], 16)
            with sp.Fori(1, E // XB) as i:
                for s in range(XB):
                    if s % XG == 0:
                        sp.wait_ge(s_t, i * (XB // 2) + ((s + XG) // 2 - XB // 2))
                        sp.dma_start(rows[s // XG][:, :, :], xv[:, ds(i * XB + s, XG), :]).then_inc(s_row[s // XG], 16)
                    sp.wait_ge(s_dn, i * XB + (s - XB + 3))
                    sp.dma_start(g.wgu[s][:, :, :], g.t["wgu"][ds(i * XB + s, 1), :, :, :].rearrange(
                        "o p c n -> (o p) c n")).then_inc(g.s_wgu[s], 16)
                    sp.dma_start(g.wd[s][:, :, :], g.t["wd"][ds(i * XB + s, 1), :, :, :].rearrange(
                        "o p c n -> (o p) c n")).then_inc(g.s_wgu[s], 16)

        @block.tensor
        def _(pe):
            def turn_pair(p_num, s):
                if s % XG == 0:
                    pe.wait_ge(s_row[s // XG], p_num * 4 + (16 - 2 * s))
                pe.wait_ge(s_tc, p_num + 1)
                b_ = g.bank[0][:, (s // 2) % 2, :]
                for a in range(2):
                    for c_ in range(DC):
                        o = (a * DC + c_) * C
                        ins = pe.transpose(b_[:, o:o + C], rows[s // XG][:, (s + a) % XG, c_ * P:(c_ + 1) * P],
                                           g.identf[0:C, 0:C])
                ins.then_inc(s_t, 1)

            def gu(e, s, half_e):
                pe.wait_ge(s_tc, half_e + 3)
                pe.wait_ge(g.s_wgu[s], e * 4 + (32 - 4 * s))
                pe.wait_ge(s_h, e + 1)
                b_ = g.bank[1][0:MH, s % 2, :]
                for m in range(4):
                    for c_ in range(DC):
                        ins = pe.matmul(b_[:, m * C:(m + 1) * C], g.wgu[s][:, c_, m * MH:(m + 1) * MH],
                                        xeT[(s // 2) % 2][:, s % 2, c_, :], start=(c_ == 0), stop=(c_ == DC - 1))
                ins.then_inc(s_gu, 1)

            def down(e, s):
                pe.wait_ge(s_h, e + 3)
                pe.wait_ge(s_o, e + 1)
                for m in range(2):
                    ins = pe.matmul(g.bank[2][0:C, s % 2, 0:D], h[s % 2][:, m, :], g.wd[s][:, m, :],
                                    start=(m == 0), stop=(m == 1))
                ins.then_inc(s_dn, 1)

            pe.nop().then_inc(s_gu, 4)
            pe.nop().then_inc(s_dn, 2)
            turn_pair(0, 0)
            gu(0, 0, 0)

            def one_pass(i, more):
                for s in range(XB):
                    if s % 2 == 0 and (more or s + 2 < XB):
                        turn_pair(i * (XB // 2) + (s // 2 + 1), (s + 2) % XB)
                    if more or s + 1 < XB:
                        gu(i * XB + (s + 1), (s + 1) % XB, i * (XB // 2) + (s + 1) // 2)
                    down(i * XB + s, s)

            with pe.Fori(0, E // XB - 1) as i:
                one_pass(i, True)
            one_pass(E // XB - 1, False)

        def walk(eng, step_turn, step_expert, step_down):
            step_turn(0, 0)
            step_expert(0, 0)

            def one_pass(i, more):
                for s in range(XB):
                    if s % 2 == 0 and (more or s + 2 < XB):
                        step_turn(i * (XB // 2) + (s // 2 + 1), (s + 2) % XB)
                    if more or s + 1 < XB:
                        step_expert(i * XB + (s + 1), (s + 1) % XB)
                    step_down(i, i * XB + s, s)

            with eng.Fori(0, E // XB - 1) as i:
                one_pass(i, True)
            one_pass(E // XB - 1, False)

        @block.scalar
        def _(act):
            act.nop().then_inc(s_o, 2)
            for i in range(NR):
                act.nop().then_inc(s_out[i], 16)

            def silu(e, s):
                act.wait_ge(s_gu, e + 5)
                act.wait_ge(s_h, e + 1)
                act.activation(sg[s % 2][:, :, :], g.bank[1][0:MH, s % 2, 0:2 * C].rearrange(
                    "p (m c) -> p m c", c=C), ACT.Silu).then_inc(s_sil, 1)

            def out_rows(i, e, s):
                act.wait_ge(s_dn, e + 3)
                if s % XG == 0:
                    act.wait_ge(s_out[s // XG], i * 16 + 16)
                act.activation(orow[s // XG][:, s % XG, :], g.bank[2][0:C, s % 2, 0:D], ACT.Copy).then_inc(s_o, 1)
                if s % XG == XG - 1:
                    act.wait_ge(s_o, e + 3)
                    act.dma_start(ov[:, ds(e - (XG - 1), XG), :], orow[s // XG][:, :, :]).then_inc(s_out[s // XG], 16)

            walk(act, lambda p_num, s: None, silu, out_rows)
            for i in range(NR):
                act.wait_ge(s_out[i], 16 * (E // XB) + 16)

        @block.vector
        def _(dve):
            dve.nop().then_inc(s_tc, 2)
            dve.nop().then_inc(s_h, 2)

            def turned(p_num, s):
                dve.wait_ge(s_t, p_num + 1)
                dve.wait_ge(s_gu, p_num * 2 + 2)
                dve.tensor_copy(xeT[(s // 2) % 2].rearrange("p a c n -> p (a c n)"),
                                g.bank[0][:, (s // 2) % 2, 0:2 * DC * C]).then_inc(s_tc, 1)

            def product(e, s):
                dve.wait_ge(s_sil, e + 1)
                dve.wait_ge(s_dn, e + 1)
                dve.tensor_tensor(h[s % 2][:, :, :], g.bank[1][0:MH, s % 2, 2 * C:4 * C].rearrange(
                    "p (m c) -> p m c", c=C), sg[s % 2][:, :, :], ALU.mult).then_inc(s_h, 1)

            walk(dve, turned, product, lambda i, e, s: None)


def combine(nc, g, c, out):
    NB = 4
    rows = [g.sb(f"c_rows{i}", [P, K, D], F32, c) for i in range(NB)]
    s_g = [g.sem(f"c_gather{i}") for i in range(NB)]
    s_acc, s_done, s_st = g.sem("c_acc"), g.sem("c_done"), g.sem("c_store")
    ov = out.rearrange("b (n p) d -> p (b n) d", p=P)
    with nc.Block() as block:
        @block.gpsimd
        def _(pool):
            for t in range(NT):
                if t >= NB:
                    pool.wait_ge(s_acc, K * (t - NB + 1))
                for k in range(K):
                    pool.indirect_dma_start(out=rows[t % NB][:, k, :], out_offset=None, in_=g.orows,
                                            in_offset=bass.IndirectOffsetOnAxis(ap=g.ridx[:, k, t:t + 1], axis=0),
                                            bounds_check=E * C - 1, oob_is_err=False).then_inc(s_g[t % NB], 16)

        @block.vector
        def _(dve):
            for t in range(NT):
                dve.wait_ge(s_g[t % NB], 16 * K * (t // NB + 1))
                for k in range(K):
                    if k:
                        dve.wait_ge(s_acc, K * t + k)
                    dve.scalar_tensor_tensor(g.x[:, t, :], rows[t % NB][:, k, :], g.wk[:, t, k:k + 1],
                                             g.x[:, t, :], ALU.mult, ALU.add).then_inc(s_acc, 1)

        @block.sync
        def _(sp):
            for t in range(NT):
                sp.wait_ge(s_acc, K * (t + 1))
                sp.dma_start(ov[:, t, :], g.x[:, t, :]).then_inc(s_st, 16)
            sp.wait_ge(s_st, 16 * NT)



def kernel(**inputs):
    import numpy as _np
    import concourse.bacc as _bacc
    from concourse import mybir as _mybir
    from concourse.bass_utils import run_bass_kernel_spmd as _run

    a = {k: _np.asarray(v) for k, v in inputs.items()}
    host = {
        "x": a["L0_attn_x"],
        "wqkv0": _np.concatenate([a["L0_attn_Wq"].T, a["L0_attn_Wk"].T, a["L0_attn_Wv"].T], axis=1),
        "wo0": a["L0_attn_Wo"].T,
        "ffn_w": a["L0_ffn_weight"].T,
        "gamma": a["L0_ffn_gamma"],
        "beta": a["L0_ffn_beta"],
        "ln_w": a["L0_ffn_ln_weight"].reshape(DC, P).T,
        "ln_b": a["L0_ffn_ln_bias"].reshape(DC, P).T,
        "wqkv1": _np.concatenate([a[f"L1_attn_W_{n}"] for n in "QKV"], axis=2).reshape(
            H, DC, P, 3 * DH1).transpose(0, 2, 1, 3),
        "wo1": a["L1_attn_W_O"].transpose(1, 0, 2),
        "b_Q": a["L1_attn_b_Q"].T, "b_K": a["L1_attn_b_K"].T, "b_V": a["L1_attn_b_V"].T,
        "b_O": a["L1_attn_b_O"],
        "gate": a["L1_ffn_gate_weight"].T,
        "wgu": _np.concatenate([a["L1_ffn_Wg"], a["L1_ffn_Wu"]], axis=1).transpose(0, 2, 1).reshape(
            E, DC, P, 2 * M).transpose(0, 2, 1, 3),
        "wd": a["L1_ffn_Wd"].transpose(0, 2, 1).reshape(E, 2, MH, D).transpose(0, 2, 1, 3),
        "sgu": _np.concatenate([a["L1_ffn_Sg"].T, a["L1_ffn_Su"].T], axis=1).reshape(
            DC, P, 2 * MS).transpose(1, 0, 2),
        "sd": a["L1_ffn_Sd"].T.reshape(NMS, MH, D).transpose(1, 0, 2),
    }
    host.update(constants())
    nc = _bacc.Bacc("TRN2", target_bir_lowering=False, num_devices=1)
    arrays, t_in = {}, {}
    for name, arr in host.items():
        arrays[f"in_{name}"] = _np.ascontiguousarray(arr)
        t_in[name] = nc.dram_tensor(f"in_{name}", arr.shape, _mybir.dt.from_np(arr.dtype), kind="ExternalInput").ap()
    out = nc.dram_tensor("out_0", (B, S, D), _mybir.dt.float32, kind="ExternalOutput").ap()
    build(nc, t_in, out)
    r = _run(nc, [arrays], core_ids=[0])
    return r.results[0]["out_0"]
```

```python
from contextlib import ExitStack

import numpy as np
import concourse.bass as bass
from concourse import mybir

F32 = mybir.dt.float32
F16 = mybir.dt.float16
BF16 = mybir.dt.bfloat16
U32 = mybir.dt.uint32
ALU = mybir.AluOpType
ACT = mybir.ActivationFunctionType
AX = mybir.AxisListType
ds = bass.ds

P = 128
B, S, D = 2, 1024, 256
T = B * S
NT = T // P
BT = S // P
DC = D // P
H = 16
DH0 = D // H
DH1 = 128
EPS = 1e-5
THETA = 10000.0
E, M, C = 64, 176, 96
MH = M // 2
K, NG, TG = 6, 8, 3
GS = E // NG
MS = 352
NMS = MS // MH
NEG = -1e30
ZD = 6
STOP = None


def constants():
    inv = THETA ** (-np.arange(0, DH0, 2, dtype=np.float32) / DH0)
    ang = np.arange(S, dtype=np.float32)[:, None] * inv[None, :].astype(np.float32)
    cos = np.repeat(np.cos(ang), 2, axis=1).astype(np.float32)
    sin = np.repeat(np.sin(ang), 2, axis=1).astype(np.float32)
    sin[:, 0::2] *= -1
    rope = np.stack([cos, sin], 1).reshape(BT, P, 2, DH0).transpose(1, 0, 2, 3)
    ident = np.eye(P, dtype=np.float32)
    mask = np.where(np.arange(P)[:, None] >= np.arange(P)[None, :], 0.0, NEG).astype(np.float32)
    before = (np.arange(P)[:, None] < np.arange(P)[None, :]).astype(np.float32)
    iota = np.broadcast_to(np.arange(E, dtype=np.float32), (P, E))
    return {"c_rope": np.ascontiguousarray(rope), "c_ident": ident, "c_mask": mask,
            "c_before": before, "c_iota": np.ascontiguousarray(iota)}


class Prog:
    pass


def build(nc, t_in, out):
    g = Prog()
    with ExitStack() as ctx:
        def sb(name, shape, dt=F32, c=ctx):
            return c.enter_context(nc.sbuf_tensor(name, shape, dt))

        made = {}

        def sem(name):
            if name not in made:
                made[name] = ctx.enter_context(nc.semaphore(name))
            return made[name]

        g.sb, g.sem, g.t = sb, sem, t_in
        g.bank = [ctx.enter_context(nc.psum_tensor(f"bank{i}", [P, 2, 512], F32)) for i in range(4)]
        g.x = sb("x", [P, NT, D])
        g.xT = sb("xT", [P, DC, T])
        g.identf = sb("identf", [P, P])
        g.identh = sb("identh", [P, P], F16)
        g.identb = sb("identb", [P, P], BF16)
        g.maskb = sb("maskb", [P, P], BF16)
        g.rstd = sb("rstd", [P, NT])
        g.zero = sb("zero", [P, E * C * D // P // ZD])
        g.xrows = nc.dram_tensor("slot_rows", (E * C, D), F32, kind="Internal").ap()
        g.orows = nc.dram_tensor("expert_rows", (E * C, D), F32, kind="Internal").ap()
        g.s_zero, g.s_memset = sem("zeros_landed"), sem("zeros_ready")
        g.mean = sb("mean", [P, NT])

        load(nc, g)
        norm(nc, g, "n0", None)
        with ExitStack() as c0:
            l0_qkv(nc, g, c0)
            l0_attention(nc, g)
            proj_out(nc, g, "o0", 0)
        if STOP == "att0":
            return finish(nc, g, out)
        with ExitStack() as c1:
            ffn_weights(nc, g, c1)
            norm(nc, g, "n1", "ffn")
            l0_ffn(nc, g)
        if STOP == "ffn0":
            return finish(nc, g, out)
        norm(nc, g, "n2", None)
        with ExitStack() as c2:
            l1_buffers(nc, g, c2)
            for b in range(B):
                l1_attention(nc, g, b)
                proj_out(nc, g, "o1", 1, b)
        if STOP == "att1":
            return finish(nc, g, out)
        moe(nc, g, out)


def finish(nc, g, out):
    s_out = g.sem("dbg_out")
    with nc.Block() as block:
        @block.sync
        def _(sp):
            sp.dma_start(out.rearrange("b (n p) d -> p (b n) d", p=P), g.x[:, :, :]).then_inc(s_out, 16)
            sp.wait_ge(s_out, 16)


def load(nc, g):
    s_x, s_c, s_v = g.sem("ld_x"), g.sem("ld_const"), g.sem("ld_cast")
    with ExitStack() as c:
        maskf = g.sb("maskf", [P, P], F32, c)
        with nc.Block() as block:
            @block.sync
            def _(sp):
                sp.dma_start(g.identf[:, :], g.t["c_ident"]).then_inc(s_c, 16)
                sp.dma_start(maskf[:, :], g.t["c_mask"]).then_inc(s_c, 16)
                sp.dma_start(g.x[:, :, :], g.t["x"].rearrange("b (n p) d -> p (b n) d", p=P)).then_inc(s_x, 16)

                sp.wait_ge(g.s_memset, 1)
                zv = g.xrows.rearrange("(z p n) d -> z p (n d)", p=P, z=ZD)
                for z in range(ZD):
                    sp.dma_start(zv[z], g.zero[:, :]).then_inc(g.s_zero, 16)

            @block.gpsimd
            def _(pool):
                pool.memset(g.zero[:, :], 0.0).then_inc(g.s_memset, 1)

            @block.vector
            def _(dve):
                dve.wait_ge(s_c, 32)
                dve.tensor_copy(g.identh[:, :], g.identf[:, :]).then_inc(s_v, 1)
                dve.tensor_copy(g.identb[:, :], g.identf[:, :]).then_inc(s_v, 1)
                dve.tensor_copy(g.maskb[:, :], maskf[:, :]).then_inc(s_v, 1)
                dve.wait_ge(s_x, 16)
                dve.wait_ge(s_v, 3)


def norm(nc, g, tag, kind):
    s_st, s_ag, s_sq, s_ch = [g.sem(f"{tag}_{n}") for n in ("stats", "aggr", "sqrt", "chain")]
    s_xn, s_tr = g.sem(f"{tag}_xn"), g.sem(f"{tag}_tr")
    s_ev = [g.sem(f"{tag}_evac{i}") for i in range(2)]
    with ExitStack() as c:
        st = g.sb(f"{tag}_st", [P, NT, 6], F32, c)
        mv = g.sb(f"{tag}_mv", [P, NT, 2], F32, c)
        sq = g.sb(f"{tag}_sq", [P, NT], F32, c)
        tmp = g.sb(f"{tag}_tmp", [P, 2, NT], F32, c)
        xn = g.xn if kind == "keep" else g.sb(f"{tag}_xnb", [P, NT, D], F32, c)
        ve = tmp[:, 0, :]
        t1 = tmp[:, 1, :]
        levels = 2 if kind == "ffn" else 1
        with nc.Block() as block:
            def evac(eng, p):
                eng.wait_ge(s_tr, p + 1)
                for c_ in range(DC):
                    src = g.bank[p % 2][:, 0, c_ * 256:(c_ + 1) * 256]
                    dst = g.xT[:, c_, p * 256:(p + 1) * 256]
                    if p % 2:
                        if kind == "ffn":
                            ins = eng.tensor_scalar(dst, src, g.lnw[:, c_:c_ + 1], g.lnb[:, c_:c_ + 1],
                                                    ALU.mult, ALU.add)
                        else:
                            ins = eng.tensor_copy(dst, src)
                    elif kind == "ffn":
                        ins = eng.activation(dst, src, ACT.Identity, bias=g.lnb[:, c_:c_ + 1],
                                             scale=g.lnw[:, c_:c_ + 1])
                    else:
                        ins = eng.activation(dst, src, ACT.Copy)
                ins.then_inc(s_ev[p % 2], 1)

            @block.vector
            def _(dve):
                n = 0

                def chained(ins):
                    nonlocal n
                    n += 1
                    ins.then_inc(s_ch, 1)
                    dve.wait_ge(s_ch, n)

                for t in range(NT):
                    dve.bn_stats(st[:, t, :], g.x[:, t, :]).then_inc(s_st, 1)
                for t in range(NT):
                    dve.wait_ge(s_st, t + 1)
                    dve.bn_aggr(mv[:, t, :], st[:, t, :]).then_inc(s_ag, 1)
                dve.wait_ge(s_ag, NT)
                chained(dve.tensor_copy(g.mean[:, :], mv[:, :, 0]))
                chained(dve.tensor_copy(t1, mv[:, :, 1]))
                for lv in range(levels):
                    chained(dve.tensor_scalar(ve, t1, EPS, None, ALU.add))
                    dve.wait_ge(s_sq, lv + 1)
                    chained(dve.reciprocal(sq[:, :], sq[:, :]))
                    r = g.rstd[:, :]
                    one = sq[:, :]
                    chained(dve.tensor_tensor(t1, one, one, ALU.mult))
                    chained(dve.tensor_tensor(t1, t1, ve, ALU.mult))
                    chained(dve.tensor_scalar(t1, t1, -0.5, 1.5, ALU.mult, ALU.add))
                    if lv == 0:
                        chained(dve.tensor_tensor(r, one, t1, ALU.mult))
                    else:
                        chained(dve.tensor_tensor(one, one, t1, ALU.mult))
                        chained(dve.tensor_tensor(r, r, one, ALU.mult))
                    if lv + 1 < levels:
                        chained(dve.tensor_tensor(t1, r, r, ALU.mult))
                        chained(dve.tensor_tensor(t1, t1, mv[:, :, 1], ALU.mult))
                for t in range(NT):
                    dve.tensor_scalar(xn[:, t, :], g.x[:, t, :], g.mean[:, t:t + 1], g.rstd[:, t:t + 1],
                                      ALU.subtract, ALU.mult).then_inc(s_xn, 1)
                for p in range(1, NT // 2, 2):
                    evac(dve, p)

            @block.scalar
            def _(act):
                for lv in range(levels):
                    act.wait_ge(s_ch, 3 if lv == 0 else 11)
                    act.activation(sq[:, :], ve, ACT.Sqrt).then_inc(s_sq, 1)
                for p in range(0, NT // 2, 2):
                    evac(act, p)

            @block.tensor
            def _(pe):
                for p in range(NT // 2):
                    pe.wait_ge(s_xn, 2 * p + 2)
                    if p >= 2:
                        pe.wait_ge(s_ev[p % 2], p // 2)
                    for c_ in range(DC):
                        for j in range(2):
                            ins = pe.transpose(g.bank[p % 2][:, 0, (2 * c_ + j) * P:(2 * c_ + j + 1) * P],
                                               xn[:, 2 * p + j, c_ * P:(c_ + 1) * P], g.identf[:, :])
                    ins.then_inc(s_tr, 1)


def l0_qkv(nc, g, c0):
    g.qk = g.sb("qk_parts", [P, B * H + 2, BT, 2, 2 * DH0], F16, c0)
    g.v0 = g.sb("v0", [P, B * H, BT, DH0], F32, c0)
    g.zl = g.sb("z_by_head", [P, B * H + 1, BT * DH0], F32, c0)
    g.wo0 = g.sb("wo0", [P, DC, D], F32, c0)
    s_w, s_mm = g.sem("q0_w"), g.sem("q0_mm")
    s_wo, s_sw = g.sem("q0_wo"), g.sem("q0_scaled")
    s_rot, s_v, s_add, s_hi, s_lo = [g.sem(f"q0_{n}") for n in ("rot", "v", "add", "hi", "lo")]
    with ExitStack() as c:
        w = g.sb("wqkv0", [P, DC, 3 * D], F32, c)
        rope = g.sb("rope", [P, BT, 2, DH0], F32, c)
        rot = [g.sb(f"rot{i}", [P, 2, 2 * D], F32, c) for i in range(2)]
        with nc.Block() as block:
            @block.sync
            def _(sp):
                sp.dma_start(w[:, :, :], g.t["wqkv0"].rearrange("(c p) n -> p c n", p=P)).then_inc(s_w, 16)
                sp.dma_start(rope[:, :, :, :], g.t["c_rope"]).then_inc(s_w, 16)
                sp.dma_start(g.wo0[:, :, :], g.t["wo0"].rearrange("(c p) n -> p c n", p=P)).then_inc(s_wo, 16)
                sp.wait_ge(s_wo, 16)

            @block.tensor
            def _(pe):
                pe.wait_ge(s_w, 32)
                pe.wait_ge(s_sw, 1)
                for t in range(NT):
                    if t >= 2:
                        pe.wait_ge(s_rot, t - 1)
                        pe.wait_ge(s_v, t - 1)
                    for half in range(2):
                        cols = slice(0, 512) if half == 0 else slice(512, 768)
                        for c_ in range(DC):
                            ins = pe.matmul(g.bank[2 * half + t % 2][:, 0, 0:cols.stop - cols.start],
                                            g.xT[:, c_, t * P:(t + 1) * P], w[:, c_, cols],
                                            start=(c_ == 0), stop=(c_ == DC - 1))
                    ins.then_inc(s_mm, 1)

            @block.vector
            def _(dve):
                dve.wait_ge(s_w, 32)
                dve.tensor_scalar(w[:, :, D:2 * D], w[:, :, D:2 * D], float(DH0) ** -0.5, None,
                                  ALU.mult).then_inc(s_sw, 1)

                def low(t):
                    dve.wait_ge(s_add, t + 1)
                    dve.wait_ge(s_hi, t + 1)
                    r = rot[t % 2][:, 0, :].rearrange("p (q h d) -> p q h d", q=2, h=H)
                    hs = slice(t // BT * H, (t // BT + 1) * H)
                    for q in range(2):
                        part = g.qk[:, hs, t % BT, q, :]
                        ins = dve.tensor_tensor(part[:, :, DH0:2 * DH0], r[:, q], part[:, :, 0:DH0], ALU.subtract)
                    ins.then_inc(s_lo, 1)

                for t in range(NT):
                    dve.wait_ge(s_mm, t + 1)
                    ps = g.bank[t % 2][:, 0, :]
                    r = rot[t % 2]
                    if t >= 2:
                        dve.wait_ge(s_lo, t - 1)
                    cs = rope[:, t % BT, 0, :].unsqueeze(1).to_broadcast([P, 2 * H, DH0])
                    dve.tensor_tensor(r[:, 0, :].rearrange("p (h d) -> p h d", d=DH0),
                                      ps.rearrange("p (h d) -> p h d", d=DH0), cs, ALU.mult)
                    for e in range(2):
                        sn = rope[:, t % BT, 1, e::2].unsqueeze(1).to_broadcast([P, 2 * H, DH0 // 2])
                        ins = dve.tensor_tensor(
                            r[:, 1, :].rearrange("p (h i two) -> p h i two", i=DH0 // 2, two=2)[:, :, :, e],
                            ps.rearrange("p (h i two) -> p h i two", i=DH0 // 2, two=2)[:, :, :, 1 - e],
                            sn, ALU.mult)
                    ins.then_inc(s_rot, 1)
                    if t >= 1:
                        low(t - 1)
                low(NT - 1)

            @block.gpsimd
            def _(pool):
                pool.memset(g.qk[:, B * H:B * H + 2, :, :, :], 0.0)
                for t in range(NT):
                    pool.wait_ge(s_rot, t + 1)
                    r = rot[t % 2]
                    pool.tensor_tensor(r[:, 0, :], r[:, 0, :], r[:, 1, :], ALU.add).then_inc(s_add, 1)

            @block.scalar
            def _(act):
                for t in range(NT):
                    act.wait_ge(s_mm, t + 1)
                    hs = slice(t // BT * H, (t // BT + 1) * H)
                    act.activation(g.v0[:, hs, t % BT, :], g.bank[2 + t % 2][:, 0, 0:D].rearrange(
                        "p (h d) -> p h d", d=DH0), ACT.Copy).then_inc(s_v, 1)
                    act.wait_ge(s_add, t + 1)
                    r = rot[t % 2][:, 0, :].rearrange("p (q h d) -> p q h d", q=2, h=H)
                    for q in range(2):
                        ins = act.activation(g.qk[:, hs, t % BT, q, 0:DH0], r[:, q], ACT.Copy)
                    ins.then_inc(s_hi, 1)


def l0_attention(nc, g):
    NH = B * H
    R = 96
    CH = 4
    QW = S // CH
    VW = 32
    PRO_MISC, PRO_DVE, PRO_ACT = 10, 4, 6
    names = ("st_ready", "e_ready", "s1_ready", "m_ready", "misc_ready", "misc_dve", "misc_act",
             "pv_ready", "zt_out", "inv", "preset")
    st_ready, e_ready, s1_ready, m_ready, misc_ready, misc_dve, misc_act, pv_ready, zt_out, s_inv, s_pre = \
        [g.sem(f"a0_{n}") for n in names]
    w_in = [g.sem(f"a0_w{i}") for i in range(2)]
    v_in = g.sem("a0_v_in")
    P0, ZT, MA, MB = 0, 4, 5, 6
    with ExitStack() as c:
        qT = [g.sb(f"a0_q{i}", [R, S], F16, c) for i in range(4)]
        kT = [g.sb(f"a0_k{i}", [R, S], F16, c) for i in range(4)]
        qh = [g.sb(f"a0_qh{i}", [P, BT, 2, R], F16, c) for i in range(2)]
        vh = [g.sb(f"a0_vh{i}", [P, BT, VW], F32, c) for i in range(4)]
        pT = [g.sb(f"a0_p{i}", [P, S], F32, c) for i in range(2)]
        negm = [g.sb(f"a0_negm{i}", [P, BT], F16, c) for i in range(2)]
        zts = [g.sb(f"a0_zt{i}", [P, QW], F32, c) for i in range(2)]
        rinv = g.sb("a0_rinv", [P, 2, CH], F32, c)
        ST = [g.bank[i].rearrange("p a n -> p (a n)") for i in range(2)]
        S1 = g.bank[2]
        zT = g.bank[3][:, 0, 0:QW]
        misc = g.bank[3][:, 1, :]

        def s1_place(t):
            i = BT - 1 - t
            return S1.rearrange("p a n -> p (a n)")[:, 0:(i + 1) * P] if i >= 4 else S1[:, t % 2, 0:(i + 1) * P]

        s1_steps = [[0], [1], [2], [3], [4, 5], [6, 7], [], []]

        def bodies(eng, body):
            with eng.Fori(0, NH // 4) as i:
                for s in range(4):
                    body(i * 4 + s, s)

        with nc.Block() as block:
            @block.gpsimd
            def _(pool):
                for i in range(2):
                    pool.memset(qh[i][:, :, :, 4 * DH0:R], 0.0).then_inc(s_pre, 1)
                pool.wait_ge(s_pre, 2)
                for i in range(2):
                    pool.memset(qh[i][:, :, 1, 4 * DH0:4 * DH0 + 1], 1.0).then_inc(s_pre, 1)
                for i in range(4):
                    pool.memset(vh[i][:, :, DH0 + 1:VW], 0.0).then_inc(s_pre, 1)
                    pool.memset(vh[i][:, :, DH0:DH0 + 1], 1.0).then_inc(s_pre, 1)
                pool.memset(zts[1][:, :], 1.0).then_inc(zt_out, 1)
                pool.wait_ge(s_pre, 12)

                def fetch(m, s, v):
                    for a in range(2):
                        src = g.qk[:, ds(m, 1), :, 0, :].rearrange("p o t d -> p (o t) d")
                        pool.tensor_copy(qh[s % 2][:, :, 0, a * 2 * DH0:(a + 1) * 2 * DH0], src
                                         ).then_inc(w_in[s % 2], 1)
                        src = g.qk[:, ds(m, 1), :, 1, a * DH0:(a + 1) * DH0].rearrange("p o t d -> p (o t) d")
                        dst = qh[s % 2][:, :, 1, a * 2 * DH0:(a + 1) * 2 * DH0].rearrange("p t (r d) -> p t r d", r=2)
                        pool.tensor_copy(dst, src.unsqueeze(2).to_broadcast([P, BT, 2, DH0])).then_inc(w_in[s % 2], 1)
                    if v:
                        src = g.v0[:, ds(m, 1), :, :].rearrange("p o t d -> p (o t) d")
                        pool.tensor_copy(vh[s][:, :, 0:DH0], src).then_inc(v_in, 1)

                for m in range(4):
                    if m >= 2:
                        pool.wait_ge(misc_ready, 4 * (m - 1))
                    fetch(m, m, True)
                with pool.Fori(1, NH // 4) as i:
                    for s in range(4):
                        pool.wait_ge(st_ready, (i * 4 + s) * BT - (3 * BT - 1))
                        fetch(i * 4 + s, s, True)
                for m in range(NH, NH + 2):
                    pool.wait_ge(st_ready, (m - 3) * BT + 1)
                    fetch(m, m % 4, False)

            def turn_chunk(pe, k, s):
                for j in range(4):
                    ins = pe.matmul(misc[0:R, j * P:(j + 1) * P], qh[s % 2][:, (k % 2) * 4 + j, k // 2, :],
                                    g.identh[:, :], start=True, stop=True)
                ins.then_inc(misc_ready, 1)

            def max_scores(pe, t, s):
                i = BT - 1 - t
                ps = s1_place(t)
                for c4 in range(-(-(i + 1) // 4)):
                    w_ = min(4, i + 1 - 4 * c4) * P
                    diag = c4 == i // 4
                    pe.matmul(ps[:, c4 * 512:c4 * 512 + w_], qT[s][:, i * P:(i + 1) * P],
                              kT[s][:, c4 * 512:c4 * 512 + w_], start=True, stop=not diag)
                    if diag:
                        ins = pe.matmul(ps[:, i * P:(i + 1) * P], g.identb[:, :], g.maskb[:, :],
                                        start=False, stop=True)
                ins.then_inc(s1_ready, 1)

            def max_rows(pe, half, s):
                for j in range(4):
                    i = (1 - half) * 4 + j
                    t = BT - 1 - i
                    ins = pe.matmul(misc[64:65, j * P:(j + 1) * P], negm[s % 2][:, t:t + 1], g.identh[:, :],
                                    start=True, stop=True)
                ins.then_inc(misc_ready, 1)

            @block.tensor
            def _(pe):
                pe.nop().then_inc(pv_ready, BT)
                for m in range(2):
                    for k in range(4):
                        if k == 0:
                            pe.wait_ge(w_in[m], 4)
                        if k in (1, 2):
                            pe.wait_ge(misc_dve, 2 * m + k)
                        elif k == 3 or m:
                            pe.wait_ge(misc_act, 2 * m + (1 if k == 3 else 0))
                        turn_chunk(pe, k, m)
                pe.wait_ge(misc_act, 4)
                pe.wait_ge(misc_dve, 4)
                for t in range(BT):
                    if t:
                        pe.wait_ge(m_ready, t if t < 5 else t - 1)
                    max_scores(pe, t, 0)
                for half in range(2):
                    pe.wait_ge(m_ready, 4 + 4 * half)
                    if half:
                        pe.wait_ge(misc_act, 5)
                    max_rows(pe, half, 0)

                def body(n, s):
                    def values(k):
                        pe.wait_ge(e_ready, n * BT + (BT + k + 1))
                        if k == 0:
                            pe.wait_ge(v_in, n + 1)
                            pe.wait_ge(zt_out, n + 1)
                        for q in range(k // 2, CH):
                            lo = max(k * P, q * QW)
                            hi = (q + 1) * QW
                            ins = pe.matmul(zT[VW * q:VW * (q + 1), lo - q * QW:hi - q * QW], vh[s][:, k, :],
                                            pT[k % 2][:, lo - k * P:hi - k * P], start=(k == 0),
                                            stop=(k == min(2 * q + 1, BT - 1)), skip_group_check=True)
                        ins.then_inc(pv_ready, 1)

                    for k in range(BT):
                        if k == 0:
                            pe.wait_ge(misc_act, n * 4 + PRO_ACT)
                        pe.wait_ge(e_ready, n * BT + (BT + k - 1))
                        width = (BT - k) * P
                        for c4 in range(-(-width // 512)):
                            w_ = min(512, width - c4 * 512)
                            ins = pe.matmul(ST[k % 2][:, c4 * 512:c4 * 512 + w_], kT[s][:, k * P:(k + 1) * P],
                                            qT[s][:, k * P + c4 * 512:k * P + c4 * 512 + w_],
                                            start=True, stop=c4 > 0)
                            if c4 == 0:
                                ins = pe.matmul(ST[k % 2][:, 0:P], g.maskb[:, :], g.identb[:, :],
                                                start=False, stop=True)
                        ins.then_inc(st_ready, 1)
                        for t in s1_steps[k]:
                            if t == 0:
                                pe.wait_ge(misc_dve, n * 3 + (PRO_DVE - 1))
                                pe.wait_ge(m_ready, n * BT + BT)
                            else:
                                pe.wait_ge(m_ready, n * BT + (BT + (t if t < 5 else t - 1)))
                            max_scores(pe, t, (s + 1) % 4)
                        if k < 4:
                            if k == 0:
                                pe.wait_ge(w_in[s % 2], n * 2 + (8 - 2 * (s % 2)))
                            elif k < 3:
                                pe.wait_ge(misc_dve, n * 3 + (PRO_DVE + k))
                            else:
                                pe.wait_ge(misc_act, n * 4 + (PRO_ACT + 1))
                            turn_chunk(pe, k, s)
                        if k == 4:
                            pe.wait_ge(misc_act, n * 4 + (PRO_ACT + 2))
                            pe.wait_ge(zt_out, n + 1)
                            for half in range(2):
                                ins = pe.transpose(misc[:, half * P:(half + 1) * P],
                                                   zts[(s + 1) % 2][:, half * P:(half + 1) * P], g.identf[:, :])
                            ins.then_inc(misc_ready, 1)
                        if k == 5:
                            pe.wait_ge(misc_dve, n * 3 + (PRO_DVE + 3))
                            pe.wait_ge(m_ready, n * BT + (BT + 4))
                            max_rows(pe, 0, s + 1)
                        if k >= 1:
                            values(k - 1)
                        if k == 7:
                            pe.wait_ge(misc_act, n * 4 + (PRO_ACT + 3))
                            pe.wait_ge(m_ready, n * BT + (BT + 8))
                            max_rows(pe, 1, s + 1)
                    values(BT - 1)
                bodies(pe, body)
                pe.wait_ge(zt_out, NH + 1)
                pe.wait_ge(misc_act, PRO_ACT + 4 * NH)
                for half in range(2):
                    ins = pe.transpose(misc[:, half * P:(half + 1) * P],
                                       zts[1][:, half * P:(half + 1) * P], g.identf[:, :])
                ins.then_inc(misc_ready, 1)

            def chunk_out(eng, k, s, is_act):
                dst = (qT if k < 2 else kT)[s][:, (k % 2) * 512:(k % 2 + 1) * 512]
                if is_act:
                    return eng.activation(dst, misc[0:R, :], ACT.Copy)
                return eng.tensor_copy(dst, misc[0:R, :])

            def rows_out(act, half, s):
                cols = slice(512, 1024) if half == 0 else slice(0, 512)
                return act.activation(qT[s][64:65, cols], misc[64:65, :], ACT.Copy)

            @block.scalar
            def _(act):
                act.nop().then_inc(e_ready, BT)
                for m in range(2):
                    for k in (2, 3):
                        act.wait_ge(misc_ready, 4 * m + k + 1)
                        chunk_out(act, k, m, True).then_inc(misc_act, 1)
                for half in range(2):
                    act.wait_ge(misc_ready, 9 + half)
                    rows_out(act, half, 0).then_inc(misc_act, 1)

                def body(n, s):
                    for k in range(BT):
                        act.wait_ge(st_ready, n * BT + (k + 1))
                        act.wait_ge(pv_ready, n * BT + (BT + k - 1))
                        width = (BT - k) * P
                        act.activation(pT[k % 2][:, 0:width], ST[k % 2][:, 0:width], ACT.Exp).then_inc(e_ready, 1)
                        if k in (2, 3):
                            act.wait_ge(misc_ready, n * 7 + (PRO_MISC + P0 + k + 1))
                            chunk_out(act, k, (s + 2) % 4, True).then_inc(misc_act, 1)
                        if k in (5, 7):
                            act.wait_ge(misc_ready, n * 7 + (PRO_MISC + (MA if k == 5 else MB) + 1))
                            rows_out(act, 0 if k == 5 else 1, (s + 1) % 4).then_inc(misc_act, 1)
                bodies(act, body)

            @block.vector
            def _(dve):
                def maximum(t, s, count):
                    dve.wait_ge(s1_ready, count)
                    dve.tensor_reduce(negm[s % 2][:, t:t + 1], s1_place(t), AX.X, ALU.max,
                                      negate=True).then_inc(m_ready, 1)

                def z_out(n, count):
                    dve.wait_ge(misc_ready, count)
                    zv = misc[:, 0:2 * P].rearrange("p (a q v) -> p a q v", a=2, v=VW)
                    dve.reciprocal(rinv[:, :, :], zv[:, :, :, DH0]).then_inc(s_inv, 1)
                    dve.wait_ge(s_inv, n + 1)
                    dst = g.zl[:, ds(n, 1), :].rearrange("p o (q a d) -> p (o a) q d", q=CH, a=2)
                    dve.tensor_tensor(dst, zv[:, :, :, 0:DH0],
                                      rinv[:, :, :].unsqueeze(3).to_broadcast([P, 2, CH, DH0]),
                                      ALU.mult).then_inc(misc_dve, 1)

                for m in range(2):
                    for k in range(2):
                        dve.wait_ge(misc_ready, 4 * m + k + 1)
                        chunk_out(dve, k, m, False).then_inc(misc_dve, 1)
                for t in range(BT):
                    maximum(t, 0, t + 1)

                def body(n, s):
                    for k in range(BT):
                        for t in s1_steps[k]:
                            maximum(t, s + 1, n * BT + (BT + t + 1))
                        if k < 2:
                            dve.wait_ge(misc_ready, n * 7 + (PRO_MISC + P0 + k + 1))
                            chunk_out(dve, k, (s + 2) % 4, False).then_inc(misc_dve, 1)
                        if k == 4:
                            z_out(n, n * 7 + (PRO_MISC + ZT + 1))
                    dve.wait_ge(pv_ready, n * BT + 2 * BT)
                    dve.tensor_copy(zts[s % 2][:, :], zT).then_inc(zt_out, 1)
                bodies(dve, body)
                z_out(NH, PRO_MISC + 7 * NH + 1)


def l1_attention(nc, g, b):
    AHEAD = {0: 0, 1: 1, 4: 2, 5: 3, 6: 4, 7: 5}
    NCH = len(AHEAD)
    GU = BT + NCH
    blocks = [BT - j for j in range(BT)]
    chunks = [-(-n // 4) for n in blocks]
    first = [sum(chunks[:j]) for j in range(BT + 1)]
    TC = first[BT]
    s_ready, m_ready, e_ready, r_ready, t_ready, g_ready, hi_ready, w_split = \
        [g.sem(f"a1_{n}") for n in ("scores", "max", "exp", "inv", "turned", "g_ready", "hi_ready", "w_split")]
    g_free = [g.sem("a1_g_even_free"), g.sem("a1_g_odd_free")]
    t_dve, t_act = g.sem("a1_t_dve"), g.sem("a1_t_act")
    w_in = [g.sem(f"a1_w{i}") for i in range(2)]
    N0 = b * H
    WS = 4

    def body_items(is_first, is_last):
        items, use = [], 6 if is_first else 4
        for j in range(BT + (2 if is_last else 0)):
            if j < BT:
                items.append(("scores", j, False, None))
                if not is_last and j in AHEAD:
                    items.append(("ahead", AHEAD[j], False, use))
                    use += 1
            if j >= 1 or not is_first:
                if j <= BT:
                    items.append(("turn", (j - 1) % BT, j == 0, None))
            if j >= 2 or not is_first:
                items.append(("values", (j - 2) % BT, j < 2, use))
                use += 1
        return items

    first_items, mid_items, last_items = body_items(True, False), body_items(False, False), body_items(False, True)

    def back_use(items, j, before):
        if before:
            return [it[3] for it in mid_items if it[:3] == ("values", j - 2, False)][0] - GU
        return [it[3] for it in items if it[:3] == ("values", (j - 2) % BT, j < 2)][0]

    def all_heads(eng, head):
        head(eng, N0, 0, first_items)
        with eng.Fori(0, H // 2 - 1) as pair:
            head(eng, pair * 2 + (N0 + 1), 1, mid_items)
            head(eng, pair * 2 + (N0 + 2), 0, mid_items)
        head(eng, N0 + H - 1, 1, last_items)

    with ExitStack() as c:
        probs = [g.sb(f"a1{b}_p{i}", [P, S], F32, c) for i in range(2)]
        turned = [g.sb(f"a1{b}_pt{i}", [P, S], F32, c) for i in range(2)]
        qT = [[g.sb(f"a1{b}_q{i}{a}", [P, S], F16, c) for a in range(2)] for i in range(2)]
        kT = [[g.sb(f"a1{b}_k{i}{a}", [P, S], F16, c) for a in range(2)] for i in range(2)]
        negm = g.sb(f"a1{b}_negm", [P, 2, BT], F32, c)
        rsum = g.sb(f"a1{b}_rsum", [P, 2, BT], F32, c)
        rinv = g.sb(f"a1{b}_rinv", [P, 2, BT], F32, c)
        S_ps = [g.bank[0], g.bank[1]]
        T_ps = [g.bank[2][:, 0, :], g.bank[2][:, 1, :]]
        G_ps = [g.bank[3][:, 0, :], g.bank[3][:, 1, :]]
        PARTS = [(0, 0), (0, 1), (1, 0)]

        def prep_pe(pe, k, par, ps):
            w = g.wsplit[par]
            if k < 4:
                for c_ in range(DC):
                    for a, x_ in PARTS:
                        ins = pe.matmul(ps, w[a][:, c_, (k // 2) * P:(k // 2 + 1) * P],
                                        g.xs[x_][:, c_, b * S + (k % 2) * 512:b * S + (k % 2 + 1) * 512],
                                        start=(c_ == 0 and (a, x_) == PARTS[0]),
                                        stop=(c_ == DC - 1 and (a, x_) == PARTS[-1]))
            else:
                for j in range(4):
                    t = b * BT + (k - 4) * 4 + j
                    for c_ in range(DC):
                        for a, x_ in PARTS:
                            ins = pe.matmul(ps[:, j * P:(j + 1) * P], g.xs[x_][:, c_, t * P:(t + 1) * P],
                                            w[a][:, c_, 2 * P:3 * P],
                                            start=(c_ == 0 and (a, x_) == PARTS[0]),
                                            stop=(c_ == DC - 1 and (a, x_) == PARTS[-1]))
            return ins

        def prep_hi(act, k, par, ps, use):
            if k == 4:
                act.activation(g.vh[par][:, 0:4, :].rearrange("p t d -> p (t d)"), ps, ACT.Copy
                               ).then_inc(g_free[use % 2], 1)
            elif k < 4:
                dst = (qT if k < 2 else kT)[par][0][:, (k % 2) * 512:(k % 2 + 1) * 512]
                bias = g.bias[par][:, k // 2:k // 2 + 1]
                act.activation(dst, ps, ACT.Identity, bias=bias).then_inc(hi_ready, 1)

        def prep_lo(dve, k, par, ps, n, use):
            if k == 5:
                dve.tensor_copy(g.vh[par][:, 4:8, :].rearrange("p t d -> p (t d)"), ps
                                ).then_inc(g_free[use % 2], 1)
            elif k < 4:
                cols = slice((k % 2) * 512, (k % 2 + 1) * 512)
                parts = (qT if k < 2 else kT)[par]
                bias = g.bias[par][:, k // 2:k // 2 + 1]
                dve.wait_ge(hi_ready, n * 4 + (k + 1))
                dve.scalar_tensor_tensor(parts[1][:, cols], ps, bias, parts[0][:, cols], ALU.add, ALU.subtract
                                         ).then_inc(g_free[use % 2], 1)

        with nc.Block() as block:
            @block.sync
            def _(sp):
                def fetch(h, par):
                    if not isinstance(h, int) or N0 + h >= 2:
                        sp.wait_ge(w_split, h * WS + (N0 - 1) * WS)
                    sp.dma_start(g.wh[par][:, :, :], g.t["wqkv1"][ds(h, 1), :, :, :].rearrange(
                        "o p c n -> (o p) c n")).then_inc(w_in[par], 16)
                fetch(0, 0)
                fetch(1, 1)
                with sp.Fori(1, H // 2) as pair:
                    fetch(pair * 2, 0)
                    fetch(pair * 2 + 1, 1)

            @block.gpsimd
            def _(pool):
                zeros = g.zero[:, 0:DC * 3 * P].rearrange("p (c n) -> p c n", c=DC)

                def split(h, par):
                    if not isinstance(h, int) or N0 + h >= 2:
                        pool.wait_ge(s_ready, h * BT + ((N0 - 2) * BT + 1))
                    pool.wait_ge(w_in[par], h * 8 + (N0 * 8 + 16 - 8 * par))
                    w = g.wh[par]
                    pool.tensor_tensor(w[:, :, :], w[:, :, :], g.wscale[:, :, :], ALU.mult).then_inc(w_split, 1)
                    pool.wait_ge(w_split, h * WS + (N0 * WS + 1))
                    pool.tensor_tensor(g.wsplit[par][0][:, :, :], w[:, :, :], zeros, ALU.add).then_inc(w_split, 1)
                    pool.tensor_tensor(g.bias[par][:, :], g.bqk[:, ds(h, 1), :].rearrange("p o q -> p (o q)"),
                                       g.zero[:, 0:2], ALU.add).then_inc(w_split, 1)
                    pool.wait_ge(w_split, h * WS + (N0 * WS + 3))
                    pool.tensor_tensor(g.wsplit[par][1][:, :, :], w[:, :, :], g.wsplit[par][0][:, :, :],
                                       ALU.subtract).then_inc(w_split, 1)
                split(0, 0)
                split(1, 1)
                with pool.Fori(1, H // 2) as pair:
                    split(pair * 2, 0)
                    split(pair * 2 + 1, 1)

            @block.tensor
            def _(pe):
                pe.wait_ge(w_split, N0 * WS + WS)
                for k in range(NCH):
                    if k >= 2:
                        pe.wait_ge(g_free[k % 2], N0 * GU // 2 + k // 2)
                    prep_pe(pe, k, 0, G_ps[k % 2]).then_inc(g_ready, 1)
                pe.wait_ge(g_free[0], N0 * GU // 2 + NCH // 2)
                pe.wait_ge(g_free[1], N0 * GU // 2 + NCH // 2)

                def head(eng, n, par, items):
                    start = items is first_items and b == 0
                    for kind, j, before, u in items:
                        p_ = 1 - par if before else par
                        if kind == "scores":
                            nb, i = blocks[j], blocks[j] - 1
                            if j == 0 and items is not first_items:
                                eng.wait_ge(g_free[0], n * (GU // 2))
                            if not (start and j < 2):
                                eng.wait_ge(e_ready, n * BT + (j - 1))
                            ps = S_ps[j % 2]
                            for c4 in range(-(-nb // 4)):
                                w_ = min(4, nb - 4 * c4) * P
                                diag = c4 == i // 4
                                for a, k_ in PARTS:
                                    ins = eng.matmul(ps[:, c4, 0:w_], qT[par][a][:, i * P:(i + 1) * P],
                                                     kT[par][k_][:, c4 * 512:c4 * 512 + w_],
                                                     start=(a, k_) == PARTS[0],
                                                     stop=(a, k_) == PARTS[-1] and not diag)
                                if diag:
                                    o = (i % 4) * P
                                    ins = eng.matmul(ps[:, c4, o:o + P], g.identb[:, :], g.maskb[:, :],
                                                     start=False, stop=True)
                            ins.then_inc(s_ready, 1)
                        elif kind == "turn":
                            nn = n - 1 if before else n
                            eng.wait_ge(e_ready, nn * BT + (j + 1))
                            for k in range(chunks[j]):
                                ch = first[j] + k
                                if not (start and ch < 2):
                                    eng.wait_ge((t_dve, t_act)[ch % 2], nn * (TC // 2) + ch // 2)
                                for q in range(4 * k, min(4 * k + 4, blocks[j])):
                                    ins = eng.transpose(T_ps[ch % 2][:, (q % 4) * P:(q % 4 + 1) * P],
                                                        probs[j % 2][:, q * P:(q + 1) * P], g.identf[:, :])
                                ins.then_inc(t_ready, 1)
                        elif kind == "values":
                            nn = n - 1 if before else n
                            last = first[j + 1]
                            eng.wait_ge(t_dve, nn * (TC // 2) + (last + 1) // 2)
                            eng.wait_ge(t_act, nn * (TC // 2) + last // 2)
                            eng.wait_ge(g_free[u % 2], n * (GU // 2) + u // 2)
                            for q in range(blocks[j]):
                                ins = eng.matmul(G_ps[u % 2][:, 0:DH1], turned[j % 2][:, q * P:(q + 1) * P],
                                                 g.vh[p_][:, q, :], start=(q == 0), stop=(q == blocks[j] - 1))
                            ins.then_inc(g_ready, 1)
                        else:
                            if j == 0:
                                eng.wait_ge(w_split, n * WS + 2 * WS)
                            eng.wait_ge(g_free[u % 2], n * (GU // 2) + u // 2)
                            prep_pe(eng, j, 1 - par, G_ps[u % 2]).then_inc(g_ready, 1)
                all_heads(pe, head)

            def turned_copy(eng, is_act, n, j, before, items):
                nn = n - 1 if before else n
                for k in range(chunks[j]):
                    ch = first[j] + k
                    if (ch % 2 == 1) != is_act:
                        continue
                    eng.wait_ge(t_ready, nn * TC + (ch + 1))
                    if not (items is first_items and j < 2):
                        eng.wait_ge(g_ready, n * GU + back_use(items, j, before) + 1)
                    w_ = min(4, blocks[j] - 4 * k) * P
                    dst = turned[j % 2][:, k * 512:k * 512 + w_]
                    src = T_ps[ch % 2][:, 0:w_]
                    ins = eng.activation(dst, src, ACT.Copy) if is_act else eng.tensor_copy(dst, src)
                    ins.then_inc(t_act if is_act else t_dve, 1)

            @block.scalar
            def _(act):
                for k in range(5):
                    act.wait_ge(g_ready, N0 * GU + k + 1)
                    prep_hi(act, k, 0, G_ps[k % 2], k)

                def head(eng, n, par, items):
                    for kind, j, before, u in items:
                        if kind == "scores":
                            eng.wait_ge(m_ready, n * BT + (j + 1))
                            if j >= 2 or not (items is first_items and b == 0):
                                eng.wait_ge(t_ready, n * TC + (first[j - 1] if j >= 2 else j - 1))
                            w_ = blocks[j] * P
                            eng.activation(probs[j % 2][:, 0:w_],
                                           S_ps[j % 2].rearrange("p a n -> p (a n)")[:, 0:w_], ACT.Exp,
                                           bias=negm[:, par, j:j + 1],
                                           accum_out=rsum[:, par, j:j + 1]).then_inc(e_ready, 1)
                        elif kind == "turn":
                            turned_copy(eng, True, n, j, before, items)
                        elif kind == "values":
                            nn = n - 1 if before else n
                            eng.wait_ge(g_ready, n * GU + (u + 1))
                            eng.wait_ge(r_ready, nn * BT + (j + 1))
                            p_ = 1 - par if before else par
                            eng.activation(g.z[:, blocks[j] - 1, ds(nn * DH1 - N0 * DH1, DH1)], G_ps[u % 2][:, 0:DH1],
                                           ACT.Copy, scale=rinv[:, p_, j:j + 1]).then_inc(g_free[u % 2], 1)
                        elif j < 5:
                            eng.wait_ge(g_ready, n * GU + (u + 1))
                            prep_hi(eng, j, 1 - par, G_ps[u % 2], u)
                all_heads(act, head)

            @block.vector
            def _(dve):
                for k in (0, 1, 2, 3, 5):
                    dve.wait_ge(g_ready, N0 * GU + k + 1)
                    prep_lo(dve, k, 0, G_ps[k % 2], N0, k)

                def head(eng, n, par, items):
                    for kind, j, before, u in items:
                        if kind == "scores":
                            eng.wait_ge(s_ready, n * BT + (j + 1))
                            w_ = blocks[j] * P
                            eng.tensor_reduce(negm[:, par, j:j + 1],
                                              S_ps[j % 2].rearrange("p a n -> p (a n)")[:, 0:w_],
                                              AX.X, ALU.max, negate=True).then_inc(m_ready, 1)
                        elif kind == "turn":
                            turned_copy(eng, False, n, j, before, items)
                        elif kind == "values":
                            nn = n - 1 if before else n
                            p_ = 1 - par if before else par
                            eng.wait_ge(e_ready, nn * BT + (j + 1))
                            eng.reciprocal(rinv[:, p_, j:j + 1], rsum[:, p_, j:j + 1]).then_inc(r_ready, 1)
                        elif j != 4:
                            eng.wait_ge(g_ready, n * GU + (u + 1))
                            prep_lo(eng, j, 1 - par, G_ps[u % 2], n + 1, u)
                all_heads(dve, head)


def proj_out(nc, g, tag, layer, b=0):
    NC = H if layer else DC
    GR = -(-NC // 4)
    tiles = list(range(BT)) if layer else list(range(NT))
    w = g.wo1 if layer else g.wo0
    s_t, s_c, s_mm, s_add, s_w = [g.sem(f"{tag}_{n}") for n in ("turn", "copy", "mm", "add", "w")]
    s_bo = g.sem(f"{tag}_bo")
    N0 = b * BT
    s_z = g.sem(f"{tag}_z")
    with ExitStack() as c:
        if not layer:
            g.z = g.sb("z0", [P, NT, D], F32, c)
        zT = [g.sb(f"{tag}{b}_zT{i}", [P, NC, P], F32, c) for i in range(2)]
        with nc.Block() as block:
            @block.tensor
            def _(pe):
                def out(n):
                    pe.wait_ge(s_c, (N0 + n + 1) * GR)
                    if n >= 2:
                        pe.wait_ge(s_add, N0 + n - 1)
                    for k in range(NC):
                        ins = pe.matmul(g.bank[2 + n % 2][:, 0, 0:D], zT[n % 2][:, k, :], w[:, k, :],
                                        start=(k == 0), stop=(k == NC - 1))
                    ins.then_inc(s_mm, 1)

                for n, t in enumerate(tiles):
                    if not layer:
                        pe.wait_ge(s_z, n + 1)
                    for r in range(GR):
                        m = n * GR + r
                        if m >= 2:
                            pe.wait_ge(s_c, N0 * GR + m - 1)
                        nk = min(4, NC - 4 * r)
                        for k in range(nk):
                            ins = pe.transpose(g.bank[m % 2][:, 0, k * P:(k + 1) * P],
                                               g.z[:, t, (4 * r + k) * P:(4 * r + k + 1) * P], g.identf[:, :])
                        ins.then_inc(s_t, 1)
                    if n:
                        out(n - 1)
                out(len(tiles) - 1)

            @block.vector
            def _(dve):
                def add(n):
                    t = b * BT + tiles[n] if layer else tiles[n]
                    dve.wait_ge(s_mm, N0 + n + 1)
                    if layer:
                        dve.wait_ge(s_bo, N0 + n + 1)
                    dve.tensor_tensor(g.x[:, t, :], g.bank[2 + n % 2][:, 0, 0:D], g.x[:, t, :],
                                      ALU.add).then_inc(s_add, 1)

                for n, t in enumerate(tiles):
                    for r in range(GR):
                        m = n * GR + r
                        nk = min(4, NC - 4 * r)
                        dve.wait_ge(s_t, N0 * GR + m + 1)
                        if n >= 2:
                            dve.wait_ge(s_mm, N0 + n - 1)
                        dst = zT[n % 2][:, 4 * r:4 * r + nk, :]
                        src = g.bank[m % 2][:, 0, 0:nk * P].rearrange("p (k q) -> p k q", k=nk)
                        if layer:
                            bv = g.bv[:, 4 * r:4 * r + nk].unsqueeze(2).to_broadcast([P, nk, P])
                            dve.tensor_tensor(dst, src, bv, ALU.add).then_inc(s_c, 1)
                        else:
                            dve.tensor_copy(dst, src).then_inc(s_c, 1)
                    if n:
                        add(n - 1)
                add(len(tiles) - 1)

            if not layer:
                @block.scalar
                def _(act):
                    for t in tiles:
                        b0 = t // BT
                        src = g.zl[:, 1 + b0 * H:1 + (b0 + 1) * H, (t % BT) * DH0:(t % BT + 1) * DH0]
                        act.activation(g.z[:, t, :].rearrange("p (h d) -> p h d", d=DH0), src,
                                       ACT.Copy).then_inc(s_z, 1)

            if layer:
                @block.gpsimd
                def _(pool):
                    for n, t in enumerate(tiles):
                        pool.tensor_tensor(g.x[:, b * BT + t, :], g.x[:, b * BT + t, :], g.bo[:, :],
                                           ALU.add).then_inc(s_bo, 1)


def ffn_weights(nc, g, c1):
    g.wf = g.sb("wf", [P, DC, D], F32, c1)
    g.lnw = g.sb("lnw", [P, DC], F32, c1)
    g.lnb = g.sb("lnb", [P, DC], F32, c1)
    g.beta = g.sb("beta", [P, D], F32, c1)
    s_in, s_ch, s_ab, s_all = [g.sem(f"fw_{n}") for n in ("in", "chain", "absmax", "all")]
    s_sg = g.sem("fw_sign")
    with ExitStack() as c:
        w = g.sb("fw_w", [P, DC, D], F32, c)
        gam = g.sb("fw_gamma", [P, D], F32, c)
        am = g.sb("fw_am", [P, 2], F32, c)
        with nc.Block() as block:
            @block.sync
            def _(sp):
                sp.dma_start(w[:, :, :], g.t["ffn_w"].rearrange("(c p) n -> p c n", p=P)).then_inc(s_in, 16)
                sp.dma_start(gam[:, :], g.t["gamma"].partition_broadcast(P)).then_inc(s_in, 16)
                sp.dma_start(g.beta[:, :], g.t["beta"].partition_broadcast(P)).then_inc(s_in, 16)
                sp.dma_start(g.lnw[:, :], g.t["ln_w"]).then_inc(s_in, 16)
                sp.dma_start(g.lnb[:, :], g.t["ln_b"]).then_inc(s_in, 16)

            @block.vector
            def _(dve):
                dve.wait_ge(s_in, 80)
                dve.tensor_reduce(am[:, 0:1], w[:, :, :], AX.XY, ALU.max,
                                  apply_absolute_value=True).then_inc(s_ab, 1)
                dve.wait_ge(s_all, 1)
                dve.tensor_scalar(gam[:, :], gam[:, :], am[:, 1:2], None, ALU.mult).then_inc(s_ch, 1)
                dve.wait_ge(s_ch, 1)
                dve.wait_ge(s_sg, 1)
                dve.tensor_tensor(g.wf[:, :, :], g.wf[:, :, :],
                                  gam[:, :].unsqueeze(1).to_broadcast([P, DC, D]), ALU.mult).then_inc(s_ch, 1)
                dve.wait_ge(s_ch, 2)

            @block.gpsimd
            def _(pool):
                pool.wait_ge(s_ab, 1)
                pool.partition_all_reduce(am[:, 1:2], am[:, 0:1], P, bass.bass_isa.ReduceOp.max).then_inc(s_all, 1)

            @block.scalar
            def _(act):
                act.wait_ge(s_in, 80)
                act.activation(g.wf[:, :, :], w[:, :, :], ACT.Sign).then_inc(s_sg, 1)


def l0_ffn(nc, g):
    s_mm, s_bt, s_add = [g.sem(f"f0_{n}") for n in ("mm", "beta", "add")]
    with nc.Block() as block:
        @block.tensor
        def _(pe):
            for t in range(NT):
                if t >= 4:
                    pe.wait_ge(s_add, t - 3)
                for c_ in range(DC):
                    ins = pe.matmul(g.bank[t % 4][:, 0, 0:D], g.xT[:, c_, t * P:(t + 1) * P], g.wf[:, c_, :],
                                    start=(c_ == 0), stop=(c_ == DC - 1))
                ins.then_inc(s_mm, 1)

        @block.gpsimd
        def _(pool):
            for t in range(NT):
                pool.tensor_tensor(g.x[:, t, :], g.x[:, t, :], g.beta[:, :], ALU.add).then_inc(s_bt, 1)

        @block.vector
        def _(dve):
            for t in range(NT):
                dve.wait_ge(s_mm, t + 1)
                dve.wait_ge(s_bt, t + 1)
                dve.tensor_tensor(g.x[:, t, :], g.bank[t % 4][:, 0, 0:D], g.x[:, t, :], ALU.add).then_inc(s_add, 1)


def l1_buffers(nc, g, c2):
    g.wh = [g.sb(f"wh{i}", [P, DC, 3 * P], F32, c2) for i in range(2)]
    g.wsplit = [[g.sb(f"wsplit{i}{a}", [P, DC, 3 * P], F16, c2) for a in range(2)] for i in range(2)]
    g.xs = [g.sb(f"x_part{a}", [P, DC, T], F16, c2) for a in range(2)]
    g.vh = [g.sb(f"vh{i}", [P, BT, P], F32, c2) for i in range(2)]
    g.z = g.sb("z1", [P, BT, H * DH1], F32, c2)
    g.wo1 = g.sb("wo1", [P, H, D], F32, c2)
    g.bqk = g.sb("bqk1", [P, H, 2], F32, c2)
    g.bv = g.sb("bv1", [P, H], F32, c2)
    g.bias = [g.sb(f"bias{i}", [P, 2], F32, c2) for i in range(2)]
    g.wscale = g.sb("wscale", [P, DC, 3 * P], F32, c2)
    g.bo = g.sb("bo1", [P, D], F32, c2)
    s_in, s_b = g.sem("l1_in"), g.sem("l1_bias")
    with nc.Block() as block:
        @block.sync
        def _(sp):
            sp.dma_start(g.bqk[:, :, :], g.t["b_QK"]).then_inc(s_in, 16)
            sp.dma_start(g.bv[:, :], g.t["b_V"]).then_inc(s_in, 16)
            sp.dma_start(g.bo[:, :], g.t["b_O"].partition_broadcast(P)).then_inc(s_in, 16)
            sp.dma_start(g.wo1[:, :, :], g.t["wo1"]).then_inc(s_in, 16)
            sp.wait_ge(s_in, 64)

        @block.gpsimd
        def _(pool):
            pool.memset(g.wscale[:, :, 0:P], float(DH1) ** -0.5)
            pool.memset(g.wscale[:, :, P:3 * P], 1.0)

        @block.scalar
        def _(act):
            for q in range(4):
                cols = slice(q * 512, (q + 1) * 512)
                act.activation(g.xs[0][:, :, cols], g.xT[:, :, cols], ACT.Copy).then_inc(s_b, 1)

        @block.vector
        def _(dve):
            for q in range(4):
                cols = slice(q * 512, (q + 1) * 512)
                dve.wait_ge(s_b, q + 1)
                dve.tensor_tensor(g.xs[1][:, :, cols], g.xT[:, :, cols], g.xs[0][:, :, cols], ALU.subtract)
            dve.wait_ge(s_in, 64)
            dve.tensor_scalar(g.bqk[:, :, 0], g.bqk[:, :, 0], float(DH1) ** -0.5, None, ALU.mult)


OOB = 16384
XB = 8
XG = 4


def moe(nc, g, out):
    with ExitStack() as c:
        g.xn = g.sb("xn", [P, NT, D], F32, c)
        g.wk = g.sb("wk", [P, NT, 8], F32, c)
        g.widx = g.sb("widx", [P, K, NT], U32, c)
        g.ridx = g.sb("ridx", [P, K, NT], U32, c)
        g.wgu = [g.sb(f"wgu{i}", [P, DC, 2 * M], F32, c) for i in range(XB)]
        g.wd = [g.sb(f"wd{i}", [MH, 2, D], F32, c) for i in range(XB)]
        norm(nc, g, "n3", "keep")
        with ExitStack() as c2:
            router(nc, g, c2)
        with ExitStack() as c3:
            experts(nc, g, c3)
        with ExitStack() as c4:
            combine(nc, g, c4, out)


def router(nc, g, c):
    gate = g.sb("gate", [P, DC, E], F32, c)
    sgu = g.sb("sgu", [P, DC, 2 * MS], F32, c)
    sd = g.sb("sd", [MH, NMS, D], F32, c)
    before = g.sb("before", [P, P], F32, c)
    beforeb = g.sb("beforeb", [P, P], BF16, c)
    onesb = g.sb("onesb", [P, P], BF16, c)
    iota = g.sb("iota", [P, E], F32, c)
    base = g.sb("slot_base", [P, E], F32, c)
    sc = g.sb("scores", [P, NT, E], F32, c)
    msc = g.sb("masked_scores", [P, NT, E], F32, c)
    tmp = g.sb("r_tmp", [P, NT, E], F32, c)
    slot = g.sb("slot", [P, NT, E], F32, c)
    oh = g.sb("onehot", [P, K, NT, E], BF16, c)
    mask = g.sb("mask", [P, NT, E], BF16, c)
    cm = g.sb("cumulated", [P, NT + 1, E], BF16, c)
    small = g.sb("r_small", [P, 4, NT], F32, c)
    gmx = g.sb("gmx", [P, NT, NG], F32, c)
    g8 = g.sb("g8", [P, NT, 8], F32, c)
    gi = g.sb("gi", [P, NT, 8], U32, c)
    gif = g.sb("gif", [P, NT, 8], F32, c)
    gmask = g.sb("gmask", [P, 2, NT, NG], F32, c)
    cnt = g.sb("cnt", [P, E], F32, c)
    v = g.sb("v", [P, K, NT], F32, c)
    v2 = g.sb("v2", [P, K, NT], F32, c)
    hT = g.sb("shared_h", [MH, NMS, T], F32, c)
    sg = [g.sb(f"shared_g{i}", [MH, 512], F32, c) for i in range(2)]
    s_in, s_ch, s_lg, s_ex, s_m, s_pos, s_w = [g.sem(f"r_{n}") for n in
                                              ("in", "chain", "logits", "exp", "mask", "pos", "weights")]
    s_gu, s_sil, s_h, s_dn, s_add, s_idx, s_sc, s_cst = [g.sem(f"r_{n}") for n in
                                                       ("gu", "silu", "h", "down", "add", "idx", "scatter", "const")]
    g.s_wgu = [g.sem(f"x_wgu{i}") for i in range(XB)]
    logits = g.bank[0].rearrange("p a n -> p (a n)").rearrange("p (t e) -> p t e", e=E)
    pos = g.bank[1].rearrange("p a n -> p (a n)").rearrange("p (t e) -> p t e", e=E)
    count = g.bank[0][:, 0, 0:E]
    NQ = T // 512
    with nc.Block() as block:
        @block.sync
        def _(sp):
            for dst, name in ((gate, "gate"), ):
                sp.dma_start(dst[:, :, :], g.t[name].rearrange("(c p) n -> p c n", p=P)).then_inc(s_in, 16)
            sp.dma_start(before[:, :], g.t["c_before"]).then_inc(s_in, 16)
            sp.dma_start(iota[:, :], g.t["c_iota"]).then_inc(s_in, 16)
            sp.dma_start(sgu[:, :, :], g.t["sgu"]).then_inc(s_w, 16)
            sp.dma_start(sd[:, :, :], g.t["sd"]).then_inc(s_w, 16)
            for e in range(XB):
                sp.dma_start(g.wgu[e][:, :, :], g.t["wgu"][e]).then_inc(g.s_wgu[e], 16)
                sp.dma_start(g.wd[e][:, :, :], g.t["wd"][e]).then_inc(g.s_wgu[e], 16)

        gu_steps = [(q, m) for q in range(NQ) for m in range(NMS)]

        @block.tensor
        def _(pe):
            pe.wait_ge(s_in, 48)
            for t in range(NT):
                for c_ in range(DC):
                    ins = pe.matmul(logits[:, t, :], g.xT[:, c_, t * P:(t + 1) * P], gate[:, c_, :],
                                    start=(c_ == 0), stop=(c_ == DC - 1))
            ins.then_inc(s_lg, 1)
            pe.wait_ge(s_w, 32)

            def gate_up(n):
                q, m = gu_steps[n]
                if n >= 2:
                    pe.wait_ge(s_h, n - 1)
                for half in range(2):
                    for c_ in range(DC):
                        ins = pe.matmul(g.bank[2 + half][0:MH, n % 2, :],
                                        sgu[:, c_, half * MS + m * MH:half * MS + (m + 1) * MH],
                                        g.xT[:, c_, q * 512:(q + 1) * 512],
                                        start=(c_ == 0), stop=(c_ == DC - 1))
                ins.then_inc(s_gu, 1)

            for n in range(len(gu_steps)):
                gate_up(n)
            pe.wait_ge(s_m, 1)
            for half in range(2):
                pe.matmul(g.bank[1][:, half, :], beforeb[:, :],
                          mask[:, half * 8:half * 8 + 8, :].rearrange("p t e -> p (t e)"), start=True, stop=False)
                pe.matmul(g.bank[1][:, half, :], onesb[:, :],
                          cm[:, half * 8:half * 8 + 8, :].rearrange("p t e -> p (t e)"), start=False, stop=True)
            pe.matmul(count, onesb[:, :], cm[:, NT, :], start=True, stop=True).then_inc(s_pos, 1)
            for t in range(NT):
                if t == 0:
                    pe.wait_ge(s_h, len(gu_steps))
                if t >= 2:
                    pe.wait_ge(s_add, t - 1)
                for m in range(NMS):
                    ins = pe.matmul(g.bank[2 + t % 2][:, 0, 0:D], hT[:, m, t * P:(t + 1) * P], sd[:, m, :],
                                    start=(m == 0), stop=(m == NMS - 1))
                ins.then_inc(s_dn, 1)

        @block.scalar
        def _(act):
            act.wait_ge(s_ex, 1)
            act.activation(sc[:, :, :], tmp[:, :, :], ACT.Exp).then_inc(s_ex, 1)
            for n in range(len(gu_steps)):
                act.wait_ge(s_gu, n + 1)
                if n >= 2:
                    act.wait_ge(s_h, n - 1)
                act.activation(sg[n % 2][:, :], g.bank[2][0:MH, n % 2, :], ACT.Silu).then_inc(s_sil, 1)

        @block.vector
        def _(dve):
            n = 0

            def chained(ins):
                nonlocal n
                n += 1
                ins.then_inc(s_ch, 1)
                dve.wait_ge(s_ch, n)

            done = 0

            def shared(upto):
                nonlocal done
                while done < upto:
                    q, m = gu_steps[done]
                    dve.wait_ge(s_sil, done + 1)
                    dve.tensor_tensor(hT[:, m, q * 512:(q + 1) * 512], g.bank[3][0:MH, done % 2, :],
                                      sg[done % 2][:, :], ALU.mult).then_inc(s_h, 1)
                    done += 1

            dve.wait_ge(s_in, 48)
            chained(dve.tensor_copy(beforeb[:, :], before[:, :]))
            chained(dve.memset(onesb[:, :], 1.0))
            chained(dve.memset(cm[:, 0, :], 0.0))
            dve.tensor_scalar(base[:, :], iota[:, :], float(C), None, ALU.mult).then_inc(s_cst, 1)
            dve.wait_ge(s_cst, 1)
            dve.wait_ge(s_lg, 1)
            mx, rs = small[:, 0, :], small[:, 1, :]
            chained(dve.tensor_reduce(mx, logits, AX.X, ALU.max))
            dve.tensor_tensor(tmp[:, :, :], logits, mx.unsqueeze(2).to_broadcast([P, NT, E]),
                              ALU.subtract).then_inc(s_ex, 1)
            dve.wait_ge(s_ex, 2)
            chained(dve.tensor_reduce(rs, sc[:, :, :], AX.X, ALU.add))
            chained(dve.reciprocal(rs, rs))
            chained(dve.tensor_tensor(sc[:, :, :], sc[:, :, :], rs.unsqueeze(2).to_broadcast([P, NT, E]), ALU.mult))
            shared(2)
            chained(dve.tensor_reduce(gmx[:, :, :], sc.rearrange("p t (a b) -> p t a b", b=GS), AX.X, ALU.max))
            for t in range(NT):
                ins = dve.max(g8[:, t, :], gmx[:, t, :])
            chained(ins)
            for t in range(NT):
                ins = dve.max_index(gi[:, t, :], g8[:, t, :], gmx[:, t, :])
            chained(ins)
            chained(dve.tensor_copy(gif[:, :, :], gi[:, :, :]))
            gid = iota[:, 0:NG].unsqueeze(1).to_broadcast([P, NT, NG])
            for k in range(TG):
                chained(dve.tensor_tensor(gmask[:, min(k, 1)], gid, gif[:, :, k:k + 1].to_broadcast([P, NT, NG]),
                                          ALU.is_equal))
                if k:
                    chained(dve.tensor_tensor(gmask[:, 0], gmask[:, 0], gmask[:, 1], ALU.add))
            chained(dve.tensor_tensor(msc.rearrange("p t (a b) -> p (t a) b", b=GS),
                                      sc.rearrange("p t (a b) -> p (t a) b", b=GS),
                                      gmask[:, 0].rearrange("p t a -> p (t a)").unsqueeze(2).to_broadcast(
                                          [P, NT * NG, GS]), ALU.mult))
            shared(4)
            for t in range(NT):
                ins = dve.max(g.wk[:, t, :], msc[:, t, :])
            chained(ins)
            for t in range(NT):
                ins = dve.max_index(gi[:, t, :], g.wk[:, t, :], msc[:, t, :])
            chained(ins)
            chained(dve.tensor_copy(gif[:, :, :], gi[:, :, :]))
            shared(6)
            eid = iota[:, :].unsqueeze(1).to_broadcast([P, NT, E])
            for k in range(K):
                chained(dve.tensor_tensor(oh[:, k], eid, gif[:, :, k:k + 1].to_broadcast([P, NT, E]), ALU.is_equal))
                if k:
                    chained(dve.tensor_tensor(mask[:, :, :], oh[:, 0] if k == 1 else mask[:, :, :], oh[:, k], ALU.add))
                shared(7 + k)
            for t in range(NT):
                chained(dve.tensor_tensor(cm[:, t + 1, :], cm[:, t, :], mask[:, t, :], ALU.add))
            dve.nop().then_inc(s_m, 1)
            shared(len(gu_steps))
            dve.wait_ge(s_pos, 1)
            chained(dve.tensor_scalar(cnt[:, :], count, -1.0, None, ALU.add))
            chained(dve.tensor_tensor(tmp[:, :, :], pos, cnt[:, :].unsqueeze(1).to_broadcast([P, NT, E]),
                                      ALU.not_equal))
            chained(dve.tensor_scalar(slot[:, :, :], pos, C - 1.5, float(OOB), ALU.is_gt, ALU.mult))
            chained(dve.tensor_tensor(tmp[:, :, :], tmp[:, :, :], slot[:, :, :], ALU.mult))
            chained(dve.tensor_scalar(slot[:, :, :], pos, float(C - 1), None, ALU.min))
            chained(dve.tensor_tensor(slot[:, :, :], slot[:, :, :], tmp[:, :, :], ALU.add))
            chained(dve.tensor_tensor(slot[:, :, :], slot[:, :, :], base[:, :].unsqueeze(1).to_broadcast([P, NT, E]),
                                      ALU.add))
            for k in range(K):
                chained(dve.tensor_tensor(tmp[:, :, :], slot[:, :, :], oh[:, k], ALU.mult))
                chained(dve.tensor_reduce(v[:, k, :], tmp[:, :, :], AX.X, ALU.add))
            chained(dve.tensor_copy(g.widx[:, :, :], v[:, :, :]))
            dve.nop().then_inc(s_idx, 1)
            chained(dve.tensor_scalar(v2[:, :, :], v[:, :, :], float(OOB) - 0.5, -float(OOB), ALU.is_gt, ALU.mult))
            chained(dve.tensor_tensor(v[:, :, :], v[:, :, :], v2[:, :, :], ALU.add))
            chained(dve.tensor_copy(g.ridx[:, :, :], v[:, :, :]))
            for t in range(NT):
                dve.wait_ge(s_dn, t + 1)
                dve.tensor_tensor(g.x[:, t, :], g.bank[2 + t % 2][:, 0, 0:D], g.x[:, t, :], ALU.add).then_inc(s_add, 1)

        @block.gpsimd
        def _(pool):
            pool.wait_ge(g.s_zero, 16 * ZD)
            pool.wait_ge(s_idx, 1)
            for t in range(NT):
                for k in range(K):
                    pool.indirect_dma_start(out=g.xrows, out_offset=bass.IndirectOffsetOnAxis(
                        ap=g.widx[:, k, t:t + 1], axis=0), in_=g.xn[:, t, :], in_offset=None,
                        bounds_check=E * C - 1, oob_is_err=False).then_inc(s_sc, 16)
            pool.wait_ge(s_sc, 16 * NT * K)


def experts(nc, g, c):
    rows = [g.sb(f"x_rows{i}", [C, XG, D], F32, c) for i in range(XB // XG)]
    xeT = [g.sb(f"x_T{i}", [P, 2, DC, C], F32, c) for i in range(2)]
    sg = [g.sb(f"x_sg{i}", [MH, 2, C], F32, c) for i in range(2)]
    h = [g.sb(f"x_h{i}", [MH, 2, C], F32, c) for i in range(2)]
    orow = [g.sb(f"x_o{i}", [C, XG, D], F32, c) for i in range(XB // XG)]
    NR = XB // XG
    s_row = [g.sem(f"x_row{i}") for i in range(NR)]
    s_out = [g.sem(f"x_out{i}") for i in range(NR)]
    s_t, s_tc, s_gu, s_sil, s_h, s_dn, s_o = [g.sem(f"x_{n}") for n in ("t", "tc", "gu", "silu", "h", "down", "o")]
    xv = g.xrows.rearrange("(e c) d -> c e d", c=C)
    ov = g.orows.rearrange("(e c) d -> c e d", c=C)

    with nc.Block() as block:
        @block.sync
        def _(sp):
            for i in range(NR):
                sp.dma_start(rows[i][:, :, :], xv[:, i * XG:(i + 1) * XG, :]).then_inc(s_row[i], 16)
            with sp.Fori(1, E // XB) as i:
                for s in range(XB):
                    if s % XG == 0:
                        sp.wait_ge(s_t, i * (XB // 2) + ((s + XG) // 2 - XB // 2))
                        sp.dma_start(rows[s // XG][:, :, :], xv[:, ds(i * XB + s, XG), :]).then_inc(s_row[s // XG], 16)
                    sp.wait_ge(s_dn, i * XB + (s - XB + 3))
                    sp.dma_start(g.wgu[s][:, :, :], g.t["wgu"][ds(i * XB + s, 1), :, :, :].rearrange(
                        "o p c n -> (o p) c n")).then_inc(g.s_wgu[s], 16)
                    sp.dma_start(g.wd[s][:, :, :], g.t["wd"][ds(i * XB + s, 1), :, :, :].rearrange(
                        "o p c n -> (o p) c n")).then_inc(g.s_wgu[s], 16)

        @block.tensor
        def _(pe):
            def turn_pair(p_num, s):
                if s % XG == 0:
                    pe.wait_ge(s_row[s // XG], p_num * 4 + (16 - 2 * s))
                pe.wait_ge(s_tc, p_num + 1)
                b_ = g.bank[0][:, (s // 2) % 2, :]
                for a in range(2):
                    for c_ in range(DC):
                        o = (a * DC + c_) * C
                        ins = pe.transpose(b_[:, o:o + C], rows[s // XG][:, (s + a) % XG, c_ * P:(c_ + 1) * P],
                                           g.identf[0:C, 0:C])
                ins.then_inc(s_t, 1)

            def gu(e, s, half_e):
                pe.wait_ge(s_tc, half_e + 3)
                pe.wait_ge(g.s_wgu[s], e * 4 + (32 - 4 * s))
                pe.wait_ge(s_h, e + 1)
                b_ = g.bank[1][0:MH, s % 2, :]
                for m in range(4):
                    for c_ in range(DC):
                        ins = pe.matmul(b_[:, m * C:(m + 1) * C], g.wgu[s][:, c_, m * MH:(m + 1) * MH],
                                        xeT[(s // 2) % 2][:, s % 2, c_, :], start=(c_ == 0), stop=(c_ == DC - 1))
                ins.then_inc(s_gu, 1)

            def down(e, s):
                pe.wait_ge(s_h, e + 3)
                pe.wait_ge(s_o, e + 1)
                for m in range(2):
                    ins = pe.matmul(g.bank[2][0:C, s % 2, 0:D], h[s % 2][:, m, :], g.wd[s][:, m, :],
                                    start=(m == 0), stop=(m == 1))
                ins.then_inc(s_dn, 1)

            pe.nop().then_inc(s_gu, 4)
            pe.nop().then_inc(s_dn, 2)
            turn_pair(0, 0)
            gu(0, 0, 0)

            def one_pass(i, more):
                for s in range(XB):
                    if s % 2 == 0 and (more or s + 2 < XB):
                        turn_pair(i * (XB // 2) + (s // 2 + 1), (s + 2) % XB)
                    if more or s + 1 < XB:
                        gu(i * XB + (s + 1), (s + 1) % XB, i * (XB // 2) + (s + 1) // 2)
                    down(i * XB + s, s)

            with pe.Fori(0, E // XB - 1) as i:
                one_pass(i, True)
            one_pass(E // XB - 1, False)

        def walk(eng, step_turn, step_expert, step_down):
            step_turn(0, 0)
            step_expert(0, 0)

            def one_pass(i, more):
                for s in range(XB):
                    if s % 2 == 0 and (more or s + 2 < XB):
                        step_turn(i * (XB // 2) + (s // 2 + 1), (s + 2) % XB)
                    if more or s + 1 < XB:
                        step_expert(i * XB + (s + 1), (s + 1) % XB)
                    step_down(i, i * XB + s, s)

            with eng.Fori(0, E // XB - 1) as i:
                one_pass(i, True)
            one_pass(E // XB - 1, False)

        @block.scalar
        def _(act):
            act.nop().then_inc(s_o, 2)
            for i in range(NR):
                act.nop().then_inc(s_out[i], 16)

            def silu(e, s):
                act.wait_ge(s_gu, e + 5)
                act.wait_ge(s_h, e + 1)
                act.activation(sg[s % 2][:, :, :], g.bank[1][0:MH, s % 2, 0:2 * C].rearrange(
                    "p (m c) -> p m c", c=C), ACT.Silu).then_inc(s_sil, 1)

            def out_rows(i, e, s):
                act.wait_ge(s_dn, e + 3)
                if s % XG == 0:
                    act.wait_ge(s_out[s // XG], i * 16 + 16)
                act.activation(orow[s // XG][:, s % XG, :], g.bank[2][0:C, s % 2, 0:D], ACT.Copy).then_inc(s_o, 1)
                if s % XG == XG - 1:
                    act.wait_ge(s_o, e + 3)
                    act.dma_start(ov[:, ds(e - (XG - 1), XG), :], orow[s // XG][:, :, :]).then_inc(s_out[s // XG], 16)

            walk(act, lambda p_num, s: None, silu, out_rows)
            for i in range(NR):
                act.wait_ge(s_out[i], 16 * (E // XB) + 16)

        @block.vector
        def _(dve):
            dve.nop().then_inc(s_tc, 2)
            dve.nop().then_inc(s_h, 2)

            def turned(p_num, s):
                dve.wait_ge(s_t, p_num + 1)
                dve.wait_ge(s_gu, p_num * 2 + 2)
                dve.tensor_copy(xeT[(s // 2) % 2].rearrange("p a c n -> p (a c n)"),
                                g.bank[0][:, (s // 2) % 2, 0:2 * DC * C]).then_inc(s_tc, 1)

            def product(e, s):
                dve.wait_ge(s_sil, e + 1)
                dve.wait_ge(s_dn, e + 1)
                dve.tensor_tensor(h[s % 2][:, :, :], g.bank[1][0:MH, s % 2, 2 * C:4 * C].rearrange(
                    "p (m c) -> p m c", c=C), sg[s % 2][:, :, :], ALU.mult).then_inc(s_h, 1)

            walk(dve, turned, product, lambda i, e, s: None)


def combine(nc, g, c, out):
    NB = 4
    rows = [g.sb(f"c_rows{i}", [P, K, D], F32, c) for i in range(NB)]
    s_g = [g.sem(f"c_gather{i}") for i in range(NB)]
    s_acc, s_done, s_st = g.sem("c_acc"), g.sem("c_done"), g.sem("c_store")
    ov = out.rearrange("b (n p) d -> p (b n) d", p=P)
    with nc.Block() as block:
        @block.gpsimd
        def _(pool):
            for t in range(NT):
                if t >= NB:
                    pool.wait_ge(s_acc, K * (t - NB + 1))
                for k in range(K):
                    pool.indirect_dma_start(out=rows[t % NB][:, k, :], out_offset=None, in_=g.orows,
                                            in_offset=bass.IndirectOffsetOnAxis(ap=g.ridx[:, k, t:t + 1], axis=0),
                                            bounds_check=E * C - 1, oob_is_err=False).then_inc(s_g[t % NB], 16)

        @block.vector
        def _(dve):
            for t in range(NT):
                dve.wait_ge(s_g[t % NB], 16 * K * (t // NB + 1))
                for k in range(K):
                    if k:
                        dve.wait_ge(s_acc, K * t + k)
                    dve.scalar_tensor_tensor(g.x[:, t, :], rows[t % NB][:, k, :], g.wk[:, t, k:k + 1],
                                             g.x[:, t, :], ALU.mult, ALU.add).then_inc(s_acc, 1)

        @block.sync
        def _(sp):
            for t in range(NT):
                sp.wait_ge(s_acc, K * (t + 1))
                sp.dma_start(ov[:, t, :], g.x[:, t, :]).then_inc(s_st, 16)
            sp.wait_ge(s_st, 16 * NT)



def kernel(**inputs):
    import numpy as _np
    import concourse.bacc as _bacc
    from concourse import mybir as _mybir
    from concourse.bass_utils import run_bass_kernel_spmd as _run

    a = {k: _np.asarray(v) for k, v in inputs.items()}
    host = {
        "x": a["L0_attn_x"],
        "wqkv0": _np.concatenate([a["L0_attn_Wq"].T, a["L0_attn_Wk"].T, a["L0_attn_Wv"].T], axis=1),
        "wo0": a["L0_attn_Wo"].T,
        "ffn_w": a["L0_ffn_weight"].T,
        "gamma": a["L0_ffn_gamma"],
        "beta": a["L0_ffn_beta"],
        "ln_w": a["L0_ffn_ln_weight"].reshape(DC, P).T,
        "ln_b": a["L0_ffn_ln_bias"].reshape(DC, P).T,
        "wqkv1": _np.concatenate([a[f"L1_attn_W_{n}"] for n in "QKV"], axis=2).reshape(
            H, DC, P, 3 * DH1).transpose(0, 2, 1, 3),
        "wo1": a["L1_attn_W_O"].transpose(1, 0, 2),
        "b_QK": np.stack([a["L1_attn_b_Q"].T, a["L1_attn_b_K"].T], 2), "b_V": a["L1_attn_b_V"].T,
        "b_O": a["L1_attn_b_O"],
        "gate": a["L1_ffn_gate_weight"].T,
        "wgu": _np.concatenate([a["L1_ffn_Wg"], a["L1_ffn_Wu"]], axis=1).transpose(0, 2, 1).reshape(
            E, DC, P, 2 * M).transpose(0, 2, 1, 3),
        "wd": a["L1_ffn_Wd"].transpose(0, 2, 1).reshape(E, 2, MH, D).transpose(0, 2, 1, 3),
        "sgu": _np.concatenate([a["L1_ffn_Sg"].T, a["L1_ffn_Su"].T], axis=1).reshape(
            DC, P, 2 * MS).transpose(1, 0, 2),
        "sd": a["L1_ffn_Sd"].T.reshape(NMS, MH, D).transpose(1, 0, 2),
    }
    host.update(constants())
    nc = _bacc.Bacc("TRN2", target_bir_lowering=False, num_devices=1)
    arrays, t_in = {}, {}
    for name, arr in host.items():
        arrays[f"in_{name}"] = _np.ascontiguousarray(arr)
        t_in[name] = nc.dram_tensor(f"in_{name}", arr.shape, _mybir.dt.from_np(arr.dtype), kind="ExternalInput").ap()
    out = nc.dram_tensor("out_0", (B, S, D), _mybir.dt.float32, kind="ExternalOutput").ap()
    build(nc, t_in, out)
    r = _run(nc, [arrays], core_ids=[0])
    return r.results[0]["out_0"]
```

```python
from contextlib import ExitStack

import numpy as np
import concourse.bass as bass
from concourse import mybir

F32 = mybir.dt.float32
F16 = mybir.dt.float16
BF16 = mybir.dt.bfloat16
U32 = mybir.dt.uint32
ALU = mybir.AluOpType
ACT = mybir.ActivationFunctionType
AX = mybir.AxisListType
ds = bass.ds

P = 128
B, S, D = 2, 1024, 256
T = B * S
NT = T // P
BT = S // P
DC = D // P
H = 16
DH0 = D // H
DH1 = 128
EPS = 1e-5
THETA = 10000.0
E, M, C = 64, 176, 96
MH = M // 2
K, NG, TG = 6, 8, 3
GS = E // NG
MS = 352
SM = [(m, min(P, MS - m)) for m in range(0, MS, P)]
NMS = len(SM)
NEG = -1e30
OOB = 65536
ZD = 24


def constants():
    inv = THETA ** (-np.arange(0, DH0, 2, dtype=np.float32) / DH0)
    ang = np.arange(S, dtype=np.float32)[:, None] * inv[None, :].astype(np.float32)
    cos = np.repeat(np.cos(ang), 2, axis=1).astype(np.float32)
    sin = np.repeat(np.sin(ang), 2, axis=1).astype(np.float32)
    sin[:, 0::2] *= -1
    rope = np.stack([cos, sin], 1).reshape(BT, P, 2, DH0).transpose(1, 0, 2, 3)
    ident = np.eye(P, dtype=np.float32)
    mask = np.where(np.arange(P)[:, None] >= np.arange(P)[None, :], 0.0, NEG).astype(np.float32)
    before = (np.arange(P)[:, None] < np.arange(P)[None, :]).astype(np.float32)
    iota = np.broadcast_to(np.arange(C, dtype=np.float32), (P, C))
    token = np.arange(T, dtype=np.float32).reshape(NT, P).T
    last = np.where(np.arange(P) == C - 1, OOB, -T).astype(np.float32)[:, None]
    return {"c_rope": np.ascontiguousarray(rope), "c_ident": ident, "c_mask": mask,
            "c_before": before, "c_iota": np.ascontiguousarray(iota),
            "c_token": np.ascontiguousarray(token), "c_last": last}


class Prog:
    pass


def build(nc, t_in, out):
    g = Prog()
    with ExitStack() as ctx:
        def sb(name, shape, dt=F32, c=ctx):
            return c.enter_context(nc.sbuf_tensor(name, shape, dt))

        made = {}

        def sem(name):
            if name not in made:
                made[name] = ctx.enter_context(nc.semaphore(name))
            return made[name]

        g.sb, g.sem, g.t = sb, sem, t_in
        g.bank = [ctx.enter_context(nc.psum_tensor(f"bank{i}", [P, 2, 512], F32)) for i in range(4)]
        g.x = sb("x", [P, NT, D])
        g.identf = sb("identf", [P, P])
        g.identh = sb("identh", [P, P], F16)
        g.identb = sb("identb", [P, P], BF16)
        g.maskb = sb("maskb", [P, P], BF16)
        g.rstd = sb("rstd", [P, NT])
        g.stats = sb("stats", [P, NT, 6])
        g.zero = sb("zero", [P, K * T * D // P // ZD])
        g.xrows = nc.dram_tensor("token_rows", (T, D), F32, kind="Internal").ap()
        g.krows = nc.dram_tensor("choice_rows", (K * T, D), F32, kind="Internal").ap()
        g.lrows = nc.dram_tensor("last_rows", (E, D), F32, kind="Internal").ap()
        g.s_zero = sem("zeros_landed")
        g.mean = sb("mean", [P, NT])

        load(nc, g)
        with ExitStack() as cx:
            g.xT = g.sb("xT0", [P, DC, T], F32, cx)
            ffn_loads, *ffn_work = ffn_weights(g, cx)
            with ExitStack() as c0:
                with ExitStack() as cw:
                    norm(nc, g, "n0", None, l0_buffers(nc, g, c0, cw, ffn_loads))
                    l0_qkv(nc, g, *ffn_work)
                l0_attention(nc, g)
                proj_out(nc, g, "o0", 0)
            norm(nc, g, "n1", "ffn")
            l0_ffn(nc, g)
        with ExitStack() as c2:
            norm(nc, g, "n2", "split", *l1_buffers(nc, g, c2))
            for b in range(B):
                l1_attention(nc, g, b)
                proj_out(nc, g, "o1", 1, b)
        moe(nc, g, out)


def load(nc, g):
    s_x, s_c, s_v = g.sem("ld_x"), g.sem("ld_const"), g.sem("ld_cast")
    with ExitStack() as c:
        maskf = g.sb("maskf", [P, P], F32, c)
        with nc.Block() as block:
            @block.sync
            def _(sp):
                sp.dma_start(g.identf[:, :], g.t["c_ident"]).then_inc(s_c, 16)
                sp.dma_start(maskf[:, :], g.t["c_mask"]).then_inc(s_c, 16)
                sp.dma_start(g.x[:, :, :], g.t["x"].rearrange("b (n p) d -> p (b n) d", p=P)).then_inc(s_x, 16)

            @block.gpsimd
            def _(pool):
                pool.memset(g.zero[:, :], 0.0)

            @block.vector
            def _(dve):
                dve.wait_ge(s_c, 32)
                dve.tensor_copy(g.identh[:, :], g.identf[:, :]).then_inc(s_v, 1)
                dve.tensor_copy(g.identb[:, :], g.identf[:, :]).then_inc(s_v, 1)
                dve.tensor_copy(g.maskb[:, :], maskf[:, :]).then_inc(s_v, 1)
                dve.wait_ge(s_x, 16)
                dve.wait_ge(s_v, 3)


def norm(nc, g, tag, kind, loads=None, pool_work=None):
    s_st, s_ag, s_sq, s_ch = [g.sem(f"{tag}_{n}") for n in ("stats", "aggr", "sqrt", "chain")]
    s_xn, s_tr = g.sem(f"{tag}_xn"), g.sem(f"{tag}_tr")
    s_ev = [g.sem(f"{tag}_evac{i}") for i in range(2)]
    s_hi = g.sem(f"{tag}_hi") if kind == "split" else None
    s_kept = g.sem(f"{tag}_stored") if kind == "keep" else None
    with ExitStack() as c:
        st = g.stats
        mv = g.sb(f"{tag}_mv", [P, NT, 2], F32, c)
        sq = g.sb(f"{tag}_sq", [P, NT], F32, c)
        tmp = g.sb(f"{tag}_tmp", [P, 2, NT], F32, c)
        xn = g.xn if kind == "keep" else g.sb(f"{tag}_xnb", [P, NT, D], F32, c)
        ve = tmp[:, 0, :]
        t1 = tmp[:, 1, :]
        levels = 2 if kind == "ffn" else 1
        with nc.Block() as block:
            def evac(eng, p):
                eng.wait_ge(s_tr, p + 1)
                for c_ in range(DC):
                    src = g.bank[p % 2][:, 0, c_ * 256:(c_ + 1) * 256]
                    dst = g.xT[:, c_, p * 256:(p + 1) * 256]
                    if p % 2:
                        if kind == "ffn":
                            ins = eng.tensor_scalar(dst, src, g.lnw[:, c_:c_ + 1], g.lnb[:, c_:c_ + 1],
                                                    ALU.mult, ALU.add)
                        else:
                            ins = eng.tensor_copy(dst, src)
                    elif kind == "ffn":
                        ins = eng.activation(dst, src, ACT.Identity, bias=g.lnb[:, c_:c_ + 1],
                                             scale=g.lnw[:, c_:c_ + 1])
                    else:
                        ins = eng.activation(dst, src, ACT.Copy)
                ins.then_inc(s_ev[p % 2], 1)

            @block.vector
            def _(dve):
                n = 0

                def chained(ins):
                    nonlocal n
                    n += 1
                    ins.then_inc(s_ch, 1)
                    dve.wait_ge(s_ch, n)

                if tag == "n0":
                    for t in range(NT):
                        dve.bn_stats(st[:, t, :], g.x[:, t, :]).then_inc(s_st, 1)
                for t in range(NT):
                    if tag == "n0":
                        dve.wait_ge(s_st, t + 1)
                    dve.bn_aggr(mv[:, t, :], st[:, t, :]).then_inc(s_ag, 1)
                dve.wait_ge(s_ag, NT)
                chained(dve.tensor_copy(g.mean[:, :], mv[:, :, 0]))
                chained(dve.tensor_copy(t1, mv[:, :, 1]))
                for lv in range(levels):
                    chained(dve.tensor_scalar(ve, t1, EPS, None, ALU.add))
                    dve.wait_ge(s_sq, lv + 1)
                    chained(dve.reciprocal(sq[:, :], sq[:, :]))
                    r = g.rstd[:, :]
                    one = sq[:, :]
                    chained(dve.tensor_tensor(t1, one, one, ALU.mult))
                    chained(dve.tensor_tensor(t1, t1, ve, ALU.mult))
                    chained(dve.tensor_scalar(t1, t1, -0.5, 1.5, ALU.mult, ALU.add))
                    if lv == 0:
                        chained(dve.tensor_tensor(r, one, t1, ALU.mult))
                    else:
                        chained(dve.tensor_tensor(one, one, t1, ALU.mult))
                        chained(dve.tensor_tensor(r, r, one, ALU.mult))
                    if lv + 1 < levels:
                        chained(dve.tensor_tensor(t1, r, r, ALU.mult))
                        chained(dve.tensor_tensor(t1, t1, mv[:, :, 1], ALU.mult))
                for t in range(NT):
                    dve.tensor_scalar(xn[:, t, :], g.x[:, t, :], g.mean[:, t:t + 1], g.rstd[:, t:t + 1],
                                      ALU.subtract, ALU.mult).then_inc(s_xn, 1)
                if kind == "split":
                    for p in range(NT // 2):
                        dve.wait_ge(s_hi, DC * (p + 1))
                        for c_ in range(DC):
                            cols = slice(p * 256, (p + 1) * 256)
                            ins = dve.tensor_tensor(g.xs[1][:, c_, cols], g.bank[p % 2][:, 0, c_ * 256:(c_ + 1) * 256],
                                                    g.xs[0][:, c_, cols], ALU.subtract)
                        ins.then_inc(s_ev[p % 2], 1)
                else:
                    for p in range(1, NT // 2, 2):
                        evac(dve, p)

            @block.scalar
            def _(act):
                for lv in range(levels):
                    act.wait_ge(s_ch, 3 if lv == 0 else 11)
                    act.activation(sq[:, :], ve, ACT.Sqrt).then_inc(s_sq, 1)
                if kind == "split":
                    for p in range(NT // 2):
                        act.wait_ge(s_tr, p + 1)
                        for c_ in range(DC):
                            act.activation(g.xs[0][:, c_, p * 256:(p + 1) * 256],
                                           g.bank[p % 2][:, 0, c_ * 256:(c_ + 1) * 256], ACT.Copy).then_inc(s_hi, 1)
                else:
                    for p in range(0, NT // 2, 2):
                        evac(act, p)

            @block.tensor
            def _(pe):
                for p in range(NT // 2):
                    pe.wait_ge(s_xn, 2 * p + 2)
                    if p >= 2:
                        pe.wait_ge(s_ev[p % 2], p // 2)
                    for c_ in range(DC):
                        for j in range(2):
                            ins = pe.transpose(g.bank[p % 2][:, 0, (2 * c_ + j) * P:(2 * c_ + j + 1) * P],
                                               xn[:, 2 * p + j, c_ * P:(c_ + 1) * P], g.identf[:, :])
                    ins.then_inc(s_tr, 1)

            @block.gpsimd
            def _(pool):
                if pool_work:
                    pool_work(pool)

            @block.sync
            def _(sp):
                if loads:
                    loads(sp)
                if kind == "keep":
                    xv = g.xrows.rearrange("(n p) d -> p n d", p=P)
                    for q in range(4):
                        sp.wait_ge(s_xn, 4 * q + 4)
                        sp.dma_start(xv[:, 4 * q:4 * q + 4, :], xn[:, 4 * q:4 * q + 4, :]).then_inc(s_kept, 16)
                    sp.wait_ge(s_kept, 64)


def ffn_weights(g, c):
    g.wf = g.sb("wf", [P, DC, D], F32, c)
    g.lnw = g.sb("lnw", [P, DC], F32, c)
    g.lnb = g.sb("lnb", [P, DC], F32, c)
    g.beta = g.sb("beta", [P, D], F32, c)
    s_in, s_scale, s_ab, s_all, s_sg = [g.sem(f"fw_{n}") for n in ("in", "scale", "absmax", "all", "sign")]
    w = g.sb("fw_w", [P, DC, D], F32, c)
    gam = g.sb("fw_gamma", [P, D], F32, c)
    am = g.sb("fw_am", [P, 2], F32, c)

    def loads(sp):
        sp.dma_start(w[:, :, :], g.t["ffn_w"].rearrange("(c p) n -> p c n", p=P)).then_inc(s_in, 16)
        sp.dma_start(gam[:, :], g.t["gamma"].partition_broadcast(P)).then_inc(s_in, 16)
        sp.dma_start(g.beta[:, :], g.t["beta"].partition_broadcast(P)).then_inc(s_in, 16)
        sp.dma_start(g.lnw[:, :], g.t["ln_w"]).then_inc(s_in, 16)
        sp.dma_start(g.lnb[:, :], g.t["ln_b"]).then_inc(s_in, 16)
        sp.wait_ge(s_in, 80)

    def sign(act):
        act.activation(g.wf[:, :, :], w[:, :, :], ACT.Sign).then_inc(s_sg, 1)

    def absmax(dve):
        dve.tensor_reduce(am[:, 0:1], w[:, :, :], AX.XY, ALU.max, apply_absolute_value=True).then_inc(s_ab, 1)

    def all_reduce(pool):
        pool.wait_ge(s_ab, 1)
        pool.partition_all_reduce(am[:, 1:2], am[:, 0:1], P, bass.bass_isa.ReduceOp.max).then_inc(s_all, 1)

    def scaled(dve):
        dve.wait_ge(s_all, 1)
        dve.tensor_scalar(gam[:, :], gam[:, :], am[:, 1:2], None, ALU.mult).then_inc(s_scale, 1)
        dve.wait_ge(s_scale, 1)
        dve.wait_ge(s_sg, 1)
        dve.tensor_tensor(g.wf[:, :, :], g.wf[:, :, :], gam[:, :].unsqueeze(1).to_broadcast([P, DC, D]), ALU.mult)

    return loads, sign, absmax, all_reduce, scaled


def l0_buffers(nc, g, c0, c, ffn_loads):
    g.qk = g.sb("qk_parts", [P, B * H + 3, BT, 2, 2 * DH0], F16, c0)
    g.v0 = g.sb("v0", [P, B * H, BT, DH0], F32, c0)
    g.zl = g.sb("z_by_head", [P, B * H + 1, BT * DH0], F32, c0)
    g.wo0 = g.sb("wo0", [P, DC, D], F32, c0)
    g.w0 = g.sb("wqkv0", [P, DC, 3 * D], F32, c)
    g.rope = g.sb("rope", [P, BT, 2, DH0], F32, c)
    s_in = g.sem("q0_in")

    def loads(sp):
        sp.dma_start(g.w0[:, :, :], g.t["wqkv0"].rearrange("(c p) n -> p c n", p=P)).then_inc(s_in, 16)
        sp.dma_start(g.rope[:, :, :, :], g.t["c_rope"]).then_inc(s_in, 16)
        sp.dma_start(g.wo0[:, :, :], g.t["wo0"].rearrange("(c p) n -> p c n", p=P)).then_inc(s_in, 16)
        ffn_loads(sp)
        sp.wait_ge(s_in, 48)
    return loads


def l0_qkv(nc, g, sign, absmax, all_reduce, scaled):
    w, rope = g.w0, g.rope
    s_mm, s_sw = g.sem("q0_mm"), g.sem("q0_scaled")
    s_rot, s_v, s_add, s_hi, s_lo = [g.sem(f"q0_{n}") for n in ("rot", "v", "add", "hi", "lo")]
    with ExitStack() as c:
        rot = [g.sb(f"rot{i}", [P, 2, 2 * D], F32, c) for i in range(2)]
        with nc.Block() as block:
            @block.tensor
            def _(pe):
                pe.wait_ge(s_sw, 1)
                for t in range(NT):
                    if t >= 2:
                        pe.wait_ge(s_rot, t - 1)
                        pe.wait_ge(s_v, t - 1)
                    for half in range(2):
                        cols = slice(0, 512) if half == 0 else slice(512, 768)
                        for c_ in range(DC):
                            ins = pe.matmul(g.bank[2 * half + t % 2][:, 0, 0:cols.stop - cols.start],
                                            g.xT[:, c_, t * P:(t + 1) * P], w[:, c_, cols],
                                            start=(c_ == 0), stop=(c_ == DC - 1))
                    ins.then_inc(s_mm, 1)

            @block.vector
            def _(dve):
                absmax(dve)
                dve.tensor_scalar(w[:, :, D:2 * D], w[:, :, D:2 * D], float(DH0) ** -0.5, None,
                                  ALU.mult).then_inc(s_sw, 1)

                def low(t):
                    dve.wait_ge(s_add, t + 1)
                    dve.wait_ge(s_hi, t + 1)
                    r = rot[t % 2][:, 0, :].rearrange("p (q h d) -> p q h d", q=2, h=H)
                    hs = slice(t // BT * H, (t // BT + 1) * H)
                    for q in range(2):
                        part = g.qk[:, hs, t % BT, q, :]
                        ins = dve.tensor_tensor(part[:, :, DH0:2 * DH0], r[:, q], part[:, :, 0:DH0], ALU.subtract)
                    ins.then_inc(s_lo, 1)

                for t in range(NT):
                    dve.wait_ge(s_mm, t + 1)
                    ps = g.bank[t % 2][:, 0, :]
                    r = rot[t % 2]
                    if t >= 2:
                        dve.wait_ge(s_lo, t - 1)
                    cs = rope[:, t % BT, 0, :].unsqueeze(1).to_broadcast([P, 2 * H, DH0])
                    dve.tensor_tensor(r[:, 0, :].rearrange("p (h d) -> p h d", d=DH0),
                                      ps.rearrange("p (h d) -> p h d", d=DH0), cs, ALU.mult)
                    for e in range(2):
                        sn = rope[:, t % BT, 1, e::2].unsqueeze(1).to_broadcast([P, 2 * H, DH0 // 2])
                        ins = dve.tensor_tensor(
                            r[:, 1, :].rearrange("p (h i two) -> p h i two", i=DH0 // 2, two=2)[:, :, :, e],
                            ps.rearrange("p (h i two) -> p h i two", i=DH0 // 2, two=2)[:, :, :, 1 - e],
                            sn, ALU.mult)
                    ins.then_inc(s_rot, 1)
                    if t >= 1:
                        low(t - 1)
                low(NT - 1)
                scaled(dve)

            @block.gpsimd
            def _(pool):
                pool.memset(g.qk[:, B * H:B * H + 3, :, :, :], 0.0)
                all_reduce(pool)
                for t in range(NT):
                    pool.wait_ge(s_rot, t + 1)
                    r = rot[t % 2]
                    pool.tensor_tensor(r[:, 0, :], r[:, 0, :], r[:, 1, :], ALU.add).then_inc(s_add, 1)

            @block.scalar
            def _(act):
                sign(act)
                for t in range(NT):
                    act.wait_ge(s_mm, t + 1)
                    hs = slice(t // BT * H, (t // BT + 1) * H)
                    act.activation(g.v0[:, hs, t % BT, :], g.bank[2 + t % 2][:, 0, 0:D].rearrange(
                        "p (h d) -> p h d", d=DH0), ACT.Copy).then_inc(s_v, 1)
                    act.wait_ge(s_add, t + 1)
                    r = rot[t % 2][:, 0, :].rearrange("p (q h d) -> p q h d", q=2, h=H)
                    for q in range(2):
                        ins = act.activation(g.qk[:, hs, t % BT, q, 0:DH0], r[:, q], ACT.Copy)
                    ins.then_inc(s_hi, 1)


def l0_attention(nc, g):
    NH = B * H
    R = P
    CH = 4
    QW = S // CH
    VW = 32
    PRO_MISC, PRO_DVE, PRO_ACT = 10, 4, 6
    names = ("st_ready", "e_ready", "s1_ready", "m_ready", "misc_ready", "misc_dve", "misc_act",
             "pv_ready", "zt_out", "inv", "preset")
    st_ready, e_ready, s1_ready, m_ready, misc_ready, misc_dve, misc_act, pv_ready, zt_out, s_inv, s_pre = \
        [g.sem(f"a0_{n}") for n in names]
    w_in = [g.sem(f"a0_w{i}") for i in range(2)]
    v_in = g.sem("a0_v_in")
    P0, ZT, MA, MB = 0, 4, 5, 6
    with ExitStack() as c:
        qT = [g.sb(f"a0_q{i}", [R, S], F16, c) for i in range(4)]
        kT = [g.sb(f"a0_k{i}", [R, S], F16, c) for i in range(4)]
        qh = [g.sb(f"a0_qh{i}", [P, BT, 2, R], F16, c) for i in range(2)]
        vh = [g.sb(f"a0_vh{i}", [P, BT, VW], F32, c) for i in range(4)]
        pT = [g.sb(f"a0_p{i}", [P, S], F32, c) for i in range(4)]
        negm = [g.sb(f"a0_negm{i}", [P, BT], F16, c) for i in range(2)]
        zts = [g.sb(f"a0_zt{i}", [P, QW], F32, c) for i in range(2)]
        rinv = g.sb("a0_rinv", [P, 2, CH], F32, c)
        ST = [g.bank[i].rearrange("p a n -> p (a n)") for i in range(2)]
        S1 = g.bank[2]
        zT = g.bank[3][:, 0, 0:QW]
        misc = g.bank[3][:, 1, :]

        def s1_place(t):
            i = BT - 1 - t
            return S1.rearrange("p a n -> p (a n)")[:, 0:(i + 1) * P] if i >= 4 else S1[:, t % 2, 0:(i + 1) * P]

        s1_steps = [[(1, 1)], [(1, 2)], [(1, 3)], [(1, 4)], [(1, 5), (1, 6)], [(1, 7)], [], [(2, 0)]]

        def all_steps(eng, step):
            for k in range(2):
                step(0, 0, k, True)
            with eng.Fori(0, NH // 4) as i:
                for s in range(4):
                    for k in range(2, BT):
                        step(i * 4 + s, s, k, False)
                    for k in range(2):
                        step(i * 4 + (s + 1), (s + 1) % 4, k, False)

        with nc.Block() as block:
            @block.gpsimd
            def _(pool):
                for i in range(2):
                    pool.memset(qh[i][:, :, :, 4 * DH0:R], 0.0).then_inc(s_pre, 1)
                pool.wait_ge(s_pre, 2)
                for i in range(2):
                    pool.memset(qh[i][:, :, 1, 4 * DH0:4 * DH0 + 1], 1.0).then_inc(s_pre, 1)
                for i in range(4):
                    pool.memset(vh[i][:, :, DH0 + 1:VW], 0.0).then_inc(s_pre, 1)
                    pool.memset(vh[i][:, :, DH0:DH0 + 1], 1.0).then_inc(s_pre, 1)
                pool.memset(zts[1][:, :], 1.0).then_inc(zt_out, 1)
                pool.wait_ge(s_pre, 12)

                def fetch(m, s, v):
                    for a in range(2):
                        src = g.qk[:, ds(m, 1), :, 0, :].rearrange("p o t d -> p (o t) d")
                        pool.tensor_copy(qh[s % 2][:, :, 0, a * 2 * DH0:(a + 1) * 2 * DH0], src
                                         ).then_inc(w_in[s % 2], 1)
                        src = g.qk[:, ds(m, 1), :, 1, a * DH0:(a + 1) * DH0].rearrange("p o t d -> p (o t) d")
                        dst = qh[s % 2][:, :, 1, a * 2 * DH0:(a + 1) * 2 * DH0].rearrange("p t (r d) -> p t r d", r=2)
                        pool.tensor_copy(dst, src.unsqueeze(2).to_broadcast([P, BT, 2, DH0])).then_inc(w_in[s % 2], 1)
                    if v:
                        src = g.v0[:, ds(m, 1), :, :].rearrange("p o t d -> p (o t) d")
                        pool.tensor_copy(vh[s][:, :, 0:DH0], src).then_inc(v_in, 1)

                for m in range(4):
                    if m >= 2:
                        pool.wait_ge(misc_ready, 4 * (m - 1))
                    fetch(m, m, True)
                with pool.Fori(1, NH // 4) as i:
                    for s in range(4):
                        pool.wait_ge(st_ready, (i * 4 + s) * BT - (3 * BT - 3))
                        fetch(i * 4 + s, s, True)
                for m in range(NH, NH + 3):
                    pool.wait_ge(st_ready, (m - 3) * BT + 3)
                    fetch(m, m % 4, False)

            def turn_chunk(pe, k, s):
                for j in range(4):
                    ins = pe.matmul(misc[0:R, j * P:(j + 1) * P], qh[s % 2][:, (k % 2) * 4 + j, k // 2, :],
                                    g.identh[:, :], start=True, stop=True)
                ins.then_inc(misc_ready, 1)

            def max_scores(pe, t, s):
                i = BT - 1 - t
                ps = s1_place(t)
                for c4 in range(-(-(i + 1) // 4)):
                    w_ = min(4, i + 1 - 4 * c4) * P
                    diag = c4 == i // 4
                    pe.matmul(ps[:, c4 * 512:c4 * 512 + w_], qT[s][:, i * P:(i + 1) * P],
                              kT[s][:, c4 * 512:c4 * 512 + w_], start=True, stop=not diag)
                    if diag:
                        ins = pe.matmul(ps[:, i * P:(i + 1) * P], g.identb[:, :], g.maskb[:, :],
                                        start=False, stop=True)
                ins.then_inc(s1_ready, 1)

            def max_rows(pe, half, s):
                for j in range(4):
                    i = (1 - half) * 4 + j
                    t = BT - 1 - i
                    ins = pe.matmul(misc[64:65, j * P:(j + 1) * P], negm[s % 2][:, t:t + 1], g.identh[:, :],
                                    start=True, stop=True)
                ins.then_inc(misc_ready, 1)

            @block.tensor
            def _(pe):
                pe.nop().then_inc(pv_ready, BT)
                for m in range(2):
                    for k in range(4):
                        if k == 0:
                            pe.wait_ge(w_in[m], 4)
                        if k in (1, 2):
                            pe.wait_ge(misc_dve, 2 * m + k)
                        elif k == 3 or m:
                            pe.wait_ge(misc_act, 2 * m + (1 if k == 3 else 0))
                        turn_chunk(pe, k, m)
                pe.wait_ge(misc_act, 4)
                pe.wait_ge(misc_dve, 4)
                for t in range(BT):
                    if t:
                        pe.wait_ge(m_ready, t if t < 5 else t - 1)
                    max_scores(pe, t, 0)
                for half in range(2):
                    pe.wait_ge(m_ready, 4 + 4 * half)
                    if half:
                        pe.wait_ge(misc_act, 5)
                    max_rows(pe, half, 0)
                max_scores(pe, 0, 1)

                def step(n, s, k, first):
                    def values(n, s, k):
                        pe.wait_ge(e_ready, n * BT + (BT + k + 1))
                        if k == 0:
                            pe.wait_ge(v_in, n + 1)
                            pe.wait_ge(zt_out, n + 1)
                        for q in range(k // 2, CH):
                            lo = max(k * P, q * QW)
                            hi = (q + 1) * QW
                            ins = pe.matmul(zT[VW * q:VW * (q + 1), lo - q * QW:hi - q * QW], vh[s][:, k, :],
                                            pT[k % 4][:, lo - k * P:hi - k * P], start=(k == 0),
                                            stop=(k == min(2 * q + 1, BT - 1)), skip_group_check=True)
                        ins.then_inc(pv_ready, 1)

                    if k == 0:
                        pe.wait_ge(misc_act, n * 4 + PRO_ACT)
                    pe.wait_ge(e_ready, n * BT + (BT + k - 1))
                    width = (BT - k) * P
                    for c4 in range(-(-width // 512)):
                        w_ = min(512, width - c4 * 512)
                        ins = pe.matmul(ST[k % 2][:, c4 * 512:c4 * 512 + w_], kT[s][:, k * P:(k + 1) * P],
                                        qT[s][:, k * P + c4 * 512:k * P + c4 * 512 + w_],
                                        start=True, stop=c4 > 0)
                        if c4 == 0:
                            ins = pe.matmul(ST[k % 2][:, 0:P], g.maskb[:, :], g.identb[:, :],
                                            start=False, stop=True)
                    ins.then_inc(st_ready, 1)
                    for ahead, t in s1_steps[k]:
                        if t == 0:
                            pe.wait_ge(misc_act, n * 4 + (PRO_ACT + 2))
                            pe.wait_ge(misc_dve, n * 3 + (PRO_DVE + 2))
                        pe.wait_ge(m_ready, (n + ahead) * BT + (t if t < 5 else t - 1))
                        max_scores(pe, t, (s + ahead) % 4)
                    if k < 4:
                        if k == 0:
                            pe.wait_ge(w_in[s % 2], n * 2 + (8 - 2 * (s % 2)))
                        elif k < 3:
                            pe.wait_ge(misc_dve, n * 3 + (PRO_DVE + k))
                        else:
                            pe.wait_ge(misc_act, n * 4 + (PRO_ACT + 1))
                        turn_chunk(pe, k, s)
                    if k == 4:
                        pe.wait_ge(misc_act, n * 4 + (PRO_ACT + 2))
                        pe.wait_ge(zt_out, n + 1)
                        for half in range(2):
                            ins = pe.transpose(misc[:, half * P:(half + 1) * P],
                                               zts[(s + 1) % 2][:, half * P:(half + 1) * P], g.identf[:, :])
                        ins.then_inc(misc_ready, 1)
                    if k == 5:
                        pe.wait_ge(misc_dve, n * 3 + (PRO_DVE + 3))
                        pe.wait_ge(m_ready, n * BT + (BT + 4))
                        max_rows(pe, 0, s + 1)
                    if k == 6:
                        pe.wait_ge(misc_act, n * 4 + (PRO_ACT + 3))
                        pe.wait_ge(m_ready, n * BT + (BT + 8))
                        max_rows(pe, 1, s + 1)
                    if k >= 2:
                        values(n, s, k - 2)
                    elif not first:
                        values(n - 1, (s - 1) % 4, BT - 2 + k)
                all_steps(pe, step)
                pe.wait_ge(zt_out, NH + 1)
                pe.wait_ge(misc_dve, PRO_DVE + 3 * NH + 2)
                for half in range(2):
                    ins = pe.transpose(misc[:, half * P:(half + 1) * P],
                                       zts[1][:, half * P:(half + 1) * P], g.identf[:, :])
                ins.then_inc(misc_ready, 1)

            def chunk_out(eng, k, s, is_act):
                dst = (qT if k < 2 else kT)[s][:, (k % 2) * 512:(k % 2 + 1) * 512]
                if is_act:
                    return eng.activation(dst, misc[0:R, :], ACT.Copy)
                return eng.tensor_copy(dst, misc[0:R, :])

            def rows_out(act, half, s):
                cols = slice(512, 1024) if half == 0 else slice(0, 512)
                return act.activation(qT[s][64:65, cols], misc[64:65, :], ACT.Copy)

            @block.scalar
            def _(act):
                act.nop().then_inc(e_ready, BT)
                for m in range(2):
                    for k in (2, 3):
                        act.wait_ge(misc_ready, 4 * m + k + 1)
                        chunk_out(act, k, m, True).then_inc(misc_act, 1)
                for half in range(2):
                    act.wait_ge(misc_ready, 9 + half)
                    rows_out(act, half, 0).then_inc(misc_act, 1)

                def step(n, s, k, first):
                    act.wait_ge(st_ready, n * BT + (k + 1))
                    act.wait_ge(pv_ready, n * BT + (BT + k - 3))
                    width = (BT - k) * P
                    act.activation(pT[k % 4][:, 0:width], ST[k % 2][:, 0:width], ACT.Exp).then_inc(e_ready, 1)
                    if k in (2, 3):
                        act.wait_ge(misc_ready, n * 7 + (PRO_MISC + P0 + k + 1))
                        chunk_out(act, k, (s + 2) % 4, True).then_inc(misc_act, 1)
                    if k in (5, 6):
                        act.wait_ge(misc_ready, n * 7 + (PRO_MISC + (MA if k == 5 else MB) + 1))
                        rows_out(act, 0 if k == 5 else 1, (s + 1) % 4).then_inc(misc_act, 1)
                all_steps(act, step)

            @block.vector
            def _(dve):
                def maximum(t, s, count):
                    dve.wait_ge(s1_ready, count)
                    dve.tensor_reduce(negm[s % 2][:, t:t + 1], s1_place(t), AX.X, ALU.max,
                                      negate=True).then_inc(m_ready, 1)

                def z_out(n, count):
                    dve.wait_ge(misc_ready, count)
                    zv = misc[:, 0:2 * P].rearrange("p (a q v) -> p a q v", a=2, v=VW)
                    dve.reciprocal(rinv[:, :, :], zv[:, :, :, DH0]).then_inc(s_inv, 1)
                    dve.wait_ge(s_inv, n + 1)
                    dst = g.zl[:, ds(n, 1), :].rearrange("p o (q a d) -> p (o a) q d", q=CH, a=2)
                    dve.tensor_tensor(dst, zv[:, :, :, 0:DH0],
                                      rinv[:, :, :].unsqueeze(3).to_broadcast([P, 2, CH, DH0]),
                                      ALU.mult).then_inc(misc_dve, 1)

                for m in range(2):
                    for k in range(2):
                        dve.wait_ge(misc_ready, 4 * m + k + 1)
                        chunk_out(dve, k, m, False).then_inc(misc_dve, 1)
                for t in range(BT):
                    maximum(t, 0, t + 1)
                maximum(0, 1, BT + 1)

                def step(n, s, k, first):
                    for ahead, t in s1_steps[k]:
                        maximum(t, s + ahead, (n + ahead) * BT + (t + 1))
                    if k < 2:
                        dve.wait_ge(misc_ready, n * 7 + (PRO_MISC + P0 + k + 1))
                        chunk_out(dve, k, (s + 2) % 4, False).then_inc(misc_dve, 1)
                    if k == 4:
                        z_out(n, n * 7 + (PRO_MISC + ZT + 1))
                    if k == 1 and not first:
                        dve.wait_ge(pv_ready, n * BT + BT)
                        dve.tensor_copy(zts[(s - 1) % 2][:, :], zT).then_inc(zt_out, 1)
                all_steps(dve, step)
                z_out(NH, PRO_MISC + 7 * NH + 3)

            @block.sync
            def _(sp):
                zv = g.krows.rearrange("(z p n) d -> z p (n d)", p=P, z=ZD)
                for z in range(ZD):
                    sp.dma_start(zv[z], g.zero[:, :]).then_inc(g.s_zero, 16)


WS = 4


def l1_fetch(g, sp, N0):
    w_split, w_in = g.sem("a1_w_split"), [g.sem(f"a1_w{i}") for i in range(2)]

    def fetch(h, par):
        if not isinstance(h, int) or N0 + h >= 2:
            sp.wait_ge(w_split, h * WS + (N0 - 1) * WS)
        if isinstance(h, int):
            h = h % H
        sp.dma_start(g.wh[par][:, :, :], g.t["wqkv1"][ds(h, 1), :, :, :].rearrange(
            "o p c n -> (o p) c n")).then_inc(w_in[par], 16)
    return fetch


def l1_split(g, pool, N0):
    w_split, w_in, s_ready = g.sem("a1_w_split"), [g.sem(f"a1_w{i}") for i in range(2)], g.sem("a1_scores")
    zeros = g.zero[:, 0:DC * 3 * P].rearrange("p (c n) -> p c n", c=DC)

    def split(h, par):
        if not isinstance(h, int) or N0 + h >= 2:
            pool.wait_ge(s_ready, h * BT + ((N0 - 2) * BT + 1))
        pool.wait_ge(w_in[par], h * 8 + (N0 * 8 + 16 - 8 * par))
        w = g.wh[par]
        pool.tensor_tensor(w[:, :, :], w[:, :, :], g.wscale[:, :, :], ALU.mult).then_inc(w_split, 1)
        pool.wait_ge(w_split, h * WS + (N0 * WS + 1))
        pool.tensor_tensor(g.wsplit[par][0][:, :, :], w[:, :, :], zeros, ALU.add).then_inc(w_split, 1)
        hb = h % H if isinstance(h, int) else h
        pool.tensor_tensor(g.bias[par][:, :], g.bqk[:, ds(hb, 1), :].rearrange("p o q -> p (o q)"),
                           g.bscale[:, :], ALU.mult).then_inc(w_split, 1)
        pool.wait_ge(w_split, h * WS + (N0 * WS + 3))
        pool.tensor_tensor(g.wsplit[par][1][:, :, :], w[:, :, :], g.wsplit[par][0][:, :, :],
                           ALU.subtract).then_inc(w_split, 1)
    return split


def l1_attention(nc, g, b):
    AHEAD = {0: 0, 2: 1, 4: 2, 5: 3, 6: 4, 7: 5}
    NCH = len(AHEAD)
    GU = BT + NCH
    blocks = [BT - j for j in range(BT)]
    chunks = [-(-n // 4) for n in blocks]
    first = [sum(chunks[:j]) for j in range(BT + 1)]
    TC = first[BT]
    s_ready, m_ready, e_ready, r_ready, t_ready, g_ready, hi_ready, w_split = \
        [g.sem(f"a1_{n}") for n in ("scores", "max", "exp", "inv", "turned", "g_ready", "hi_ready", "w_split")]
    g_free = [g.sem("a1_g_even_free"), g.sem("a1_g_odd_free")]
    s_wo = g.sem("a1_wo_hi")
    t_hi, t_lo = g.sem("a1_turned_hi"), g.sem("a1_turned_lo")
    w_in = [g.sem(f"a1_w{i}") for i in range(2)]
    N0 = b * H
    PE_ORDER = ("scores", "turn", "ahead", "values")
    ACT_ORDER = ("turn", "ahead", "scores", "values")
    DVE_ORDER = ("scores", "turn", "ahead", "values")

    def body_items(which, order):
        items, use = [], 6 if which == "first" else 4
        for j in range(BT + (2 if which == "last" else 0)):
            step = {}
            if j < BT:
                step["scores"] = ("scores", j, False, None)
            if j <= BT and (j >= 1 or which != "first"):
                step["turn"] = ("turn", (j - 1) % BT, j == 0, None)
            if j in AHEAD and which != "last":
                step["ahead"] = ("ahead", AHEAD[j], False, use)
                use += 1
            if j >= 2 or which != "first":
                step["values"] = ("values", (j - 2) % BT, j < 2, use)
                use += 1
            items += [step[kind] for kind in order if kind in step]
        return items

    def back_use(which, j, before):
        if before:
            return [it[3] for it in body_items("mid", PE_ORDER) if it[:3] == ("values", j - 2, False)][0] - GU
        return [it[3] for it in body_items(which, PE_ORDER) if it[:3] == ("values", (j - 2) % BT, j < 2)][0]

    def all_heads(eng, head):
        head(eng, N0, 0, "first")
        with eng.Fori(0, H // 2 - 1) as pair:
            head(eng, pair * 2 + (N0 + 1), 1, "mid")
            head(eng, pair * 2 + (N0 + 2), 0, "mid")
        head(eng, N0 + H - 1, 1, "last")

    with ExitStack() as c:
        probs = [g.sb(f"a1{b}_p{i}", [P, S], F32, c) for i in range(2)]
        turned = [[g.sb(f"a1{b}_pt{i}{a}", [P, S], F16, c) for a in range(2)] for i in range(2)]
        qT = [[g.sb(f"a1{b}_q{i}{a}", [P, S], F16, c) for a in range(2)] for i in range(2)]
        kT = [[g.sb(f"a1{b}_k{i}{a}", [P, S], F16, c) for a in range(2)] for i in range(2)]
        negm = g.sb(f"a1{b}_negm", [P, 2, BT], F32, c)
        rsum = g.sb(f"a1{b}_rsum", [P, 2, BT], F32, c)
        rinv = g.sb(f"a1{b}_rinv", [P, 2, BT], F32, c)
        S_ps = [g.bank[0], g.bank[1]]
        T_ps = [g.bank[2][:, 0, :], g.bank[2][:, 1, :]]
        G_ps = [g.bank[3][:, 0, :], g.bank[3][:, 1, :]]
        PARTS = [(0, 0), (0, 1), (1, 0)]

        def prep_pe(pe, k, par, ps):
            w = g.wsplit[par]
            if k < 4:
                for c_ in range(DC):
                    for a, x_ in PARTS:
                        ins = pe.matmul(ps, w[a][:, c_, (k // 2) * P:(k // 2 + 1) * P],
                                        g.xs[x_][:, c_, b * S + (k % 2) * 512:b * S + (k % 2 + 1) * 512],
                                        start=(c_ == 0 and (a, x_) == PARTS[0]),
                                        stop=(c_ == DC - 1 and (a, x_) == PARTS[-1]))
            else:
                for j in range(4):
                    t = b * BT + (k - 4) * 4 + j
                    for c_ in range(DC):
                        for a, x_ in PARTS:
                            ins = pe.matmul(ps[:, j * P:(j + 1) * P], g.xs[x_][:, c_, t * P:(t + 1) * P],
                                            w[a][:, c_, 2 * P:3 * P],
                                            start=(c_ == 0 and (a, x_) == PARTS[0]),
                                            stop=(c_ == DC - 1 and (a, x_) == PARTS[-1]))
            return ins

        def prep_dst(k, par, part):
            if k < 4:
                return (qT if k < 2 else kT)[par][part][:, (k % 2) * 512:(k % 2 + 1) * 512]
            return g.vs[par][part][:, (k - 4) * 4:(k - 3) * 4, :].rearrange("p t d -> p (t d)")

        def prep_hi(act, k, par, ps):
            if k < 4:
                act.activation(prep_dst(k, par, 0), ps, ACT.Identity, bias=g.bias[par][:, k // 2:k // 2 + 1]
                               ).then_inc(hi_ready, 1)
            else:
                act.activation(prep_dst(k, par, 0), ps, ACT.Copy).then_inc(hi_ready, 1)

        def prep_lo(dve, k, par, ps, n, use):
            dve.wait_ge(hi_ready, n * NCH + (k + 1))
            if k < 4:
                ins = dve.scalar_tensor_tensor(prep_dst(k, par, 1), ps, g.bias[par][:, k // 2:k // 2 + 1],
                                               prep_dst(k, par, 0), ALU.add, ALU.subtract)
            else:
                ins = dve.tensor_tensor(prep_dst(k, par, 1), ps, prep_dst(k, par, 0), ALU.subtract)
            ins.then_inc(g_free[use % 2], 1)

        with nc.Block() as block:
            @block.sync
            def _(sp):
                fetch = l1_fetch(g, sp, N0)
                with sp.Fori(1, H // 2) as pair:
                    fetch(pair * 2, 0)
                    fetch(pair * 2 + 1, 1)
                if b + 1 < B:
                    fetch(H, 0)
                    fetch(H + 1, 1)

            @block.gpsimd
            def _(pool):
                if b == 0:
                    pool.tensor_copy(g.wo1p[0][:, :, :], g.wo1[:, :, :]).then_inc(s_wo, 1)
                    pool.wait_ge(s_wo, 1)
                    pool.tensor_tensor(g.wo1p[1][:, :, :], g.wo1[:, :, :], g.wo1p[0][:, :, :], ALU.subtract)
                split = l1_split(g, pool, N0)
                with pool.Fori(1, H // 2) as pair:
                    split(pair * 2, 0)
                    split(pair * 2 + 1, 1)
                if b + 1 < B:
                    split(H, 0)
                    split(H + 1, 1)

            @block.tensor
            def _(pe):
                pe.wait_ge(w_split, N0 * WS + WS)
                for k in range(NCH):
                    if k >= 2:
                        pe.wait_ge(g_free[k % 2], N0 * GU // 2 + k // 2)
                    prep_pe(pe, k, 0, G_ps[k % 2]).then_inc(g_ready, 1)
                pe.wait_ge(g_free[0], N0 * GU // 2 + NCH // 2)
                pe.wait_ge(g_free[1], N0 * GU // 2 + NCH // 2)

                def head(eng, n, par, which):
                    start = which == "first" and b == 0
                    for kind, j, before, u in body_items(which, PE_ORDER):
                        p_ = 1 - par if before else par
                        if kind == "scores":
                            nb, i = blocks[j], blocks[j] - 1
                            if j == 0 and which != "first":
                                eng.wait_ge(g_free[0], n * (GU // 2))
                            if not (start and j < 2):
                                eng.wait_ge(e_ready, n * BT + (j - 1))
                            ps = S_ps[j % 2]
                            for c4 in range(-(-nb // 4)):
                                w_ = min(4, nb - 4 * c4) * P
                                diag = c4 == i // 4
                                for a, k_ in PARTS:
                                    ins = eng.matmul(ps[:, c4, 0:w_], qT[par][a][:, i * P:(i + 1) * P],
                                                     kT[par][k_][:, c4 * 512:c4 * 512 + w_],
                                                     start=(a, k_) == PARTS[0],
                                                     stop=(a, k_) == PARTS[-1] and not diag)
                                if diag:
                                    o = (i % 4) * P
                                    ins = eng.matmul(ps[:, c4, o:o + P], g.identb[:, :], g.maskb[:, :],
                                                     start=False, stop=True)
                            ins.then_inc(s_ready, 1)
                        elif kind == "turn":
                            nn = n - 1 if before else n
                            eng.wait_ge(e_ready, nn * BT + (j + 1))
                            for k in range(chunks[j]):
                                ch = first[j] + k
                                if not (start and ch < 2):
                                    eng.wait_ge(t_lo, nn * TC + (ch - 1))
                                for q in range(4 * k, min(4 * k + 4, blocks[j])):
                                    ins = eng.transpose(T_ps[ch % 2][:, (q % 4) * P:(q % 4 + 1) * P],
                                                        probs[j % 2][:, q * P:(q + 1) * P], g.identf[:, :])
                                ins.then_inc(t_ready, 1)
                        elif kind == "values":
                            nn = n - 1 if before else n
                            eng.wait_ge(t_lo, nn * TC + first[j + 1])
                            eng.wait_ge(g_free[u % 2], n * (GU // 2) + u // 2)
                            for q in range(blocks[j]):
                                for a, v_ in PARTS:
                                    ins = eng.matmul(G_ps[u % 2][:, 0:DH1], turned[j % 2][a][:, q * P:(q + 1) * P],
                                                     g.vs[p_][v_][:, q, :], start=(q == 0 and (a, v_) == PARTS[0]),
                                                     stop=(q == blocks[j] - 1 and (a, v_) == PARTS[-1]))
                            ins.then_inc(g_ready, 1)
                        else:
                            if j == 0:
                                eng.wait_ge(w_split, n * WS + 2 * WS)
                            eng.wait_ge(g_free[u % 2], n * (GU // 2) + u // 2)
                            prep_pe(eng, j, 1 - par, G_ps[u % 2]).then_inc(g_ready, 1)
                all_heads(pe, head)

            def turned_split(eng, is_act, n, j, before, which):
                nn = n - 1 if before else n
                for k in range(chunks[j]):
                    ch = first[j] + k
                    w_ = min(4, blocks[j] - 4 * k) * P
                    cols = slice(k * 512, k * 512 + w_)
                    src = T_ps[ch % 2][:, 0:w_]
                    if is_act:
                        if not (which == "first" and j < 2):
                            eng.wait_ge(g_ready, n * GU + back_use(which, j, before) + 1)
                        eng.wait_ge(t_ready, nn * TC + (ch + 1))
                        eng.activation(turned[j % 2][0][:, cols], src, ACT.Copy).then_inc(t_hi, 1)
                    else:
                        eng.wait_ge(t_hi, nn * TC + (ch + 1))
                        eng.tensor_tensor(turned[j % 2][1][:, cols], src, turned[j % 2][0][:, cols],
                                          ALU.subtract).then_inc(t_lo, 1)

            @block.scalar
            def _(act):
                for k in range(NCH):
                    act.wait_ge(g_ready, N0 * GU + k + 1)
                    prep_hi(act, k, 0, G_ps[k % 2])

                def head(eng, n, par, which):
                    for kind, j, before, u in body_items(which, ACT_ORDER):
                        if kind == "scores":
                            eng.wait_ge(m_ready, n * BT + (j + 1))
                            if j >= 2 or not (which == "first" and b == 0):
                                eng.wait_ge(t_ready, n * TC + (first[j - 1] if j >= 2 else j - 1))
                            w_ = blocks[j] * P
                            eng.activation(probs[j % 2][:, 0:w_],
                                           S_ps[j % 2].rearrange("p a n -> p (a n)")[:, 0:w_], ACT.Exp,
                                           bias=negm[:, par, j:j + 1],
                                           accum_out=rsum[:, par, j:j + 1]).then_inc(e_ready, 1)
                        elif kind == "turn":
                            turned_split(eng, True, n, j, before, which)
                        elif kind == "values":
                            nn = n - 1 if before else n
                            eng.wait_ge(g_ready, n * GU + (u + 1))
                            eng.wait_ge(r_ready, nn * BT + (j + 1))
                            p_ = 1 - par if before else par
                            eng.activation(g.z[:, blocks[j] - 1, ds(nn * DH1 - N0 * DH1, DH1)], G_ps[u % 2][:, 0:DH1],
                                           ACT.Copy, scale=rinv[:, p_, j:j + 1]).then_inc(g_free[u % 2], 1)
                        else:
                            eng.wait_ge(g_ready, n * GU + (u + 1))
                            prep_hi(eng, j, 1 - par, G_ps[u % 2])
                all_heads(act, head)

            @block.vector
            def _(dve):
                for k in range(NCH):
                    prep_lo(dve, k, 0, G_ps[k % 2], N0, k)

                def head(eng, n, par, which):
                    for kind, j, before, u in body_items(which, DVE_ORDER):
                        if kind == "scores":
                            eng.wait_ge(s_ready, n * BT + (j + 1))
                            w_ = blocks[j] * P
                            eng.tensor_reduce(negm[:, par, j:j + 1],
                                              S_ps[j % 2].rearrange("p a n -> p (a n)")[:, 0:w_],
                                              AX.X, ALU.max, negate=True).then_inc(m_ready, 1)
                        elif kind == "turn":
                            turned_split(eng, False, n, j, before, which)
                        elif kind == "values":
                            nn = n - 1 if before else n
                            p_ = 1 - par if before else par
                            eng.wait_ge(e_ready, nn * BT + (j + 1))
                            eng.reciprocal(rinv[:, p_, j:j + 1], rsum[:, p_, j:j + 1]).then_inc(r_ready, 1)
                        else:
                            prep_lo(eng, j, 1 - par, G_ps[u % 2], n + 1, u)
                all_heads(dve, head)


def proj_out(nc, g, tag, layer, b=0):
    NC = H if layer else DC
    GR = -(-NC // 4)
    tiles = list(range(BT)) if layer else list(range(NT))
    w = g.wo1p if layer else [g.wo0]
    PARTS = [(0, 0), (0, 1), (1, 0)] if layer else [(0, 0)]
    s_t, s_c, s_mm, s_add = [g.sem(f"{tag}_{n}") for n in ("turn", "copy", "mm", "add")]
    s_bo = g.sem(f"{tag}_bo") if layer else None
    N0 = b * BT
    s_z = None if layer else g.sem(f"{tag}_z")
    with ExitStack() as c:
        if not layer:
            g.z = g.sb("z0", [P, NT, D], F32, c)
        zT = [[g.sb(f"{tag}{b}_zT{i}{a}", [P, NC, P], F16 if layer else F32, c) for a in range(2 if layer else 1)]
              for i in range(2)]
        s_hi = g.sem(f"{tag}_hi") if layer else None
        with nc.Block() as block:
            @block.tensor
            def _(pe):
                def out(n, r):
                    if r == 0:
                        pe.wait_ge(s_c, (N0 + n + 1) * GR)
                        if n >= 2:
                            pe.wait_ge(s_add, N0 + n - 1)
                    for k in range(4 * r, min(4 * r + 4, NC)):
                        for a, w_ in PARTS:
                            ins = pe.matmul(g.bank[2 + n % 2][:, 0, 0:D], zT[n % 2][a][:, k, :], w[w_][:, k, :],
                                            start=(k == 0 and (a, w_) == PARTS[0]),
                                            stop=(k == NC - 1 and (a, w_) == PARTS[-1]))
                    if r == GR - 1:
                        ins.then_inc(s_mm, 1)

                for n, t in enumerate(tiles):
                    if not layer:
                        pe.wait_ge(s_z, n + 1)
                    for r in range(GR):
                        m = n * GR + r
                        if m >= 2:
                            pe.wait_ge(s_c, N0 * GR + m - 1)
                        for k in range(min(4, NC - 4 * r)):
                            ins = pe.transpose(g.bank[m % 2][:, 0, k * P:(k + 1) * P],
                                               g.z[:, t, (4 * r + k) * P:(4 * r + k + 1) * P], g.identf[:, :])
                        ins.then_inc(s_t, 1)
                        if n:
                            out(n - 1, r)
                for r in range(GR):
                    out(len(tiles) - 1, r)

            @block.vector
            def _(dve):
                def add(n):
                    t = b * BT + tiles[n] if layer else tiles[n]
                    dve.wait_ge(s_mm, N0 + n + 1)
                    if layer:
                        dve.wait_ge(s_bo, N0 + n + 1)
                    dve.tensor_tensor(g.x[:, t, :], g.bank[2 + n % 2][:, 0, 0:D], g.x[:, t, :],
                                      ALU.add).then_inc(s_add, 1)

                def row_stats(n):
                    t = b * BT + tiles[n] if layer else tiles[n]
                    dve.wait_ge(s_add, N0 + n + 1)
                    dve.bn_stats(g.stats[:, t, :], g.x[:, t, :])

                for n, t in enumerate(tiles):
                    for r in range(GR):
                        m = n * GR + r
                        nk = min(4, NC - 4 * r)
                        if not layer:
                            dve.wait_ge(s_t, m + 1)
                            if n >= 2:
                                dve.wait_ge(s_mm, n - 1)
                        part = [z_[:, 4 * r:4 * r + nk, :] for z_ in zT[n % 2]]
                        src = g.bank[m % 2][:, 0, 0:nk * P].rearrange("p (k q) -> p k q", k=nk)
                        if layer:
                            dve.wait_ge(s_hi, N0 * GR + m + 1)
                            for k in range(4):
                                ins = dve.scalar_tensor_tensor(part[1][:, k, :], src[:, k, :],
                                                               g.bv[:, 4 * r + k:4 * r + k + 1], part[0][:, k, :],
                                                               ALU.add, ALU.subtract)
                            ins.then_inc(s_c, 1)
                        else:
                            dve.tensor_copy(part[0], src).then_inc(s_c, 1)
                    if n:
                        add(n - 1)
                    if n >= 2:
                        row_stats(n - 2)
                add(len(tiles) - 1)
                row_stats(len(tiles) - 2)
                row_stats(len(tiles) - 1)

            if not layer:
                @block.scalar
                def _(act):
                    for t in tiles:
                        b0 = t // BT
                        src = g.zl[:, 1 + b0 * H:1 + (b0 + 1) * H, (t % BT) * DH0:(t % BT + 1) * DH0]
                        act.activation(g.z[:, t, :].rearrange("p (h d) -> p h d", d=DH0), src,
                                       ACT.Copy).then_inc(s_z, 1)

            if layer:
                @block.scalar
                def _(act):
                    for n in range(len(tiles)):
                        for r in range(GR):
                            m = n * GR + r
                            act.wait_ge(s_t, N0 * GR + m + 1)
                            if n >= 2:
                                act.wait_ge(s_mm, N0 + n - 1)
                            for k in range(4):
                                h = 4 * r + k
                                ins = act.activation(zT[n % 2][0][:, h, :], g.bank[m % 2][:, 0, k * P:(k + 1) * P],
                                                     ACT.Identity, bias=g.bv[:, h:h + 1])
                            ins.then_inc(s_hi, 1)

                @block.gpsimd
                def _(pool):
                    for n, t in enumerate(tiles):
                        pool.tensor_tensor(g.x[:, b * BT + t, :], g.x[:, b * BT + t, :], g.bo[:, :],
                                           ALU.add).then_inc(s_bo, 1)


def l0_ffn(nc, g):
    s_mm, s_bt, s_add = [g.sem(f"f0_{n}") for n in ("mm", "beta", "add")]
    with nc.Block() as block:
        @block.tensor
        def _(pe):
            for t in range(NT):
                if t >= 4:
                    pe.wait_ge(s_add, t - 3)
                for c_ in range(DC):
                    ins = pe.matmul(g.bank[t % 4][:, 0, 0:D], g.xT[:, c_, t * P:(t + 1) * P], g.wf[:, c_, :],
                                    start=(c_ == 0), stop=(c_ == DC - 1))
                ins.then_inc(s_mm, 1)

        @block.gpsimd
        def _(pool):
            for t in range(NT):
                pool.tensor_tensor(g.x[:, t, :], g.x[:, t, :], g.beta[:, :], ALU.add).then_inc(s_bt, 1)

        @block.vector
        def _(dve):
            for t in range(NT):
                dve.wait_ge(s_mm, t + 1)
                dve.wait_ge(s_bt, t + 1)
                dve.tensor_tensor(g.x[:, t, :], g.bank[t % 4][:, 0, 0:D], g.x[:, t, :], ALU.add).then_inc(s_add, 1)
                if t:
                    dve.wait_ge(s_add, t)
                    dve.bn_stats(g.stats[:, t - 1, :], g.x[:, t - 1, :])
            dve.wait_ge(s_add, NT)
            dve.bn_stats(g.stats[:, NT - 1, :], g.x[:, NT - 1, :])


def l1_buffers(nc, g, c2):
    g.wh = [g.sb(f"wh{i}", [P, DC, 3 * P], F32, c2) for i in range(2)]
    g.wsplit = [[g.sb(f"wsplit{i}{a}", [P, DC, 3 * P], F16, c2) for a in range(2)] for i in range(2)]
    g.xs = [g.sb(f"x_part{a}", [P, DC, T], F16, c2) for a in range(2)]
    g.vs = [[g.sb(f"v_part{i}{a}", [P, BT, P], F16, c2) for a in range(2)] for i in range(2)]
    g.z = g.sb("z1", [P, BT, H * DH1], F32, c2)
    g.wo1 = g.sb("wo1", [P, H, D], F32, c2)
    g.wo1p = [g.sb(f"wo1_part{a}", [P, H, D], F16, c2) for a in range(2)]
    g.bqk = g.sb("bqk1", [P, H, 2], F32, c2)
    g.bv = g.sb("bv1", [P, H], F32, c2)
    g.bias = [g.sb(f"bias{i}", [P, 2], F32, c2) for i in range(2)]
    g.wscale = g.sb("wscale", [P, DC, 3 * P], F32, c2)
    g.bscale = g.sb("bscale", [P, 2], F32, c2)
    g.bo = g.sb("bo1", [P, D], F32, c2)
    s_in, s_wo, s_set = g.sem("l1_in"), g.sem("l1_wo"), g.sem("l1_set")

    def loads(sp):
        sp.dma_start(g.bqk[:, :, :], g.t["b_QK"]).then_inc(s_in, 16)
        sp.dma_start(g.bv[:, :], g.t["b_V"]).then_inc(s_in, 16)
        sp.dma_start(g.bo[:, :], g.t["b_O"].partition_broadcast(P)).then_inc(s_in, 16)
        fetch = l1_fetch(g, sp, 0)
        fetch(0, 0)
        fetch(1, 1)
        sp.dma_start(g.wo1[:, :, :], g.t["wo1"]).then_inc(s_wo, 16)
        sp.wait_ge(s_wo, 16)

    def scales(pool):
        pool.memset(g.wscale[:, :, 0:P], float(DH1) ** -0.5).then_inc(s_set, 1)
        pool.memset(g.wscale[:, :, P:3 * P], 1.0).then_inc(s_set, 1)
        pool.memset(g.bscale[:, 0:1], float(DH1) ** -0.5).then_inc(s_set, 1)
        pool.memset(g.bscale[:, 1:2], 1.0).then_inc(s_set, 1)
        pool.wait_ge(s_set, 4)
        pool.wait_ge(s_in, 48)
        split = l1_split(g, pool, 0)
        split(0, 0)
        split(1, 1)
    return loads, scales


XB = 8
XG = 4


def moe(nc, g, out):
    with ExitStack() as c:
        g.xT = g.sb("xT1", [P, DC, T], F32, c)
        g.wk = g.sb("wk", [P, NT, 8], F32, c)
        g.src = g.sb("src", [C, E], U32, c)
        g.dst = g.sb("dst", [C, E], U32, c)
        g.wovT = g.sb("wovT", [E, T], F32, c)
        with ExitStack() as c1:
            g.xn = g.sb("xn", [P, NT, D], F32, c)
            norm(nc, g, "n3", "keep")
        with ExitStack() as c2:
            g.wgu = [g.sb(f"wgu{i}", [P, DC, 2 * M], F32, c2) for i in range(XB)]
            g.wd = [g.sb(f"wd{i}", [MH, 2, D], F32, c2) for i in range(XB)]
            with ExitStack() as c3:
                router(nc, g, c3)
            experts(nc, g, c2)
        with ExitStack() as c4:
            combine(nc, g, c4, out)


def router(nc, g, c):
    gate = g.sb("gate", [P, DC, E], F32, c)
    sgu = g.sb("sgu", [P, DC, 2 * MS], F32, c)
    sd = g.sb("sd", [P, NMS, D], F32, c)
    before = g.sb("before", [P, P], F32, c)
    beforeb = g.sb("beforeb", [P, P], BF16, c)
    onesb = g.sb("onesb", [P, P], BF16, c)
    iota = g.sb("iota", [P, C], F32, c)
    token = g.sb("token", [P, NT], F32, c)
    last = g.sb("last", [P, 1], F32, c)
    ph = [g.sb(f"at_slot{i}", [P, NT, C], F16, c) for i in range(2)]
    eh = [g.sb(f"at_expert{i}", [P, NT, 2, E], F16, c) for i in range(2)]
    dtmp = g.sb("d_tmp", [C, 2, E], F32, c)
    sc = g.sb("scores", [P, NT, E], F32, c)
    msc = g.sb("masked_scores", [P, NT, E], F32, c)
    tmp = g.sb("r_tmp", [P, NT, E], F32, c)
    slot = g.sb("slot", [P, NT, E], F32, c)
    oh = g.sb("onehot", [P, K, NT, E], BF16, c)
    mask = g.sb("mask", [P, NT, E], BF16, c)
    cm = g.sb("cumulated", [P, NT + 1, E], BF16, c)
    small = g.sb("r_small", [P, 4, NT], F32, c)
    gmx = g.sb("gmx", [P, NT, NG], F32, c)
    g8 = g.sb("g8", [P, NT, 8], F32, c)
    gi = g.sb("gi", [P, NT, 8], U32, c)
    gif = g.sb("gif", [P, NT, 8], F32, c)
    gmask = g.sb("gmask", [P, 2, NT, NG], F32, c)
    cnt = g.sb("cnt", [P, E], F32, c)
    v = g.sb("v", [P, K, NT], F32, c)
    hT = g.sb("shared_h", [P, NMS, T], F32, c)
    sg = [g.sb(f"shared_g{i}", [P, 512], F32, c) for i in range(2)]
    s_in, s_ch, s_lg, s_ex, s_m, s_pos, s_w = [g.sem(f"r_{n}") for n in
                                              ("in", "chain", "logits", "exp", "mask", "pos", "weights")]
    s_gu, s_sil, s_h, s_dn, s_add = [g.sem(f"r_{n}") for n in ("gu", "silu", "h", "down", "add")]
    s_oh, s_eh, s_ph, s_used, s_sel, s_wov, s_wt, s_we = [g.sem(f"r_{n}") for n in
                                                         ("onehot", "at_expert", "at_slot", "used", "selected",
                                                          "wov", "wov_turned", "wov_evac")]
    g.s_wgu = [g.sem(f"x_wgu{i}") for i in range(XB)]
    picked = g.bank[0][0:C, 1, 0:2 * E].rearrange("p (a e) -> p a e", a=2)
    logits = g.bank[0].rearrange("p a n -> p (a n)").rearrange("p (t e) -> p t e", e=E)
    pos = g.bank[1].rearrange("p a n -> p (a n)").rearrange("p (t e) -> p t e", e=E)
    count = g.bank[0][:, 0, 0:E]
    NQ = T // 512

    def down_bank(t):
        return g.bank[2 + t % 2][:, t // 2 % 2, 0:D]

    with nc.Block() as block:
        @block.sync
        def _(sp):
            for dst, name in ((gate, "gate"), ):
                sp.dma_start(dst[:, :, :], g.t[name].rearrange("(c p) n -> p c n", p=P)).then_inc(s_in, 16)
            sp.dma_start(before[:, :], g.t["c_before"]).then_inc(s_in, 16)
            sp.dma_start(iota[:, :], g.t["c_iota"]).then_inc(s_in, 16)
            sp.dma_start(token[:, :], g.t["c_token"]).then_inc(s_in, 16)
            sp.dma_start(last[:, :], g.t["c_last"]).then_inc(s_in, 16)
            sp.dma_start(sgu[:, :, :], g.t["sgu"]).then_inc(s_w, 16)
            for i, (m, w_) in enumerate(SM):
                sp.dma_start(sd[0:w_, i, :], g.t["sd"][m:m + w_, :]).then_inc(s_w, 16)
            for e in range(XB):
                sp.dma_start(g.wgu[e][:, :, :], g.t["wgu"][e]).then_inc(g.s_wgu[e], 16)
                sp.dma_start(g.wd[e][:, :, :], g.t["wd"][e]).then_inc(g.s_wgu[e], 16)

        gu_steps = [(q, m) for q in range(NQ) for m in range(NMS)]

        @block.tensor
        def _(pe):
            pe.wait_ge(s_in, 80)
            for t in range(NT):
                for c_ in range(DC):
                    ins = pe.matmul(logits[:, t, :], g.xT[:, c_, t * P:(t + 1) * P], gate[:, c_, :],
                                    start=(c_ == 0), stop=(c_ == DC - 1))
            ins.then_inc(s_lg, 1)
            pe.wait_ge(s_w, 16 + 16 * NMS)

            def gate_up(n):
                q, m = gu_steps[n]
                m0, w_ = SM[m]
                if n >= 2:
                    pe.wait_ge(s_h, n - 1)
                for half in range(2):
                    for c_ in range(DC):
                        ins = pe.matmul(g.bank[2 + half][0:w_, n % 2, :],
                                        sgu[:, c_, half * MS + m0:half * MS + m0 + w_],
                                        g.xT[:, c_, q * 512:(q + 1) * 512],
                                        start=(c_ == 0), stop=(c_ == DC - 1))
                ins.then_inc(s_gu, 1)

            for n in range(len(gu_steps)):
                gate_up(n)
            pe.wait_ge(s_m, 1)
            for half in range(2):
                pe.matmul(g.bank[1][:, half, :], beforeb[:, :],
                          mask[:, half * 8:half * 8 + 8, :].rearrange("p t e -> p (t e)"), start=True, stop=False)
                pe.matmul(g.bank[1][:, half, :], onesb[:, :],
                          cm[:, half * 8:half * 8 + 8, :].rearrange("p t e -> p (t e)"), start=False, stop=True)
            pe.matmul(count, onesb[:, :], cm[:, NT, :], start=True, stop=True).then_inc(s_pos, 1)
            def shared_down(t):
                if t == 0:
                    pe.wait_ge(s_h, len(gu_steps))
                if t >= 4:
                    pe.wait_ge(s_add, t - 3)
                for m in range(NMS):
                    w_ = SM[m][1]
                    ins = pe.matmul(down_bank(t), hT[0:w_, m, t * P:(t + 1) * P], sd[0:w_, m, :],
                                    start=(m == 0), stop=(m == NMS - 1))
                ins.then_inc(s_dn, 1)

            shared_down(0)
            shared_down(1)
            pe.wait_ge(s_wov, 1)
            for q in range(NQ):
                if q >= 2:
                    pe.wait_ge(s_we, q - 1)
                for j in range(4):
                    ins = pe.transpose(g.bank[2 + q % 2][0:E, 1, j * P:(j + 1) * P], msc[:, 4 * q + j, :],
                                       g.identf[:, :])
                ins.then_inc(s_wt, 1)
            for k in range(K):
                if k == 0:
                    pe.wait_ge(s_we, NQ)
                shared_down(2 * k + 2)
                shared_down(2 * k + 3)
                pe.wait_ge(s_eh, 2 * k + 2)
                pe.wait_ge(s_ph, k + 1)
                for t in range(NT):
                    ins = pe.matmul(g.bank[0][0:C, 1, 0:2 * E], ph[k % 2][:, t, :],
                                    eh[k % 2][:, t, :, :].rearrange("p a e -> p (a e)"),
                                    start=(k == 0 and t == 0), stop=(k == K - 1 and t == NT - 1))
                ins.then_inc(s_used, 1)
            for t in range(2 * K + 2, NT):
                shared_down(t)

        @block.scalar
        def _(act):
            act.wait_ge(s_ex, 1)
            act.activation(sc[:, :, :], tmp[:, :, :], ACT.Exp).then_inc(s_ex, 1)
            for n in range(len(gu_steps)):
                act.wait_ge(s_gu, n + 1)
                if n >= 2:
                    act.wait_ge(s_h, n - 1)
                w_ = SM[gu_steps[n][1]][1]
                act.activation(sg[n % 2][0:w_, :], g.bank[2][0:w_, n % 2, :], ACT.Silu).then_inc(s_sil, 1)
            for q in range(NQ):
                act.wait_ge(s_wt, q + 1)
                act.activation(g.wovT[:, q * 512:(q + 1) * 512], g.bank[2 + q % 2][0:E, 1, :],
                               ACT.Copy).then_inc(s_we, 1)

        @block.vector
        def _(dve):
            n = 0

            def chained(ins):
                nonlocal n
                n += 1
                ins.then_inc(s_ch, 1)
                dve.wait_ge(s_ch, n)

            def shared_sum(t):
                dve.wait_ge(s_dn, t + 1)
                dve.tensor_tensor(g.x[:, t, :], down_bank(t), g.x[:, t, :], ALU.add).then_inc(s_add, 1)

            done = 0

            def shared(upto):
                nonlocal done
                while done < upto:
                    q, m = gu_steps[done]
                    dve.wait_ge(s_sil, done + 1)
                    w_ = SM[m][1]
                    dve.tensor_tensor(hT[0:w_, m, q * 512:(q + 1) * 512], g.bank[3][0:w_, done % 2, :],
                                      sg[done % 2][0:w_, :], ALU.mult).then_inc(s_h, 1)
                    done += 1

            dve.wait_ge(s_in, 80)
            chained(dve.tensor_copy(beforeb[:, :], before[:, :]))
            chained(dve.memset(onesb[:, :], 1.0))
            chained(dve.memset(cm[:, 0, :], 0.0))
            dve.wait_ge(s_lg, 1)
            mx, rs = small[:, 0, :], small[:, 1, :]
            chained(dve.tensor_reduce(mx, logits, AX.X, ALU.max))
            dve.tensor_tensor(tmp[:, :, :], logits, mx.unsqueeze(2).to_broadcast([P, NT, E]),
                              ALU.subtract).then_inc(s_ex, 1)
            dve.wait_ge(s_ex, 2)
            chained(dve.tensor_reduce(rs, sc[:, :, :], AX.X, ALU.add))
            chained(dve.reciprocal(rs, rs))
            chained(dve.tensor_tensor(sc[:, :, :], sc[:, :, :], rs.unsqueeze(2).to_broadcast([P, NT, E]), ALU.mult))
            shared(2)
            chained(dve.tensor_reduce(gmx[:, :, :], sc.rearrange("p t (a b) -> p t a b", b=GS), AX.X, ALU.max))
            for t in range(NT):
                ins = dve.max(g8[:, t, :], gmx[:, t, :])
            chained(ins)
            for t in range(NT):
                ins = dve.max_index(gi[:, t, :], g8[:, t, :], gmx[:, t, :])
            chained(ins)
            chained(dve.tensor_copy(gif[:, :, :], gi[:, :, :]))
            gid = iota[:, 0:NG].unsqueeze(1).to_broadcast([P, NT, NG])
            for k in range(TG):
                chained(dve.tensor_tensor(gmask[:, min(k, 1)], gid, gif[:, :, k:k + 1].to_broadcast([P, NT, NG]),
                                          ALU.is_equal))
                if k:
                    chained(dve.tensor_tensor(gmask[:, 0], gmask[:, 0], gmask[:, 1], ALU.add))
            chained(dve.tensor_tensor(msc.rearrange("p t (a b) -> p (t a) b", b=GS),
                                      sc.rearrange("p t (a b) -> p (t a) b", b=GS),
                                      gmask[:, 0].rearrange("p t a -> p (t a)").unsqueeze(2).to_broadcast(
                                          [P, NT * NG, GS]), ALU.mult))
            shared(4)
            for t in range(NT):
                ins = dve.max(g.wk[:, t, :], msc[:, t, :])
            chained(ins)
            for t in range(NT):
                ins = dve.max_index(gi[:, t, :], g.wk[:, t, :], msc[:, t, :])
            chained(ins)
            chained(dve.tensor_copy(gif[:, :, :], gi[:, :, :]))
            shared(6)
            eid = iota[:, 0:E].unsqueeze(1).to_broadcast([P, NT, E])
            for k in range(K):
                chained(dve.tensor_tensor(oh[:, k], eid, gif[:, :, k:k + 1].to_broadcast([P, NT, E]), ALU.is_equal))
                dve.nop().then_inc(s_oh, 1)
                if k:
                    chained(dve.tensor_tensor(mask[:, :, :], oh[:, 0] if k == 1 else mask[:, :, :], oh[:, k], ALU.add))
                shared(7 + k)
            for t in range(NT):
                chained(dve.tensor_tensor(cm[:, t + 1, :], cm[:, t, :], mask[:, t, :], ALU.add))
            dve.nop().then_inc(s_m, 1)
            shared(len(gu_steps))
            dve.wait_ge(s_pos, 1)
            chained(dve.tensor_scalar(cnt[:, :], count, -1.0, None, ALU.add))
            chained(dve.scalar_tensor_tensor(msc[:, :, :], pos, C - 1.5, mask[:, :, :], ALU.is_gt, ALU.mult))
            chained(dve.tensor_tensor(msc[:, :, :], msc[:, :, :], sc[:, :, :], ALU.mult))
            dve.nop().then_inc(s_wov, 1)
            chained(dve.tensor_tensor(tmp[:, :, :], pos, cnt[:, :].unsqueeze(1).to_broadcast([P, NT, E]),
                                      ALU.not_equal))
            chained(dve.tensor_scalar(slot[:, :, :], pos, C - 1.5, float(OOB), ALU.is_gt, ALU.mult))
            chained(dve.tensor_tensor(tmp[:, :, :], tmp[:, :, :], slot[:, :, :], ALU.mult))
            chained(dve.tensor_scalar(slot[:, :, :], pos, float(C - 1), None, ALU.min))
            chained(dve.tensor_tensor(slot[:, :, :], slot[:, :, :], tmp[:, :, :], ALU.add))
            for k in range(K):
                chained(dve.tensor_tensor(tmp[:, :, :], slot[:, :, :], oh[:, k], ALU.mult))
                chained(dve.tensor_reduce(v[:, k, :], tmp[:, :, :], AX.X, ALU.add))
                if k >= 2:
                    dve.wait_ge(s_used, k - 1)
                dve.tensor_tensor(ph[k % 2][:, :, :], iota[:, :].unsqueeze(1).to_broadcast([P, NT, C]),
                                  v[:, k, :].unsqueeze(2).to_broadcast([P, NT, C]), ALU.is_equal).then_inc(s_ph, 1)
                shared_sum(2 * k)
                shared_sum(2 * k + 1)
            dve.wait_ge(s_used, K)
            dve.tensor_copy(g.src[:, :], picked[:, 0, :])
            chained(dve.tensor_copy(dtmp[:, 0, :], picked[:, 0, :]))
            chained(dve.scalar_tensor_tensor(dtmp[:, 0, :], picked[:, 1, :], float(T), dtmp[:, 0, :],
                                             ALU.mult, ALU.add))
            chained(dve.tensor_scalar(dtmp[:, 1, :], picked[:, 1, :], 0.5, float(OOB), ALU.is_lt, ALU.mult))
            chained(dve.scalar_tensor_tensor(dtmp[:, 0, :], dtmp[:, 1, :], last[0:C, 0:1], dtmp[:, 0, :],
                                             ALU.add, ALU.add))
            chained(dve.tensor_copy(g.dst[:, :], dtmp[:, 0, :]))
            for t in range(2 * K, NT):
                shared_sum(t)

        @block.gpsimd
        def _(pool):
            pool.wait_ge(s_in, 80)
            for k in range(K):
                pool.wait_ge(s_oh, k + 1)
                if k >= 2:
                    pool.wait_ge(s_used, k - 1)
                pool.tensor_tensor(eh[k % 2][:, :, 0, :], oh[:, k], token[:, :].unsqueeze(2).to_broadcast(
                    [P, NT, E]), ALU.mult).then_inc(s_eh, 1)
                pool.tensor_scalar(eh[k % 2][:, :, 1, :], oh[:, k], float(k + 1), None, ALU.mult).then_inc(s_eh, 1)
            pool.wait_ge(g.s_zero, 16 * ZD)


def experts(nc, g, c):
    rows = [g.sb(f"x_rows{i}", [C, XG, D], F32, c) for i in range(XB // XG)]
    xeT = [g.sb(f"x_T{i}", [P, 2, DC, C], F32, c) for i in range(2)]
    sg = [g.sb(f"x_sg{i}", [MH, 2, C], F32, c) for i in range(2)]
    h = [g.sb(f"x_h{i}", [MH, 2, C], F32, c) for i in range(2)]
    orow = [g.sb(f"x_o{i}", [C, XG, D], F32, c) for i in range(XB // XG)]
    NR = XB // XG
    s_row = [g.sem(f"x_row{i}") for i in range(NR)]
    s_out = [g.sem(f"x_out{i}") for i in range(NR)]
    s_t, s_tc, s_gu, s_sil, s_h, s_dn, s_o = [g.sem(f"x_{n}") for n in ("t", "tc", "gu", "silu", "h", "down", "o")]
    ROWS_IN = XG * 16
    s_scat = [g.sem(f"x_scatter{i}") for i in range(NR)]
    s_free = g.sem("x_out_free")

    with nc.Block() as block:
        @block.sync
        def _(sp):
            with sp.Fori(1, E // XB) as i:
                for s in range(XB):
                    sp.wait_ge(s_dn, i * XB + (s - XB + 3))
                    sp.dma_start(g.wgu[s][:, :, :], g.t["wgu"][ds(i * XB + s, 1), :, :, :].rearrange(
                        "o p c n -> (o p) c n")).then_inc(g.s_wgu[s], 16)
                    sp.dma_start(g.wd[s][:, :, :], g.t["wd"][ds(i * XB + s, 1), :, :, :].rearrange(
                        "o p c n -> (o p) c n")).then_inc(g.s_wgu[s], 16)

        @block.gpsimd
        def _(pool):
            def gather(e):
                pool.indirect_dma_start(out=rows[e % XB // XG][:, e % XG, :], out_offset=None, in_=g.xrows,
                                        in_offset=bass.IndirectOffsetOnAxis(ap=g.src[:, e:e + 1], axis=0),
                                        bounds_check=T - 1, oob_is_err=False).then_inc(s_row[e % XB // XG], 16)

            for e in range(XB):
                gather(e)
            for e in range(E):
                pool.wait_ge(s_o, e + 3)
                pool.indirect_dma_start(out=g.krows, out_offset=bass.IndirectOffsetOnAxis(
                    ap=g.dst[:, e:e + 1], axis=0), in_=orow[e % XB // XG][:, e % XG, :], in_offset=None,
                    bounds_check=K * T - 1, oob_is_err=False).then_inc(s_scat[e % XB // XG], 16)
                if e >= XG and e % XG == 2:
                    done = e // XG - 1
                    pool.wait_ge(s_scat[done % NR], ROWS_IN * (done // NR + 1))
                    pool.nop().then_inc(s_free, 1)
                if e + XB < E:
                    pool.wait_ge(s_t, e // 2 + 1)
                    gather(e + XB)
            for i in range(NR):
                pool.wait_ge(s_scat[i], ROWS_IN * (E // XB))

        @block.tensor
        def _(pe):
            def turn_pair(p_num, s):
                if s % XG == 0:
                    pe.wait_ge(s_row[s // XG], p_num * (2 * ROWS_IN // XB) + (ROWS_IN - ROWS_IN * s // XB))
                pe.wait_ge(s_tc, p_num + 1)
                b_ = g.bank[0][:, (s // 2) % 2, :]
                for a in range(2):
                    for c_ in range(DC):
                        o = (a * DC + c_) * C
                        ins = pe.transpose(b_[:, o:o + C], rows[s // XG][:, (s + a) % XG, c_ * P:(c_ + 1) * P],
                                           g.identf[0:C, 0:C])
                ins.then_inc(s_t, 1)

            def gu(e, s, half_e):
                pe.wait_ge(s_tc, half_e + 3)
                pe.wait_ge(g.s_wgu[s], e * 4 + (32 - 4 * s))
                pe.wait_ge(s_h, e + 1)
                b_ = g.bank[1][0:MH, s % 2, :]
                for m in range(4):
                    for c_ in range(DC):
                        ins = pe.matmul(b_[:, m * C:(m + 1) * C], g.wgu[s][:, c_, m * MH:(m + 1) * MH],
                                        xeT[(s // 2) % 2][:, s % 2, c_, :], start=(c_ == 0), stop=(c_ == DC - 1))
                ins.then_inc(s_gu, 1)

            def down(e, s):
                pe.wait_ge(s_h, e + 3)
                pe.wait_ge(s_o, e + 1)
                for m in range(2):
                    ins = pe.matmul(g.bank[2][0:C, s % 2, 0:D], h[s % 2][:, m, :], g.wd[s][:, m, :],
                                    start=(m == 0), stop=(m == 1))
                ins.then_inc(s_dn, 1)

            pe.nop().then_inc(s_gu, 4)
            pe.nop().then_inc(s_dn, 2)
            turn_pair(0, 0)
            gu(0, 0, 0)

            def one_pass(i, more):
                for s in range(XB):
                    if s % 2 == 0 and (more or s + 2 < XB):
                        turn_pair(i * (XB // 2) + (s // 2 + 1), (s + 2) % XB)
                    if more or s + 1 < XB:
                        gu(i * XB + (s + 1), (s + 1) % XB, i * (XB // 2) + (s + 1) // 2)
                    down(i * XB + s, s)

            with pe.Fori(0, E // XB - 1) as i:
                one_pass(i, True)
            one_pass(E // XB - 1, False)

        def walk(eng, step_turn, step_expert, step_down):
            step_turn(0, 0)
            step_expert(0, 0)

            def one_pass(i, more):
                for s in range(XB):
                    if s % 2 == 0 and (more or s + 2 < XB):
                        step_turn(i * (XB // 2) + (s // 2 + 1), (s + 2) % XB)
                    if more or s + 1 < XB:
                        step_expert(i * XB + (s + 1), (s + 1) % XB)
                    step_down(i, i * XB + s, s)

            with eng.Fori(0, E // XB - 1) as i:
                one_pass(i, True)
            one_pass(E // XB - 1, False)

        @block.scalar
        def _(act):
            act.nop().then_inc(s_o, 2)
            for i in range(NR):
                act.nop().then_inc(s_out[i], 16)
            act.nop().then_inc(s_free, NR)

            def silu(e, s):
                act.wait_ge(s_gu, e + 5)
                act.wait_ge(s_h, e + 1)
                act.activation(sg[s % 2][:, :, :], g.bank[1][0:MH, s % 2, 0:2 * C].rearrange(
                    "p (m c) -> p m c", c=C), ACT.Silu).then_inc(s_sil, 1)

            def out_rows(i, e, s):
                act.wait_ge(s_dn, e + 3)
                if s % XG == 0:
                    act.wait_ge(s_out[s // XG], i * 16 + 16)
                    act.wait_ge(s_free, i * NR + (s // XG + 1))
                act.activation(orow[s // XG][:, s % XG, :], g.bank[2][0:C, s % 2, 0:D], ACT.Copy).then_inc(s_o, 1)
                if s % XG == XG - 1:
                    act.wait_ge(s_o, e + 3)
                    act.dma_start(g.lrows[ds(e - (XG - 1), XG), :].rearrange("(o e) d -> o e d", o=1),
                                  orow[s // XG][C - 1:C, :, :]).then_inc(s_out[s // XG], 16)

            walk(act, lambda p_num, s: None, silu, out_rows)
            for i in range(NR):
                act.wait_ge(s_out[i], 16 * (E // XB) + 16)

        @block.vector
        def _(dve):
            dve.nop().then_inc(s_tc, 2)
            dve.nop().then_inc(s_h, 2)

            def turned(p_num, s):
                dve.wait_ge(s_t, p_num + 1)
                dve.wait_ge(s_gu, p_num * 2 + 2)
                dve.tensor_copy(xeT[(s // 2) % 2].rearrange("p a c n -> p (a c n)"),
                                g.bank[0][:, (s // 2) % 2, 0:2 * DC * C]).then_inc(s_tc, 1)

            def product(e, s):
                dve.wait_ge(s_sil, e + 1)
                dve.wait_ge(s_dn, e + 1)
                dve.tensor_tensor(h[s % 2][:, :, :], g.bank[1][0:MH, s % 2, 2 * C:4 * C].rearrange(
                    "p (m c) -> p m c", c=C), sg[s % 2][:, :, :], ALU.mult).then_inc(s_h, 1)

            walk(dve, turned, product, lambda i, e, s: None)


def combine(nc, g, c, out):
    NB = 8
    rows = [g.sb(f"c_rows{i}", [P, K, D], F32, c) for i in range(NB)]
    last = g.sb("c_last", [E, D], F32, c)
    s_g = [g.sem(f"c_load{i}") for i in range(NB)]
    s_acc, s_st, s_l, s_mm = g.sem("c_acc"), g.sem("c_store"), g.sem("c_last"), g.sem("c_mm")
    ov = out.rearrange("b (n p) d -> p (b n) d", p=P)
    kv = g.krows.rearrange("(k n p) d -> p n k d", n=NT, p=P)
    STEPS = K + 1
    with nc.Block() as block:
        @block.scalar
        def _(act):
            act.dma_start(last[:, :], g.lrows).then_inc(s_l, 16)
            for t in range(NT):
                if t >= NB:
                    act.wait_ge(s_acc, STEPS * ((t - NB) // 2 * 2 + 2))
                act.dma_start(rows[t % NB][:, :, :], kv[:, t, :, :]).then_inc(s_g[t % NB], 16)

        @block.tensor
        def _(pe):
            pe.wait_ge(s_l, 16)
            for t in range(NT):
                if t >= 4:
                    pe.wait_ge(s_acc, STEPS * ((t - 4) // 2 * 2 + 2))
                pe.matmul(g.bank[t % 4][:, 0, 0:D], g.wovT[:, t * P:(t + 1) * P], last[:, :], start=True,
                          stop=True).then_inc(s_mm, 1)

        @block.vector
        def _(dve):
            for t0 in range(0, NT, 2):
                for t in (t0, t0 + 1):
                    dve.wait_ge(s_g[t % NB], 16 * (t // NB + 1))
                for k in range(STEPS):
                    for a, t in enumerate((t0, t0 + 1)):
                        if k:
                            dve.wait_ge(s_acc, STEPS * t0 + 2 * k + a - 1)
                        if k < K:
                            ins = dve.scalar_tensor_tensor(g.x[:, t, :], rows[t % NB][:, k, :], g.wk[:, t, k:k + 1],
                                                           g.x[:, t, :], ALU.mult, ALU.add)
                        else:
                            dve.wait_ge(s_mm, t + 1)
                            ins = dve.tensor_tensor(g.x[:, t, :], g.bank[t % 4][:, 0, 0:D], g.x[:, t, :], ALU.add)
                        ins.then_inc(s_acc, 1)

        @block.sync
        def _(sp):
            for t in range(NT):
                sp.wait_ge(s_acc, STEPS * (t // 2 * 2 + 2))
                sp.dma_start(ov[:, t, :], g.x[:, t, :]).then_inc(s_st, 16)
            sp.wait_ge(s_st, 16 * NT)



def kernel(**inputs):
    import numpy as _np
    import concourse.bacc as _bacc
    from concourse import mybir as _mybir
    from concourse.bass_utils import run_bass_kernel_spmd as _run

    a = {k: _np.asarray(v) for k, v in inputs.items()}
    host = {
        "x": a["L0_attn_x"],
        "wqkv0": _np.concatenate([a["L0_attn_Wq"].T, a["L0_attn_Wk"].T, a["L0_attn_Wv"].T], axis=1),
        "wo0": a["L0_attn_Wo"].T,
        "ffn_w": a["L0_ffn_weight"].T,
        "gamma": a["L0_ffn_gamma"],
        "beta": a["L0_ffn_beta"],
        "ln_w": a["L0_ffn_ln_weight"].reshape(DC, P).T,
        "ln_b": a["L0_ffn_ln_bias"].reshape(DC, P).T,
        "wqkv1": _np.concatenate([a[f"L1_attn_W_{n}"] for n in "QKV"], axis=2).reshape(
            H, DC, P, 3 * DH1).transpose(0, 2, 1, 3),
        "wo1": a["L1_attn_W_O"].transpose(1, 0, 2),
        "b_QK": _np.stack([a["L1_attn_b_Q"].T, a["L1_attn_b_K"].T], 2), "b_V": a["L1_attn_b_V"].T,
        "b_O": a["L1_attn_b_O"],
        "gate": a["L1_ffn_gate_weight"].T,
        "wgu": _np.concatenate([a["L1_ffn_Wg"], a["L1_ffn_Wu"]], axis=1).transpose(0, 2, 1).reshape(
            E, DC, P, 2 * M).transpose(0, 2, 1, 3),
        "wd": a["L1_ffn_Wd"].transpose(0, 2, 1).reshape(E, 2, MH, D).transpose(0, 2, 1, 3),
        "sgu": _np.concatenate([a["L1_ffn_Sg"].T, a["L1_ffn_Su"].T], axis=1).reshape(
            DC, P, 2 * MS).transpose(1, 0, 2),
        "sd": a["L1_ffn_Sd"].T,
    }
    host.update(constants())
    nc = _bacc.Bacc("TRN2", target_bir_lowering=False, num_devices=1)
    arrays, t_in = {}, {}
    for name, arr in host.items():
        arrays[f"in_{name}"] = _np.ascontiguousarray(arr)
        t_in[name] = nc.dram_tensor(f"in_{name}", arr.shape, _mybir.dt.from_np(arr.dtype), kind="ExternalInput").ap()
    out = nc.dram_tensor("out_0", (B, S, D), _mybir.dt.float32, kind="ExternalOutput").ap()
    build(nc, t_in, out)
    r = _run(nc, [arrays], core_ids=[0])
    return r.results[0]["out_0"]
```
